# Optimizing a Trainium2 kernel written in Bass

```python
import numpy as np
import jax
import jax.numpy as jnp

def _softmax(x, axis=-1):
    return jax.nn.softmax(x, axis=axis)

def _gelu(x):
    return jax.nn.gelu(x, approximate=True)

def _silu(x):
    return jax.nn.silu(x)

def _sigmoid(x):
    return jax.nn.sigmoid(x)

def _layernorm(x, axis=-1, eps=1e-05):
    m = jnp.mean(x, axis=axis, keepdims=True)
    v = jnp.var(x, axis=axis, keepdims=True)
    return (x - m) / jnp.sqrt(v + eps)

def _scatter_add(tgt, idx, src, axis=0):
    return tgt.at[idx].add(src)

def _segment_sum(src, seg, n):
    return jax.ops.segment_sum(src, seg, n)
kernel_name = 'mk_xattn_seq_d4_seqx_r8_a71ed6'

def setup_inputs(seed: int=0):
    np.random.seed(seed)
    _w = jnp.asarray

    def _rec_inputs():
        import jax
        import jax.numpy as jnp
        _rk = jax.random.key(seed)
        x = -0.0002928 + 1 * jax.random.normal(jax.random.fold_in(_rk, 1), (8, 256, 128), jnp.float32)
        _lenS = 256 - jax.random.randint(jax.random.fold_in(_rk, 7), (8,), 0, max(1, 256 // 4) + 1, jnp.int32)
        _lenS2 = 256 - jax.random.randint(jax.random.fold_in(_rk, 8), (8,), 0, max(1, 256 // 4) + 1, jnp.int32)
        _ctx_1024P = jax.random.normal(jax.random.fold_in(_rk, 11), (8, 16, 128), jnp.float32)
        _ctx_1024c = jax.random.dirichlet(jax.random.fold_in(_rk, 511), 0.3 * jnp.ones((16,), jnp.float32), (8, 256))
        _ctx_1024t = jnp.einsum('bsk,bkd->bsd', _ctx_1024c, _ctx_1024P)
        _ctx_1024t = _ctx_1024t * jax.lax.rsqrt(jnp.mean(jnp.square(_ctx_1024t)) + 1e-12) * 0.953939
        ctx_1024 = -1.39393e-06 + 0.999914 * (_ctx_1024t + 0.3 * jax.random.normal(jax.random.fold_in(_rk, 611), (8, 256, 128), jnp.float32))
        _validS = jnp.arange(256)[None, :] < _lenS[:, None]
        _validS2 = jnp.arange(256)[None, :] < _lenS2[:, None]
        _causal = jnp.tril(jnp.ones((256, 256), dtype=bool))
        mask_1x1xSxS2_ik0 = jnp.where(jnp.broadcast_to(_validS2[0:1, None, None, :], (1, 1, 256, 256)), 0, 1).astype(jnp.int32)
        mask_1x1xSxS2_if1 = jnp.where(jnp.ones((1, 1, 256, 256), dtype=bool), 1, 0).astype(jnp.int32)
        return (x, ctx_1024, mask_1x1xSxS2_ik0, mask_1x1xSxS2_if1)
    x, ctx_1024, mask_1x1xSxS2_ik0, mask_1x1xSxS2_if1 = _rec_inputs()

    def _L0_xattn_setup():
        import jax, jax.numpy as jnp
        import numpy as np
        D_MODEL = 128
        N_HEADS = 16
        D_EXP = 4
        B, SQ, SKV = (2, 256, 256)
        LN_EPS = 1e-05

        def _linear_params(key, d_in, d_out):
            kw, kb = jax.random.split(key)
            w = jax.random.normal(kw, (d_in, d_out), jnp.float32) * 0.02
            b = jax.random.normal(kb, (d_out,), jnp.float32) * 0.02
            return (w, b)

        def _layernorm(x, g, b):
            mu = jnp.mean(x, axis=-1, keepdims=True)
            var = jnp.mean(jnp.square(x - mu), axis=-1, keepdims=True)
            return (x - mu) / jnp.sqrt(var + LN_EPS) * g + b

        def _mha(xq, xkv, wq, bq, wk, bk, wv, bv, wo, bo, mask):
            Bq, Sq, D = xq.shape
            Hd = D // N_HEADS
            q = (xq @ wq + bq).reshape(Bq, Sq, N_HEADS, Hd).transpose(0, 2, 1, 3)
            k = (xkv @ wk + bk).reshape(Bq, -1, N_HEADS, Hd).transpose(0, 2, 1, 3)
            v = (xkv @ wv + bv).reshape(Bq, -1, N_HEADS, Hd).transpose(0, 2, 1, 3)
            score = jnp.einsum('bhqd,bhkd->bhqk', q, k) / jnp.sqrt(jnp.float32(Hd))
            score = jnp.where(mask == 0, -jnp.inf, score)
            attn = jax.nn.softmax(score, axis=-1)
            ctx = jnp.einsum('bhqk,bhkd->bhqd', attn, v)
            ctx = ctx.transpose(0, 2, 1, 3).reshape(Bq, Sq, D)
            return ctx @ wo + bo
        key = jax.random.key(seed)
        ks = jax.random.split(key, 16)
        inp = {}
        inp['x'] = jax.random.normal(ks[0], (B, SQ, D_MODEL), jnp.float32)
        inp['encoder_out'] = jax.random.normal(ks[1], (B, SKV, D_MODEL), jnp.float32)
        inp['tgt_mask'] = jnp.tril(jnp.ones((SQ, SQ), jnp.int32))[None, None]
        inp['src_mask'] = jnp.ones((1, 1, SQ, SKV), jnp.int32)
        inp['wq_s'], inp['bq_s'] = _linear_params(ks[2], D_MODEL, D_MODEL)
        inp['wk_s'], inp['bk_s'] = _linear_params(ks[3], D_MODEL, D_MODEL)
        inp['wv_s'], inp['bv_s'] = _linear_params(ks[4], D_MODEL, D_MODEL)
        inp['wo_s'], inp['bo_s'] = _linear_params(ks[5], D_MODEL, D_MODEL)
        inp['wq_c'], inp['bq_c'] = _linear_params(ks[6], D_MODEL, D_MODEL)
        inp['wk_c'], inp['bk_c'] = _linear_params(ks[7], D_MODEL, D_MODEL)
        inp['wv_c'], inp['bv_c'] = _linear_params(ks[8], D_MODEL, D_MODEL)
        inp['wo_c'], inp['bo_c'] = _linear_params(ks[9], D_MODEL, D_MODEL)
        inp['ff1_w'], inp['ff1_b'] = _linear_params(ks[10], D_MODEL, D_MODEL * D_EXP)
        inp['ff2_w'], inp['ff2_b'] = _linear_params(ks[11], D_MODEL * D_EXP, D_MODEL)
        for i, k in zip((1, 2, 3), (ks[12], ks[13], ks[14])):
            inp[f'ln{i}_g'] = jnp.ones((D_MODEL,), jnp.float32)
            inp[f'ln{i}_b'] = jnp.zeros((D_MODEL,), jnp.float32)
        return inp
    _L0_xattn_all = _L0_xattn_setup()
    _L0_xattn_in = {k: v for k, v in _L0_xattn_all.items() if k in ('wq_s', 'bq_s', 'wk_s', 'bk_s', 'wv_s', 'bv_s', 'wo_s', 'bo_s', 'wq_c', 'bq_c', 'wk_c', 'bk_c', 'wv_c', 'bv_c', 'wo_c', 'bo_c', 'ff1_w', 'ff1_b', 'ff2_w', 'ff2_b', 'ln1_g', 'ln1_b', 'ln2_g', 'ln2_b', 'ln3_g', 'ln3_b')}
    del _L0_xattn_all

    def _L1_xattn_setup():
        import jax, jax.numpy as jnp
        import numpy as np
        EPS = 1e-05

        def _layernorm(x, g, b):
            m = jnp.mean(x, axis=-1, keepdims=True)
            v = jnp.mean((x - m) ** 2, axis=-1, keepdims=True)
            return (x - m) / jnp.sqrt(v + EPS) * g + b

        def _mha(x, kv, Wq, Wk, Wv, mask, causal):
            m = mask[:, None]
            Q = jnp.einsum('bsd,hdk->bhsk', x, Wq) * m
            K = jnp.einsum('bsd,hdk->bhsk', kv, Wk) * m
            V = jnp.einsum('bsd,hdk->bhsk', kv, Wv) * m
            energy = jnp.einsum('bhsk,bhtk->bhst', Q, K)
            S = energy.shape[-1]
            lengths = jnp.sum(energy[:, :, 0, :] != 0, axis=-1)
            cols = jnp.arange(S)
            energy = jnp.where(cols[None, None, None, :] >= lengths[:, :, None, None], -jnp.inf, energy)
            if causal:
                energy = jnp.where(cols[None, :] > cols[:, None], -jnp.inf, energy)
            dk = Wq.shape[-1]
            score = jax.nn.softmax(energy / jnp.sqrt(jnp.asarray(dk, energy.dtype)), axis=-1)
            out = jnp.einsum('bhst,bhtk->bhsk', score, V) * m
            B, H, Sx, dkk = out.shape
            return out.transpose(0, 2, 1, 3).reshape(B, Sx, H * dkk)
        key = jax.random.key(seed)
        ks = jax.random.split(key, 20)
        B, S, D, H = (2, 256, 128, 16)
        dk = D // H
        sd = 0.02
        inp = {'x': jax.random.normal(ks[0], (B, S, D), jnp.float32), 'context': jax.random.normal(ks[1], (B, S, D), jnp.float32), 'Wq1': jax.random.normal(ks[2], (H, D, dk), jnp.float32) * sd, 'Wk1': jax.random.normal(ks[3], (H, D, dk), jnp.float32) * sd, 'Wv1': jax.random.normal(ks[4], (H, D, dk), jnp.float32) * sd, 'Wq2': jax.random.normal(ks[5], (H, D, dk), jnp.float32) * sd, 'Wk2': jax.random.normal(ks[6], (H, D, dk), jnp.float32) * sd, 'Wv2': jax.random.normal(ks[7], (H, D, dk), jnp.float32) * sd, 'ln1_g': jnp.ones((D,), jnp.float32), 'ln1_b': jnp.zeros((D,), jnp.float32), 'ln2_g': jnp.ones((D,), jnp.float32), 'ln2_b': jnp.zeros((D,), jnp.float32), 'ln3_g': jnp.ones((D,), jnp.float32), 'ln3_b': jnp.zeros((D,), jnp.float32), 'fc1_w': jax.random.normal(ks[8], (D, D), jnp.float32) * sd, 'fc1_b': jnp.zeros((D,), jnp.float32), 'fc2_w': jax.random.normal(ks[9], (D, D), jnp.float32) * sd, 'fc2_b': jnp.zeros((D,), jnp.float32)}
        return inp
    _L1_xattn_all = _L1_xattn_setup()
    _L1_xattn_in = {k: v for k, v in _L1_xattn_all.items() if k in ('Wq1', 'Wk1', 'Wv1', 'Wq2', 'Wk2', 'Wv2', 'ln1_g', 'ln1_b', 'ln2_g', 'ln2_b', 'ln3_g', 'ln3_b', 'fc1_w', 'fc1_b', 'fc2_w', 'fc2_b')}
    del _L1_xattn_all

    def _L2_xattn_setup():
        import jax, jax.numpy as jnp
        import numpy as np
        N, L, C, NHEAD = (4, 256, 128, 8)
        D = C // NHEAD
        EPS_ATTN = 1e-06
        EPS_LN = 1e-05

        def _w(key, shape, scale=0.02):
            return jax.random.normal(key, shape, dtype=jnp.float32) * scale

        def layernorm(x, g, b):
            m = jnp.mean(x, axis=-1, keepdims=True)
            v = jnp.mean(jnp.square(x - m), axis=-1, keepdims=True)
            return (x - m) * jax.lax.rsqrt(v + EPS_LN) * g + b

        def linear_attention(q, k, v):
            Q = jax.nn.elu(q) + 1.0
            K = jax.nn.elu(k) + 1.0
            vlen = v.shape[1]
            v = v / vlen
            KV = jnp.einsum('nshd,nshv->nhdv', K, v)
            Z = 1.0 / (jnp.einsum('nlhd,nhd->nlh', Q, K.sum(axis=1)) + EPS_ATTN)
            out = jnp.einsum('nlhd,nhdv,nlh->nlhv', Q, KV, Z) * vlen
            return out

        def heads(x):
            n, l, c = x.shape
            return x.reshape(n, l, NHEAD, D)

        def encoder_layer(x, wq, wk, wv, wm, w1, w2, g1, b1, g2, b2):
            n, l, c = x.shape
            msg = linear_attention(heads(x @ wq), heads(x @ wk), heads(x @ wv))
            msg = msg.reshape(n, l, c) @ wm
            x = x + layernorm(msg, g1, b1)
            x = x + layernorm(jax.nn.relu(x @ w1) @ w2, g2, b2)
            return x

        def decoder_layer(x, src, wq0, wk0, wv0, wm0, wq1, wk1, wv1, wm1, w1, w2, g0, b0, g1, b1, g2, b2):
            n, l, c = x.shape
            msg = linear_attention(heads(x @ wq0), heads(x @ wk0), heads(x @ wv0))
            msg = msg.reshape(n, l, c) @ wm0
            x = x + layernorm(msg, g0, b0)
            msg = linear_attention(heads(x @ wq1), heads(src @ wk1), heads(src @ wv1))
            msg = msg.reshape(n, l, c) @ wm1
            x = x + layernorm(msg, g1, b1)
            x = x + layernorm(jax.nn.relu(x @ w1) @ w2, g2, b2)
            return x
        key = jax.random.key(seed)
        ks = jax.random.split(key, 32)
        inp = {'depth_feat': jax.random.normal(ks[0], (N, L, C), dtype=jnp.float32), 'context_feat': jax.random.normal(ks[1], (N, L, C), dtype=jnp.float32), 'depth_pos': jax.random.normal(ks[2], (N, L, C), dtype=jnp.float32), 'e_wq': _w(ks[3], (C, C)), 'e_wk': _w(ks[4], (C, C)), 'e_wv': _w(ks[5], (C, C)), 'e_wm': _w(ks[6], (C, C)), 'e_w1': _w(ks[7], (C, 2 * C)), 'e_w2': _w(ks[8], (2 * C, C)), 'e_g1': jnp.ones((C,), jnp.float32), 'e_b1': jnp.zeros((C,), jnp.float32), 'e_g2': jnp.ones((C,), jnp.float32), 'e_b2': jnp.zeros((C,), jnp.float32), 'd_wq0': _w(ks[9], (C, C)), 'd_wk0': _w(ks[10], (C, C)), 'd_wv0': _w(ks[11], (C, C)), 'd_wm0': _w(ks[12], (C, C)), 'd_wq1': _w(ks[13], (C, C)), 'd_wk1': _w(ks[14], (C, C)), 'd_wv1': _w(ks[15], (C, C)), 'd_wm1': _w(ks[16], (C, C)), 'd_w1': _w(ks[17], (C, 2 * C)), 'd_w2': _w(ks[18], (2 * C, C)), 'd_g0': jnp.ones((C,), jnp.float32), 'd_b0': jnp.zeros((C,), jnp.float32), 'd_g1': jnp.ones((C,), jnp.float32), 'd_b1': jnp.zeros((C,), jnp.float32), 'd_g2': jnp.ones((C,), jnp.float32), 'd_b2': jnp.zeros((C,), jnp.float32)}
        return inp
    _L2_xattn_all = _L2_xattn_setup()
    _L2_xattn_in = {k: v for k, v in _L2_xattn_all.items() if k in ('e_wq', 'e_wk', 'e_wv', 'e_wm', 'e_w1', 'e_w2', 'e_g1', 'e_b1', 'e_g2', 'e_b2', 'd_wq0', 'd_wk0', 'd_wv0', 'd_wm0', 'd_wq1', 'd_wk1', 'd_wv1', 'd_wm1', 'd_w1', 'd_w2', 'd_g0', 'd_b0', 'd_g1', 'd_b1', 'd_g2', 'd_b2')}
    del _L2_xattn_all

    def _L3_xattn_setup():
        import jax, jax.numpy as jnp
        import numpy as np
        D, H, E, K, DFF = (128, 16, 8, 2, 512)
        B, L, T = (4, 64, 256)
        EPS = 1e-05

        def _xavier(key, shape):
            fan_in, fan_out = (shape[-1], shape[-2])
            a = jnp.sqrt(6.0 / (fan_in + fan_out))
            return jax.random.uniform(key, shape, jnp.float32, -a, a)

        def _ln(x, g, b):
            m = x.mean(-1, keepdims=True)
            v = ((x - m) ** 2).mean(-1, keepdims=True)
            return (x - m) / jnp.sqrt(v + EPS) * g + b

        def _mha(q_in, kv_in, in_w, in_b, out_w, out_b):
            wq, wk, wv = jnp.split(in_w, 3, axis=0)
            bq, bk, bv = jnp.split(in_b, 3, axis=0)
            dh = D // H

            def heads(x, w, b):
                y = x @ w.T + b
                return y.reshape(x.shape[0], x.shape[1], H, dh).transpose(0, 2, 1, 3)
            q = heads(q_in, wq, bq)
            k = heads(kv_in, wk, bk)
            v = heads(kv_in, wv, bv)
            scores = jnp.einsum('bhqd,bhkd->bhqk', q, k) / jnp.sqrt(jnp.float32(dh))
            attn = jax.nn.softmax(scores, axis=-1)
            out = jnp.einsum('bhqk,bhkd->bhqd', attn, v)
            out = out.transpose(0, 2, 1, 3).reshape(q_in.shape[0], q_in.shape[1], D)
            return out @ out_w.T + out_b

        def _fuse_moe(x, ln_g, ln_b, rw, rb, fc1_w, fc1_b, fc2_w, fc2_b):
            h = _ln(x, ln_g, ln_b)
            logits = h @ rw.T + rb
            vals, idx = jax.lax.top_k(logits, K)
            gates = jax.nn.softmax(vals, axis=-1)
            N = x.shape[0] * x.shape[1]
            hf = h.reshape(N, D)
            h1 = jax.nn.gelu(jnp.einsum('nd,efd->enf', hf, fc1_w) + fc1_b[:, None, :], approximate=False)
            eo = jnp.einsum('enf,edf->end', h1, fc2_w) + fc2_b[:, None, :]
            idx_f = idx.reshape(N, K)
            gates_f = gates.reshape(N, K)
            gathered = eo[idx_f, jnp.arange(N)[:, None], :]
            mixed = (gathered * gates_f[..., None]).sum(axis=1).reshape(x.shape)
            return x + mixed
        key = jax.random.key(seed)
        ks = jax.random.split(key, 16)
        inp = {'latents': jax.random.normal(ks[0], (B, L, D), jnp.float32), 'tokens': jax.random.normal(ks[1], (B, T, D), jnp.float32), 'sa_ln_g': jnp.ones((D,)), 'sa_ln_b': jnp.zeros((D,)), 'sa_in_w': _xavier(ks[2], (3 * D, D)), 'sa_in_b': jnp.zeros((3 * D,)), 'sa_out_w': _xavier(ks[3], (D, D)), 'sa_out_b': jnp.zeros((D,)), 'ca_q_ln_g': jnp.ones((D,)), 'ca_q_ln_b': jnp.zeros((D,)), 'ca_kv_ln_g': jnp.ones((D,)), 'ca_kv_ln_b': jnp.zeros((D,)), 'ca_in_w': _xavier(ks[4], (3 * D, D)), 'ca_in_b': jnp.zeros((3 * D,)), 'ca_out_w': _xavier(ks[5], (D, D)), 'ca_out_b': jnp.zeros((D,)), 'moe_ln_g': jnp.ones((D,)), 'moe_ln_b': jnp.zeros((D,)), 'router_w': _xavier(ks[6], (E, D)), 'router_b': jnp.zeros((E,)), 'e_fc1_w': jax.vmap(lambda k: _xavier(k, (DFF, D)))(jax.random.split(ks[7], E)), 'e_fc1_b': jnp.zeros((E, DFF)), 'e_fc2_w': jax.vmap(lambda k: _xavier(k, (D, DFF)))(jax.random.split(ks[8], E)), 'e_fc2_b': jnp.zeros((E, D))}
        return inp
    _L3_xattn_all = _L3_xattn_setup()
    _L3_xattn_in = {k: v for k, v in _L3_xattn_all.items() if k in ('sa_ln_g', 'sa_ln_b', 'sa_in_w', 'sa_in_b', 'sa_out_w', 'sa_out_b', 'ca_q_ln_g', 'ca_q_ln_b', 'ca_kv_ln_g', 'ca_kv_ln_b', 'ca_in_w', 'ca_in_b', 'ca_out_w', 'ca_out_b', 'moe_ln_g', 'moe_ln_b', 'router_w', 'router_b', 'e_fc1_w', 'e_fc1_b', 'e_fc2_w', 'e_fc2_b')}
    del _L3_xattn_all
    return {'x': x, 'ctx_1024': ctx_1024, 'mask_1x1xSxS2_ik0': mask_1x1xSxS2_ik0, 'mask_1x1xSxS2_if1': mask_1x1xSxS2_if1, 'L0_xattn_wq_s': _L0_xattn_in['wq_s'], 'L0_xattn_bq_s': _L0_xattn_in['bq_s'], 'L0_xattn_wk_s': _L0_xattn_in['wk_s'], 'L0_xattn_bk_s': _L0_xattn_in['bk_s'], 'L0_xattn_wv_s': _L0_xattn_in['wv_s'], 'L0_xattn_bv_s': _L0_xattn_in['bv_s'], 'L0_xattn_wo_s': _L0_xattn_in['wo_s'], 'L0_xattn_bo_s': _L0_xattn_in['bo_s'], 'L0_xattn_wq_c': _L0_xattn_in['wq_c'], 'L0_xattn_bq_c': _L0_xattn_in['bq_c'], 'L0_xattn_wk_c': _L0_xattn_in['wk_c'], 'L0_xattn_bk_c': _L0_xattn_in['bk_c'], 'L0_xattn_wv_c': _L0_xattn_in['wv_c'], 'L0_xattn_bv_c': _L0_xattn_in['bv_c'], 'L0_xattn_wo_c': _L0_xattn_in['wo_c'], 'L0_xattn_bo_c': _L0_xattn_in['bo_c'], 'L0_xattn_ff1_w': _L0_xattn_in['ff1_w'], 'L0_xattn_ff1_b': _L0_xattn_in['ff1_b'], 'L0_xattn_ff2_w': _L0_xattn_in['ff2_w'], 'L0_xattn_ff2_b': _L0_xattn_in['ff2_b'], 'L0_xattn_ln1_g': _L0_xattn_in['ln1_g'], 'L0_xattn_ln1_b': _L0_xattn_in['ln1_b'], 'L0_xattn_ln2_g': _L0_xattn_in['ln2_g'], 'L0_xattn_ln2_b': _L0_xattn_in['ln2_b'], 'L0_xattn_ln3_g': _L0_xattn_in['ln3_g'], 'L0_xattn_ln3_b': _L0_xattn_in['ln3_b'], 'L1_xattn_Wq1': _L1_xattn_in['Wq1'], 'L1_xattn_Wk1': _L1_xattn_in['Wk1'], 'L1_xattn_Wv1': _L1_xattn_in['Wv1'], 'L1_xattn_Wq2': _L1_xattn_in['Wq2'], 'L1_xattn_Wk2': _L1_xattn_in['Wk2'], 'L1_xattn_Wv2': _L1_xattn_in['Wv2'], 'L1_xattn_ln1_g': _L1_xattn_in['ln1_g'], 'L1_xattn_ln1_b': _L1_xattn_in['ln1_b'], 'L1_xattn_ln2_g': _L1_xattn_in['ln2_g'], 'L1_xattn_ln2_b': _L1_xattn_in['ln2_b'], 'L1_xattn_ln3_g': _L1_xattn_in['ln3_g'], 'L1_xattn_ln3_b': _L1_xattn_in['ln3_b'], 'L1_xattn_fc1_w': _L1_xattn_in['fc1_w'], 'L1_xattn_fc1_b': _L1_xattn_in['fc1_b'], 'L1_xattn_fc2_w': _L1_xattn_in['fc2_w'], 'L1_xattn_fc2_b': _L1_xattn_in['fc2_b'], 'L2_xattn_e_wq': _L2_xattn_in['e_wq'], 'L2_xattn_e_wk': _L2_xattn_in['e_wk'], 'L2_xattn_e_wv': _L2_xattn_in['e_wv'], 'L2_xattn_e_wm': _L2_xattn_in['e_wm'], 'L2_xattn_e_w1': _L2_xattn_in['e_w1'], 'L2_xattn_e_w2': _L2_xattn_in['e_w2'], 'L2_xattn_e_g1': _L2_xattn_in['e_g1'], 'L2_xattn_e_b1': _L2_xattn_in['e_b1'], 'L2_xattn_e_g2': _L2_xattn_in['e_g2'], 'L2_xattn_e_b2': _L2_xattn_in['e_b2'], 'L2_xattn_d_wq0': _L2_xattn_in['d_wq0'], 'L2_xattn_d_wk0': _L2_xattn_in['d_wk0'], 'L2_xattn_d_wv0': _L2_xattn_in['d_wv0'], 'L2_xattn_d_wm0': _L2_xattn_in['d_wm0'], 'L2_xattn_d_wq1': _L2_xattn_in['d_wq1'], 'L2_xattn_d_wk1': _L2_xattn_in['d_wk1'], 'L2_xattn_d_wv1': _L2_xattn_in['d_wv1'], 'L2_xattn_d_wm1': _L2_xattn_in['d_wm1'], 'L2_xattn_d_w1': _L2_xattn_in['d_w1'], 'L2_xattn_d_w2': _L2_xattn_in['d_w2'], 'L2_xattn_d_g0': _L2_xattn_in['d_g0'], 'L2_xattn_d_b0': _L2_xattn_in['d_b0'], 'L2_xattn_d_g1': _L2_xattn_in['d_g1'], 'L2_xattn_d_b1': _L2_xattn_in['d_b1'], 'L2_xattn_d_g2': _L2_xattn_in['d_g2'], 'L2_xattn_d_b2': _L2_xattn_in['d_b2'], 'L3_xattn_sa_ln_g': _L3_xattn_in['sa_ln_g'], 'L3_xattn_sa_ln_b': _L3_xattn_in['sa_ln_b'], 'L3_xattn_sa_in_w': _L3_xattn_in['sa_in_w'], 'L3_xattn_sa_in_b': _L3_xattn_in['sa_in_b'], 'L3_xattn_sa_out_w': _L3_xattn_in['sa_out_w'], 'L3_xattn_sa_out_b': _L3_xattn_in['sa_out_b'], 'L3_xattn_ca_q_ln_g': _L3_xattn_in['ca_q_ln_g'], 'L3_xattn_ca_q_ln_b': _L3_xattn_in['ca_q_ln_b'], 'L3_xattn_ca_kv_ln_g': _L3_xattn_in['ca_kv_ln_g'], 'L3_xattn_ca_kv_ln_b': _L3_xattn_in['ca_kv_ln_b'], 'L3_xattn_ca_in_w': _L3_xattn_in['ca_in_w'], 'L3_xattn_ca_in_b': _L3_xattn_in['ca_in_b'], 'L3_xattn_ca_out_w': _L3_xattn_in['ca_out_w'], 'L3_xattn_ca_out_b': _L3_xattn_in['ca_out_b'], 'L3_xattn_moe_ln_g': _L3_xattn_in['moe_ln_g'], 'L3_xattn_moe_ln_b': _L3_xattn_in['moe_ln_b'], 'L3_xattn_router_w': _L3_xattn_in['router_w'], 'L3_xattn_router_b': _L3_xattn_in['router_b'], 'L3_xattn_e_fc1_w': _L3_xattn_in['e_fc1_w'], 'L3_xattn_e_fc1_b': _L3_xattn_in['e_fc1_b'], 'L3_xattn_e_fc2_w': _L3_xattn_in['e_fc2_w'], 'L3_xattn_e_fc2_b': _L3_xattn_in['e_fc2_b']}

def reference(x, ctx_1024, mask_1x1xSxS2_ik0, mask_1x1xSxS2_if1, L0_xattn_wq_s, L0_xattn_bq_s, L0_xattn_wk_s, L0_xattn_bk_s, L0_xattn_wv_s, L0_xattn_bv_s, L0_xattn_wo_s, L0_xattn_bo_s, L0_xattn_wq_c, L0_xattn_bq_c, L0_xattn_wk_c, L0_xattn_bk_c, L0_xattn_wv_c, L0_xattn_bv_c, L0_xattn_wo_c, L0_xattn_bo_c, L0_xattn_ff1_w, L0_xattn_ff1_b, L0_xattn_ff2_w, L0_xattn_ff2_b, L0_xattn_ln1_g, L0_xattn_ln1_b, L0_xattn_ln2_g, L0_xattn_ln2_b, L0_xattn_ln3_g, L0_xattn_ln3_b, L1_xattn_Wq1, L1_xattn_Wk1, L1_xattn_Wv1, L1_xattn_Wq2, L1_xattn_Wk2, L1_xattn_Wv2, L1_xattn_ln1_g, L1_xattn_ln1_b, L1_xattn_ln2_g, L1_xattn_ln2_b, L1_xattn_ln3_g, L1_xattn_ln3_b, L1_xattn_fc1_w, L1_xattn_fc1_b, L1_xattn_fc2_w, L1_xattn_fc2_b, L2_xattn_e_wq, L2_xattn_e_wk, L2_xattn_e_wv, L2_xattn_e_wm, L2_xattn_e_w1, L2_xattn_e_w2, L2_xattn_e_g1, L2_xattn_e_b1, L2_xattn_e_g2, L2_xattn_e_b2, L2_xattn_d_wq0, L2_xattn_d_wk0, L2_xattn_d_wv0, L2_xattn_d_wm0, L2_xattn_d_wq1, L2_xattn_d_wk1, L2_xattn_d_wv1, L2_xattn_d_wm1, L2_xattn_d_w1, L2_xattn_d_w2, L2_xattn_d_g0, L2_xattn_d_b0, L2_xattn_d_g1, L2_xattn_d_b1, L2_xattn_d_g2, L2_xattn_d_b2, L3_xattn_sa_ln_g, L3_xattn_sa_ln_b, L3_xattn_sa_in_w, L3_xattn_sa_in_b, L3_xattn_sa_out_w, L3_xattn_sa_out_b, L3_xattn_ca_q_ln_g, L3_xattn_ca_q_ln_b, L3_xattn_ca_kv_ln_g, L3_xattn_ca_kv_ln_b, L3_xattn_ca_in_w, L3_xattn_ca_in_b, L3_xattn_ca_out_w, L3_xattn_ca_out_b, L3_xattn_moe_ln_g, L3_xattn_moe_ln_b, L3_xattn_router_w, L3_xattn_router_b, L3_xattn_e_fc1_w, L3_xattn_e_fc1_b, L3_xattn_e_fc2_w, L3_xattn_e_fc2_b):
    import jax
    import jax.numpy as jnp

    def _L0_xattn_ref(x, encoder_out, tgt_mask, src_mask, wq_s, bq_s, wk_s, bk_s, wv_s, bv_s, wo_s, bo_s, wq_c, bq_c, wk_c, bk_c, wv_c, bv_c, wo_c, bo_c, ff1_w, ff1_b, ff2_w, ff2_b, ln1_g, ln1_b, ln2_g, ln2_b, ln3_g, ln3_b):
        import jax, jax.numpy as jnp
        import numpy as np
        D_MODEL = 128
        N_HEADS = 16
        D_EXP = 4
        B, SQ, SKV = (2, 256, 256)
        LN_EPS = 1e-05

        def _linear_params(key, d_in, d_out):
            kw, kb = jax.random.split(key)
            w = jax.random.normal(kw, (d_in, d_out), jnp.float32) * 0.02
            b = jax.random.normal(kb, (d_out,), jnp.float32) * 0.02
            return (w, b)

        def _layernorm(x, g, b):
            mu = jnp.mean(x, axis=-1, keepdims=True)
            var = jnp.mean(jnp.square(x - mu), axis=-1, keepdims=True)
            return (x - mu) / jnp.sqrt(var + LN_EPS) * g + b

        def _mha(xq, xkv, wq, bq, wk, bk, wv, bv, wo, bo, mask):
            Bq, Sq, D = xq.shape
            Hd = D // N_HEADS
            q = (xq @ wq + bq).reshape(Bq, Sq, N_HEADS, Hd).transpose(0, 2, 1, 3)
            k = (xkv @ wk + bk).reshape(Bq, -1, N_HEADS, Hd).transpose(0, 2, 1, 3)
            v = (xkv @ wv + bv).reshape(Bq, -1, N_HEADS, Hd).transpose(0, 2, 1, 3)
            score = jnp.einsum('bhqd,bhkd->bhqk', q, k) / jnp.sqrt(jnp.float32(Hd))
            score = jnp.where(mask == 0, -jnp.inf, score)
            attn = jax.nn.softmax(score, axis=-1)
            ctx = jnp.einsum('bhqk,bhkd->bhqd', attn, v)
            ctx = ctx.transpose(0, 2, 1, 3).reshape(Bq, Sq, D)
            return ctx @ wo + bo
        sa = _mha(x, x, wq_s, bq_s, wk_s, bk_s, wv_s, bv_s, wo_s, bo_s, tgt_mask)
        h = _layernorm(x + sa, ln1_g, ln1_b)
        ca = _mha(h, encoder_out, wq_c, bq_c, wk_c, bk_c, wv_c, bv_c, wo_c, bo_c, src_mask)
        h2 = _layernorm(h + ca, ln2_g, ln2_b)
        ff = jax.nn.relu(h2 @ ff1_w + ff1_b) @ ff2_w + ff2_b
        return _layernorm(h2 + ff, ln3_g, ln3_b)

    def _L1_xattn_ref(x, context, Wq1, Wk1, Wv1, Wq2, Wk2, Wv2, ln1_g, ln1_b, ln2_g, ln2_b, ln3_g, ln3_b, fc1_w, fc1_b, fc2_w, fc2_b):
        import jax, jax.numpy as jnp
        import numpy as np
        EPS = 1e-05

        def _layernorm(x, g, b):
            m = jnp.mean(x, axis=-1, keepdims=True)
            v = jnp.mean((x - m) ** 2, axis=-1, keepdims=True)
            return (x - m) / jnp.sqrt(v + EPS) * g + b

        def _mha(x, kv, Wq, Wk, Wv, mask, causal):
            m = mask[:, None]
            Q = jnp.einsum('bsd,hdk->bhsk', x, Wq) * m
            K = jnp.einsum('bsd,hdk->bhsk', kv, Wk) * m
            V = jnp.einsum('bsd,hdk->bhsk', kv, Wv) * m
            energy = jnp.einsum('bhsk,bhtk->bhst', Q, K)
            S = energy.shape[-1]
            lengths = jnp.sum(energy[:, :, 0, :] != 0, axis=-1)
            cols = jnp.arange(S)
            energy = jnp.where(cols[None, None, None, :] >= lengths[:, :, None, None], -jnp.inf, energy)
            if causal:
                energy = jnp.where(cols[None, :] > cols[:, None], -jnp.inf, energy)
            dk = Wq.shape[-1]
            score = jax.nn.softmax(energy / jnp.sqrt(jnp.asarray(dk, energy.dtype)), axis=-1)
            out = jnp.einsum('bhst,bhtk->bhsk', score, V) * m
            B, H, Sx, dkk = out.shape
            return out.transpose(0, 2, 1, 3).reshape(B, Sx, H * dkk)
        mask0 = 1.0 - jnp.all(x == 0, axis=2, keepdims=True).astype(x.dtype)
        z = _mha(x, x, Wq1, Wk1, Wv1, mask0, causal=True)
        x1 = _layernorm(x + z, ln1_g, ln1_b)
        mask1 = 1.0 - jnp.all(x1 == 0, axis=2, keepdims=True).astype(x1.dtype)
        z = _mha(x1, context, Wq2, Wk2, Wv2, mask1, causal=False)
        x2 = _layernorm(x1 + z, ln2_g, ln2_b)
        z = jnp.maximum(x2 @ fc1_w.T + fc1_b, 0.0) * mask0
        z = (z @ fc2_w.T + fc2_b) * mask0
        return _layernorm(x2 + z, ln3_g, ln3_b)

    def _L2_xattn_ref(depth_feat, context_feat, depth_pos, e_wq, e_wk, e_wv, e_wm, e_w1, e_w2, e_g1, e_b1, e_g2, e_b2, d_wq0, d_wk0, d_wv0, d_wm0, d_wq1, d_wk1, d_wv1, d_wm1, d_w1, d_w2, d_g0, d_b0, d_g1, d_b1, d_g2, d_b2):
        import jax, jax.numpy as jnp
        import numpy as np
        N, L, C, NHEAD = (4, 256, 128, 8)
        D = C // NHEAD
        EPS_ATTN = 1e-06
        EPS_LN = 1e-05

        def _w(key, shape, scale=0.02):
            return jax.random.normal(key, shape, dtype=jnp.float32) * scale

        def layernorm(x, g, b):
            m = jnp.mean(x, axis=-1, keepdims=True)
            v = jnp.mean(jnp.square(x - m), axis=-1, keepdims=True)
            return (x - m) * jax.lax.rsqrt(v + EPS_LN) * g + b

        def linear_attention(q, k, v):
            Q = jax.nn.elu(q) + 1.0
            K = jax.nn.elu(k) + 1.0
            vlen = v.shape[1]
            v = v / vlen
            KV = jnp.einsum('nshd,nshv->nhdv', K, v)
            Z = 1.0 / (jnp.einsum('nlhd,nhd->nlh', Q, K.sum(axis=1)) + EPS_ATTN)
            out = jnp.einsum('nlhd,nhdv,nlh->nlhv', Q, KV, Z) * vlen
            return out

        def heads(x):
            n, l, c = x.shape
            return x.reshape(n, l, NHEAD, D)

        def encoder_layer(x, wq, wk, wv, wm, w1, w2, g1, b1, g2, b2):
            n, l, c = x.shape
            msg = linear_attention(heads(x @ wq), heads(x @ wk), heads(x @ wv))
            msg = msg.reshape(n, l, c) @ wm
            x = x + layernorm(msg, g1, b1)
            x = x + layernorm(jax.nn.relu(x @ w1) @ w2, g2, b2)
            return x

        def decoder_layer(x, src, wq0, wk0, wv0, wm0, wq1, wk1, wv1, wm1, w1, w2, g0, b0, g1, b1, g2, b2):
            n, l, c = x.shape
            msg = linear_attention(heads(x @ wq0), heads(x @ wk0), heads(x @ wv0))
            msg = msg.reshape(n, l, c) @ wm0
            x = x + layernorm(msg, g0, b0)
            msg = linear_attention(heads(x @ wq1), heads(src @ wk1), heads(src @ wv1))
            msg = msg.reshape(n, l, c) @ wm1
            x = x + layernorm(msg, g1, b1)
            x = x + layernorm(jax.nn.relu(x @ w1) @ w2, g2, b2)
            return x
        ctx = context_feat + depth_pos
        ctx = encoder_layer(ctx, e_wq, e_wk, e_wv, e_wm, e_w1, e_w2, e_g1, e_b1, e_g2, e_b2)
        out = decoder_layer(depth_feat, ctx, d_wq0, d_wk0, d_wv0, d_wm0, d_wq1, d_wk1, d_wv1, d_wm1, d_w1, d_w2, d_g0, d_b0, d_g1, d_b1, d_g2, d_b2)
        return out

    def _L3_xattn_ref(latents, tokens, sa_ln_g, sa_ln_b, sa_in_w, sa_in_b, sa_out_w, sa_out_b, ca_q_ln_g, ca_q_ln_b, ca_kv_ln_g, ca_kv_ln_b, ca_in_w, ca_in_b, ca_out_w, ca_out_b, moe_ln_g, moe_ln_b, router_w, router_b, e_fc1_w, e_fc1_b, e_fc2_w, e_fc2_b):
        import jax, jax.numpy as jnp
        import numpy as np
        D, H, E, K, DFF = (128, 16, 8, 2, 512)
        B, L, T = (4, 64, 256)
        EPS = 1e-05

        def _xavier(key, shape):
            fan_in, fan_out = (shape[-1], shape[-2])
            a = jnp.sqrt(6.0 / (fan_in + fan_out))
            return jax.random.uniform(key, shape, jnp.float32, -a, a)

        def _ln(x, g, b):
            m = x.mean(-1, keepdims=True)
            v = ((x - m) ** 2).mean(-1, keepdims=True)
            return (x - m) / jnp.sqrt(v + EPS) * g + b

        def _mha(q_in, kv_in, in_w, in_b, out_w, out_b):
            wq, wk, wv = jnp.split(in_w, 3, axis=0)
            bq, bk, bv = jnp.split(in_b, 3, axis=0)
            dh = D // H

            def heads(x, w, b):
                y = x @ w.T + b
                return y.reshape(x.shape[0], x.shape[1], H, dh).transpose(0, 2, 1, 3)
            q = heads(q_in, wq, bq)
            k = heads(kv_in, wk, bk)
            v = heads(kv_in, wv, bv)
            scores = jnp.einsum('bhqd,bhkd->bhqk', q, k) / jnp.sqrt(jnp.float32(dh))
            attn = jax.nn.softmax(scores, axis=-1)
            out = jnp.einsum('bhqk,bhkd->bhqd', attn, v)
            out = out.transpose(0, 2, 1, 3).reshape(q_in.shape[0], q_in.shape[1], D)
            return out @ out_w.T + out_b

        def _fuse_moe(x, ln_g, ln_b, rw, rb, fc1_w, fc1_b, fc2_w, fc2_b):
            h = _ln(x, ln_g, ln_b)
            logits = h @ rw.T + rb
            vals, idx = jax.lax.top_k(logits, K)
            gates = jax.nn.softmax(vals, axis=-1)
            N = x.shape[0] * x.shape[1]
            hf = h.reshape(N, D)
            h1 = jax.nn.gelu(jnp.einsum('nd,efd->enf', hf, fc1_w) + fc1_b[:, None, :], approximate=False)
            eo = jnp.einsum('enf,edf->end', h1, fc2_w) + fc2_b[:, None, :]
            idx_f = idx.reshape(N, K)
            gates_f = gates.reshape(N, K)
            gathered = eo[idx_f, jnp.arange(N)[:, None], :]
            mixed = (gathered * gates_f[..., None]).sum(axis=1).reshape(x.shape)
            return x + mixed
        q = _ln(latents, sa_ln_g, sa_ln_b)
        x = latents + _mha(q, q, sa_in_w, sa_in_b, sa_out_w, sa_out_b)
        qc = _ln(x, ca_q_ln_g, ca_q_ln_b)
        kv = _ln(tokens, ca_kv_ln_g, ca_kv_ln_b)
        x = x + _mha(qc, kv, ca_in_w, ca_in_b, ca_out_w, ca_out_b)
        return _fuse_moe(x, moe_ln_g, moe_ln_b, router_w, router_b, e_fc1_w, e_fc1_b, e_fc2_w, e_fc2_b)
    x = _L0_xattn_ref(x, ctx_1024, mask_1x1xSxS2_ik0, mask_1x1xSxS2_if1, L0_xattn_wq_s, L0_xattn_bq_s, L0_xattn_wk_s, L0_xattn_bk_s, L0_xattn_wv_s, L0_xattn_bv_s, L0_xattn_wo_s, L0_xattn_bo_s, L0_xattn_wq_c, L0_xattn_bq_c, L0_xattn_wk_c, L0_xattn_bk_c, L0_xattn_wv_c, L0_xattn_bv_c, L0_xattn_wo_c, L0_xattn_bo_c, L0_xattn_ff1_w, L0_xattn_ff1_b, L0_xattn_ff2_w, L0_xattn_ff2_b, L0_xattn_ln1_g, L0_xattn_ln1_b, L0_xattn_ln2_g, L0_xattn_ln2_b, L0_xattn_ln3_g, L0_xattn_ln3_b)
    x = _L1_xattn_ref(x, ctx_1024, L1_xattn_Wq1, L1_xattn_Wk1, L1_xattn_Wv1, L1_xattn_Wq2, L1_xattn_Wk2, L1_xattn_Wv2, L1_xattn_ln1_g, L1_xattn_ln1_b, L1_xattn_ln2_g, L1_xattn_ln2_b, L1_xattn_ln3_g, L1_xattn_ln3_b, L1_xattn_fc1_w, L1_xattn_fc1_b, L1_xattn_fc2_w, L1_xattn_fc2_b)
    x = _L2_xattn_ref(x, ctx_1024, ctx_1024, L2_xattn_e_wq, L2_xattn_e_wk, L2_xattn_e_wv, L2_xattn_e_wm, L2_xattn_e_w1, L2_xattn_e_w2, L2_xattn_e_g1, L2_xattn_e_b1, L2_xattn_e_g2, L2_xattn_e_b2, L2_xattn_d_wq0, L2_xattn_d_wk0, L2_xattn_d_wv0, L2_xattn_d_wm0, L2_xattn_d_wq1, L2_xattn_d_wk1, L2_xattn_d_wv1, L2_xattn_d_wm1, L2_xattn_d_w1, L2_xattn_d_w2, L2_xattn_d_g0, L2_xattn_d_b0, L2_xattn_d_g1, L2_xattn_d_b1, L2_xattn_d_g2, L2_xattn_d_b2)
    x = _L3_xattn_ref(x, ctx_1024, L3_xattn_sa_ln_g, L3_xattn_sa_ln_b, L3_xattn_sa_in_w, L3_xattn_sa_in_b, L3_xattn_sa_out_w, L3_xattn_sa_out_b, L3_xattn_ca_q_ln_g, L3_xattn_ca_q_ln_b, L3_xattn_ca_kv_ln_g, L3_xattn_ca_kv_ln_b, L3_xattn_ca_in_w, L3_xattn_ca_in_b, L3_xattn_ca_out_w, L3_xattn_ca_out_b, L3_xattn_moe_ln_g, L3_xattn_moe_ln_b, L3_xattn_router_w, L3_xattn_router_b, L3_xattn_e_fc1_w, L3_xattn_e_fc1_b, L3_xattn_e_fc2_w, L3_xattn_e_fc2_b)
    return x

_drawn_inputs = setup_inputs


def setup_inputs(seed=0):
    import zlib

    import numpy as np

    out = dict(_drawn_inputs(seed))
    spreads = {'L0_xattn_ln1_g': (1.0, 0.2),
     'L0_xattn_ln1_b': (0.0, 0.1),
     'L0_xattn_ln2_g': (1.0, 0.2),
     'L0_xattn_ln2_b': (0.0, 0.1),
     'L0_xattn_ln3_g': (1.0, 0.2),
     'L0_xattn_ln3_b': (0.0, 0.1),
     'L1_xattn_ln1_g': (1.0, 0.2),
     'L1_xattn_ln1_b': (0.0, 0.1),
     'L1_xattn_ln2_g': (1.0, 0.2),
     'L1_xattn_ln2_b': (0.0, 0.1),
     'L1_xattn_ln3_g': (1.0, 0.2),
     'L1_xattn_ln3_b': (0.0, 0.1),
     'L1_xattn_fc1_b': (0.0, 0.276),
     'L1_xattn_fc2_b': (0.0, 0.1),
     'L2_xattn_e_g1': (1.0, 0.2),
     'L2_xattn_e_b1': (0.0, 0.1),
     'L2_xattn_e_g2': (1.0, 0.2),
     'L2_xattn_e_b2': (0.0, 0.1),
     'L2_xattn_d_g0': (1.0, 0.2),
     'L2_xattn_d_b0': (0.0, 0.1),
     'L2_xattn_d_g1': (1.0, 0.2),
     'L2_xattn_d_b1': (0.0, 0.1),
     'L2_xattn_d_g2': (1.0, 0.2),
     'L2_xattn_d_b2': (0.0, 0.1),
     'L3_xattn_sa_ln_g': (1.0, 0.2),
     'L3_xattn_sa_ln_b': (0.0, 0.1),
     'L3_xattn_sa_in_b': (0.0, 0.1),
     'L3_xattn_sa_out_b': (0.0, 0.1),
     'L3_xattn_ca_q_ln_g': (1.0, 0.6),
     'L3_xattn_ca_q_ln_b': (0.0, 0.8),
     'L3_xattn_ca_kv_ln_g': (1.0, 0.2),
     'L3_xattn_ca_kv_ln_b': (0.0, 0.1),
     'L3_xattn_ca_in_b': (0.0, 0.1),
     'L3_xattn_ca_out_b': (0.0, 0.1),
     'L3_xattn_moe_ln_g': (1.0, 0.2),
     'L3_xattn_moe_ln_b': (0.0, 0.321),
     'L3_xattn_router_b': (0.0, 0.1),
     'L3_xattn_e_fc1_b': (0.0, 0.295),
     'L3_xattn_e_fc2_b': (0.0, 0.1)}
    factors = {'L0_xattn_wq_s': 8.0,
     'L0_xattn_bq_s': 43.314,
     'L0_xattn_wk_s': 8.0,
     'L0_xattn_bk_s': 64.0,
     'L0_xattn_bv_s': 5.849,
     'L0_xattn_wq_c': 8.0,
     'L0_xattn_bq_c': 42.824,
     'L0_xattn_wk_c': 8.0,
     'L0_xattn_bk_c': 64.0,
     'L0_xattn_bv_c': 5.65,
     'L0_xattn_ff1_b': 5.094,
     'L1_xattn_Wq1': 8.0,
     'L1_xattn_Wk1': 8.0,
     'L1_xattn_Wq2': 8.0,
     'L1_xattn_Wk2': 8.0,
     'L2_xattn_e_wq': 8.0,
     'L2_xattn_e_wk': 3.146,
     'L2_xattn_d_wq0': 8.0,
     'L2_xattn_d_wk0': 3.057,
     'L2_xattn_d_wq1': 6.973,
     'L2_xattn_d_wk1': 2.785}
    for name, (base, spread) in spreads.items():
        noise = np.random.default_rng([zlib.crc32(name.encode()), seed]).standard_normal(out[name].shape)
        drawn = base * np.exp(spread * noise) if base else spread * noise
        out[name] = jnp.asarray(drawn.astype(out[name].dtype))
    for name, factor in factors.items():
        out[name] = (out[name] * factor).astype(out[name].dtype)
    return out
```

```python
import concourse.bass as bass
from concourse import mybir
from contextlib import ExitStack
import numpy as np

BATCHES, SEQ, D = 8, 256, 128
HEADS, HD = 16, 8
LHEADS, LHD = 8, 16
EXPERTS, DFF = 8, 512
QT = SEQ // 128
NB = 1
STREAMS = 2
T = NB * SEQ
TT = NB * QT
ROUNDS = BATCHES // (NB * STREAMS)
GROUP = 4
GROUPS = HEADS // GROUP
PAIRS = GROUP * NB
TILES = PAIRS // 2
EPS = 1e-5
MASKED = -1e30
HUGE = 3e38
ATTN_SCALE = 1.0 / float(np.sqrt(HD))
SPLIT_ROWS, LEN_ROW, MAX_ROW = 48, 64, 96

MATS = [
    [("L0_q", 128), ("L0_k", 128), ("L0_v", 128), ("L0_o", 128), ("L0_cq", 128), ("L0_ck", 128), ("L0_cv", 128),
     ("L0_co", 128), ("L0_f1", 512), ("L0_f2", 512)],
    [("L1_q", 128), ("L1_k", 128), ("L1_v", 128), ("L1_cq", 128), ("L1_ck", 128), ("L1_cv", 128), ("L1_f1", 128),
     ("L1_f2", 128)],
    [("E_q", 128), ("E_k", 128), ("E_v", 128), ("E_m", 128), ("E_f1", 256), ("E_f2", 256),
     ("S_q", 128), ("S_k", 128), ("S_v", 128), ("S_m", 128), ("C_q", 128), ("C_k", 128), ("C_v", 128), ("C_m", 128),
     ("D_f1", 256), ("D_f2", 256)],
    [("L3_q", 128), ("L3_k", 128), ("L3_v", 128), ("L3_o", 128), ("L3_cq", 128), ("L3_ck", 128), ("L3_cv", 128),
     ("L3_co", 128), ("L3_r", 8)],
    [("M_f1", EXPERTS * DFF), ("M_f2", EXPERTS * DFF)],
]
COLS = [("L0_bq", 1), ("L0_bk", 1), ("L0_bv", 1), ("L0_cbq", 1), ("L0_cbk", 1), ("L0_cbv", 1), ("L0_fb1", 4),
        ("L0_g1", 1), ("L0_b1", 1), ("L0_g2", 1), ("L0_b2", 1), ("L0_g3", 1), ("L0_b3", 1),
        ("L1_g1", 1), ("L1_b1", 1), ("L1_g2", 1), ("L1_b2", 1), ("L1_g3", 1), ("L1_b3", 1), ("L1_fb1", 1),
        ("L3_bq", 1), ("L3_bk", 1), ("L3_bv", 1), ("L3_cbq", 1), ("L3_cbk", 1), ("L3_cbv", 1),
        ("L3_g1", 1), ("L3_b1", 1), ("L3_g2", 1), ("L3_b2", 1), ("L3_gk", 1), ("L3_bkv", 1), ("L3_g3", 1), ("L3_b3", 1),
        ("M_fb1", EXPERTS * DFF // 128)]
ROWS = [("L0_bo", 128), ("L0_cbo", 128), ("L0_fb2", 128), ("L0_g1", 128), ("L0_b1", 128), ("L0_g2", 128),
        ("L0_b2", 128), ("L0_g3", 128), ("L0_b3", 128),
        ("L1_g1", 128), ("L1_b1", 128), ("L1_g2", 128), ("L1_b2", 128), ("L1_g3", 128), ("L1_b3", 128), ("L1_fb2", 128),
        ("E_g1", 128), ("E_b1", 128), ("E_g2", 128), ("E_b2", 128), ("D_g0", 128), ("D_b0", 128),
        ("D_g1", 128), ("D_b1", 128), ("D_g2", 128), ("D_b2", 128),
        ("L3_bo", 128), ("L3_cbo", 128), ("L3_rb", 8)]


def places(entries):
    at, out = 0, {}
    for name, n in entries:
        out[name] = (at, n)
        at += n
    return out, at


MAT_AT, MAT_COLS = places([e for part in MATS for e in part])
PART_ENDS = [sum(n for part in MATS[:i + 1] for _, n in part) for i in range(len(MATS))]
COL_AT, COL_COLS = places(COLS)
ROW_AT, ROW_COLS = places(ROWS)
PART_OF = {name: i for i, part in enumerate(MATS) for name, _ in part}


def expert_uses():
    out = [("bias", 0, 0)]
    for e in range(EXPERTS + 1):
        if e < EXPERTS:
            out += [("up", e, c) for c in range(DFF // 128)]
        if e >= 1:
            out.append(("down", e - 1, 0))
    return out


def uses(kind, p):
    if kind == "turn":
        return {"turned": 1}, [("turned", 1)]
    if kind == "norm":
        return {"variance": 1, "rstd": 1, "normed": 1}, []
    if kind == "affine":
        return ({"summed": 1} if p["plus"] else {"affined": 1}), []
    if kind == "rowmask":
        return ({"rowmask": 1, "row_kept": 1} if p["kv"] else {"rowmask": 1}), []
    if kind == "qkv":
        n = {"q_read": 1, "q_split": 1, "k_read": 1, "k_rest": 1, "k_second": 1, "k_split": 1, "v_ready": 1}
        w = [("q_read", 1), ("k_read", 1), ("v_ready", 1)]
        if p["lengths"]:
            n |= {"q_first": 1, "len_read": 1, "len_row": 1}
            w.append(("len_read", 1))
        return n, w
    if kind == "slot":
        g, n, w = p["g"], {}, []
        if g < GROUPS:
            n |= {"stile": TILES}
        if 0 <= g - 4 < GROUPS:
            n |= {"out_scaled": 1}
            w.append(("out_scaled", 1))
        if 0 <= g - 1 < GROUPS:
            n |= {"neg_parts": 1, "neg_turned": 1}
            w.append(("neg_turned", 1))
        if 0 <= g - 2 < GROUPS:
            n |= {"prob": PAIRS}
        if 0 <= g - 3 < GROUPS:
            n |= {"out_copied": 1}
            w.append(("out_copied", 1))
        return n, w
    if kind == "project":
        return {"turned": 1, "out_read": 1, "residual": 1}, [("turned", 1), ("out_read", 1)]
    if kind == "addz":
        return {"residual": 1}, []
    if kind == "ff":
        c = p["chunks"]
        w = [("hidden", i + 1) for i in range(c)]
        if p["b2"]:
            return {"hidden": c, "ff_read": 1, "residual": 1}, [*w, ("ff_read", 1)]
        return {"hidden": c, "residual": 1}, [*w, ("residual", 1)]
    if kind == "linear":
        n = {"lin_min": 2, "lin_exp": 2, "lin_feature": 2, "lin_v": 1, "lin_kv": NB, "lin_out": NB, "turned": 1,
             "residual": 1}
        w = [("lin_feature", 1), ("lin_feature", 2), ("lin_v", 1)] + [("lin_kv", b + 1) for b in range(NB)]
        return n, w + [("lin_out", b + 1) for b in range(NB)] + [("turned", 1), ("residual", 1)]
    if kind == "route":
        return ({"route_read": 1, "gate_diff": 1, "gate_exp": 1, "gates": 1, "gates_turned": 1},
                [("route_read", 1), ("gates_turned", 1)])
    if kind == "experts":
        w, hidden, mixed = [], 0, 0
        for what, e, c in expert_uses():
            if what == "up":
                hidden += 1
                w.append(("hidden", hidden))
            else:
                mixed += 1
                w.append(("expert_mixed", mixed))
        return {"hidden": hidden, "expert_mixed": mixed}, w
    if kind == "load":
        return {"doubled": 1}, []
    return {}, []


def stream_steps(s):
    out = []

    def add(kind, name, **p):
        out.append((kind, s, name, p))

    def attention(n, q_from, kv_from, w, bias, mask, lengths):
        add("qkv", n, q_from=q_from, kv_from=kv_from, w_names=w, bias=bias, lengths=lengths)
        for g in range(GROUPS + 4):
            add("slot", f"{n}/{g}", attn=n, g=g, mask=mask, lengths=lengths)

    add("load", "load")
    add("turn", "x", src="X", dst="XT", g=None, after=("load",))
    add("turn", "c", src="C", dst="CT", g=None, after=("load",))
    attention("a0", "XT", "XT", ("L0_q", "L0_k", "L0_v"), ("L0_bq", "L0_bk"), 0, False)
    add("project", "o0", attn="a0", wo="L0_o", bv="L0_bv", bo="L0_bo", acc="R")
    add("norm", "n0", src="R")
    add("turn", "h1", src="XH", dst="XT", g=("L0_g1", "L0_b1"), after=("norm", "n0"))
    add("affine", "f0", g="L0_g1", b="L0_b1", dst="X", plus=None)
    attention("a1", "XT", "CT", ("L0_cq", "L0_ck", "L0_cv"), ("L0_cbq", "L0_cbk"), 1, False)
    add("project", "o1", attn="a1", wo="L0_co", bv="L0_cbv", bo="L0_cbo", acc="R")
    add("norm", "n1", src="R")
    add("turn", "h2", src="XH", dst="XT", g=("L0_g2", "L0_b2"), after=("norm", "n1"))
    add("affine", "f1", g="L0_g2", b="L0_b2", dst="X", plus=None)
    add("ff", "ff0", x="XT", w1="L0_f1", b1="L0_fb1", w2="L0_f2", b2="L0_fb2", chunks=4, mask=None)
    add("norm", "n2", src="R")
    add("turn", "x1", src="XH", dst="XT", g=("L0_g3", "L0_b3"), after=("norm", "n2"))
    add("affine", "f2", g="L0_g3", b="L0_b3", dst="X", plus=None)
    add("rowmask", "m0", dst="M0", kv=False)
    attention("a2", "XT", "XT", ("L1_q", "L1_k", "L1_v"), (None, None), "causal", True)
    add("addz", "z0", mask="M0")
    add("norm", "n3", src="R")
    add("turn", "y1", src="XH", dst="XT", g=("L1_g1", "L1_b1"), after=("norm", "n3"))
    add("affine", "f3", g="L1_g1", b="L1_b1", dst="X", plus=None)
    add("rowmask", "m1", dst="M1", kv=True)
    add("turn", "cm", src="CM", dst="CMT", g=None, after=("rowmask", "m1"))
    attention("a3", "XT", "CMT", ("L1_cq", "L1_ck", "L1_cv"), (None, None), None, True)
    add("addz", "z1", mask="M1")
    add("norm", "n4", src="R")
    add("turn", "y2", src="XH", dst="XT", g=("L1_g2", "L1_b2"), after=("norm", "n4"))
    add("affine", "f4", g="L1_g2", b="L1_b2", dst="X", plus=None)
    add("ff", "ff1", x="XT", w1="L1_f1", b1="L1_fb1", w2="L1_f2", b2="L1_fb2", chunks=1, mask="M0")
    add("norm", "n5", src="R")
    add("turn", "x2", src="XH", dst="XT", g=("L1_g3", "L1_b3"), after=("norm", "n5"))
    add("affine", "f5", g="L1_g3", b="L1_b3", dst="X", plus=None)
    add("turn", "e0", src="CC", dst="ET", g=None, after=("load",))
    add("linear", "le", q="ET", kv="ET", w_names=("E_q", "E_k", "E_v", "E_m"))
    add("norm", "n6", src="R")
    add("affine", "f6", g="E_g1", b="E_b1", dst="CC", plus="CC")
    add("turn", "e1", src="CC", dst="ET", g=None, after=("affine", "f6"))
    add("ff", "ffe", x="ET", w1="E_f1", b1=None, w2="E_f2", b2=None, chunks=2, mask=None)
    add("norm", "n7", src="R")
    add("affine", "f7", g="E_g2", b="E_b2", dst="CC", plus="CC")
    add("turn", "e2", src="CC", dst="ET", g=None, after=("affine", "f7"))
    add("linear", "ls", q="XT", kv="XT", w_names=("S_q", "S_k", "S_v", "S_m"))
    add("norm", "n8", src="R")
    add("affine", "f8", g="D_g0", b="D_b0", dst="X", plus="X")
    add("turn", "d0", src="X", dst="XT", g=None, after=("affine", "f8"))
    add("linear", "lc", q="XT", kv="ET", w_names=("C_q", "C_k", "C_v", "C_m"))
    add("norm", "n9", src="R")
    add("affine", "f9", g="D_g1", b="D_b1", dst="X", plus="X")
    add("turn", "d1", src="X", dst="XT", g=None, after=("affine", "f9"))
    add("ff", "ffd", x="XT", w1="D_f1", b1=None, w2="D_f2", b2=None, chunks=2, mask=None)
    add("norm", "n10", src="R")
    add("affine", "f10", g="D_g2", b="D_b2", dst="X", plus="X")
    add("norm", "n11", src="X")
    add("turn", "q3", src="XH", dst="XT", g=("L3_g1", "L3_b1"), after=("norm", "n11"))
    attention("a4", "XT", "XT", ("L3_q", "L3_k", "L3_v"), ("L3_bq", "L3_bk"), None, False)
    add("project", "o4", attn="a4", wo="L3_o", bv="L3_bv", bo="L3_bo", acc="X")
    add("norm", "n12", src="C")
    add("turn", "k3", src="XH", dst="CT", g=("L3_gk", "L3_bkv"), after=("norm", "n12"))
    add("norm", "n13", src="X")
    add("turn", "q4", src="XH", dst="XT", g=("L3_g2", "L3_b2"), after=("norm", "n13"))
    attention("a5", "XT", "CT", ("L3_cq", "L3_ck", "L3_cv"), ("L3_cbq", "L3_cbk"), None, False)
    add("project", "o5", attn="a5", wo="L3_co", bv="L3_cbv", bo="L3_cbo", acc="X")
    add("norm", "n14", src="X")
    add("turn", "h3", src="XH", dst="XT", g=("L3_g3", "L3_b3"), after=("norm", "n14"))
    add("route", "r")
    add("experts", "mix")
    add("store", "store")
    return out


class Step:

    def __init__(self, kind, s, name, p, base, end, own, w):
        self.kind, self.s, self.name, self.base, self.end, self.own, self.w = kind, s, name, base, end, own, w
        self.src, self.dst, self.after, self.plus, self.kv = (p.get(n) for n in ("src", "dst", "after", "plus", "kv"))
        self.acc, self.mask, self.b = p.get("acc"), p.get("mask"), p.get("b")
        self.g = p.get("g")
        self.attn, self.lengths, self.bias, self.w_names = (p.get(n) for n in ("attn", "lengths", "bias", "w_names"))
        self.q_from, self.kv_from, self.q = (p.get(n) for n in ("q_from", "kv_from", "q"))
        self.wo, self.bv, self.bo = p.get("wo"), p.get("bv"), p.get("bo")
        self.x, self.w1, self.b1, self.w2, self.b2, self.chunks = (
            p.get(n) for n in ("x", "w1", "b1", "w2", "b2", "chunks"))


def plan():
    lists = [stream_steps(s) for s in range(STREAMS)]
    count, steps, by, released = {}, [], {}, []
    own = [{} for _ in range(STREAMS)]
    for entries in zip(*lists):
        for kind, s, name, p in entries:
            n, wide = uses(kind, p)
            base = dict(count)
            for what, k in n.items():
                count[what] = count.get(what, 0) + k
            st = Step(kind, s, name, p, base, dict(count), dict(own[s]), len(released))
            own[s] |= {what: count[what] for what in n}
            released += [(what, base.get(what, 0) + k) for what, k in wide]
            steps.append(st)
            by[s, name] = st
    return steps, by, released, sorted(count)


def build(nc, x, ctx, mask0, mask1, mats, cols, rows, fc2_bias, out):
    f32, bf16, i32, u32 = mybir.dt.float32, mybir.dt.bfloat16, mybir.dt.int32, mybir.dt.uint32
    ALU, ACT, AX = mybir.AluOpType, mybir.ActivationFunctionType, mybir.AxisListType
    steps, by, released, counted = plan()
    x_tok = x.rearrange("n (t p) d -> p n t d", p=128)
    ctx_tok = ctx.rearrange("n (t p) d -> p n t d", p=128)
    out_tok = out.rearrange("n (t p) d -> p n t d", p=128)

    with ExitStack() as stack:
        def sb(name, shape, dt=f32):
            return stack.enter_context(nc.sbuf_tensor(name, shape, dt))

        def psum(name, shape):
            return stack.enter_context(nc.psum_tensor(name, shape, f32))

        def per_stream(name, shape, dt=f32):
            return [sb(f"{name}{s}", shape, dt) for s in range(STREAMS)]

        MAT = sb("MAT", [128, MAT_COLS])
        COL = sb("COL", [128, COL_COLS])
        ROW = sb("ROW", [128, ROW_COLS])
        FC2B = sb("FC2B", [EXPERTS, D])
        identf = sb("identf", [128, 128])
        identb = sb("identb", [128, 128], bf16)
        head_mask = sb("head_mask", [128, HEADS])
        block_mask = sb("block_mask", [128, LHEADS, LHD])
        block_sum = sb("block_sum", [128, LHEADS])
        expert_no = sb("expert_no", [128, EXPERTS])
        key_no = sb("key_no", [HEADS, SEQ])
        minus_half = sb("minus_half", [128, TT])
        no_len = sb("no_len", [HEADS, T], bf16)
        causal_q = sb("causal_q", [128, 128], bf16)
        causal_k = sb("causal_k", [128, 128], bf16)
        mask_any = sb("mask_any", [128, 2, QT])
        mask_q = sb("mask_q", [128, 2, QT, SEQ], bf16)
        mask_k = sb("mask_k", [128, 2, QT, SEQ], bf16)
        row_nan = sb("row_nan", [128, 2, NB, QT])

        X, C, CC, CM = (per_stream(n, [128, TT, D]) for n in ("X", "C", "CC", "CM"))
        R, XH, AF, OT = (per_stream(n, [128, TT, D]) for n in ("R", "XH", "AF", "OT"))
        XT, CT, ET, OF = (per_stream(n, [128, T]) for n in ("XT", "CT", "ET", "OF"))
        CMT = ET
        BN = per_stream("BN", [128, TT, 6])
        MV = per_stream("MV", [128, TT, 2])
        RS = per_stream("RS", [128, TT])
        AM = per_stream("AM", [128, TT])
        M0, M1 = per_stream("M0", [128, TT]), per_stream("M1", [128, TT])
        Q32, K32, QR, KR = (per_stream(n, [128, T]) for n in ("Q32", "K32", "QR", "KR"))
        Q3, K3 = per_stream("Q3", [128, 3, T], bf16), per_stream("K3", [128, 3, T], bf16)
        SQ, SK = per_stream("SQ", [128, HEADS, T], bf16), per_stream("SK", [128, HEADS, T], bf16)
        V = per_stream("V", [128, TT, HEADS, 32])
        QF = per_stream("QF", [128, NB, HEADS])
        NZ = per_stream("NZ", [HEADS, NB, SEQ])
        LEN, LNAN = per_stream("LEN", [HEADS, NB]), per_stream("LNAN", [HEADS, NB])
        LB = per_stream("LB", [HEADS, T], bf16)
        NEG = per_stream("NEG", [128, HEADS * TT])
        HL = per_stream("HL", [128, 2, TT, 2 * GROUP], bf16)
        HF = per_stream("HF", [128, TT, GROUP])
        MT = per_stream("MT", [2 * GROUP, 2, T], bf16)
        P = per_stream("P", [128, 2, PAIRS, 2 * SEQ])
        OG = per_stream("OG", [128, 2, T])
        RC = per_stream("RC", [128, TT, GROUP])
        room = [P[s][:, :, :, :].rearrange("p a i k -> p a (i k)") for s in range(STREAMS)]
        HB = [r[:, :, 0:4 * T].rearrange("p a (c t) -> p a c t", c=4) for r in room]
        LM = [r[:, 0, 4 * T:6 * T].rearrange("p (i t) -> p i t", i=2) for r in room]
        LE = [r[:, 0, 6 * T:8 * T].rearrange("p (i t) -> p i t", i=2) for r in room]
        LQ = [r[:, 1, 4 * T:5 * T] for r in room]
        LK = [r[:, 1, 5 * T:6 * T].rearrange("p (t d) -> p t d", d=D) for r in room]
        mask_in = room[0][:, 0, 0:2 * QT * SEQ].rearrange("p (m k) -> p m k", m=2).bitcast(i32)
        mask_vis = room[0][:, 1, 0:2 * QT * SEQ].rearrange("p (m k) -> p m k", m=2)
        LV = per_stream("LV", [128, TT, D + 1])
        KVB = per_stream("KVB", [128, NB, D + LHEADS])
        LZ = per_stream("LZ", [128, 2, LHEADS])
        LG, MX = per_stream("LG", [128, TT, EXPERTS]), per_stream("MX", [128, TT, 8])
        IX, IXF = per_stream("IX", [128, TT, 8], u32), per_stream("IXF", [128, TT, 2])
        GD, GE, GP, GQ = (per_stream(n, [128, TT]) for n in ("GD", "GE", "GP", "GQ"))
        G, G2 = per_stream("G", [128, TT, EXPERTS]), per_stream("G2", [128, TT, EXPERTS])
        GT = per_stream("GT", [EXPERTS, T])

        SA = [psum(f"SA{i}", [128, 4 * SEQ]) for i in range(2)]
        ST = [psum(f"ST{i}", [128, 2 * SEQ]) for i in range(2)]
        W = [psum(f"W{i}", [128, 512]) for i in range(2)]

        consts_loaded = nc.alloc_semaphore("consts_loaded")
        pool_consts = nc.alloc_semaphore("pool_consts")
        dve_consts = nc.alloc_semaphore("dve_consts")
        mask_turned = nc.alloc_semaphore("mask_turned")
        mask_copied = nc.alloc_semaphore("mask_copied")
        mats_loaded = [nc.alloc_semaphore(f"mats_loaded{i}") for i in range(len(MATS))]
        sem = {n: nc.alloc_semaphore(n) for n in counted}
        wide_full = nc.alloc_semaphore("wide_full")
        tile_full = nc.alloc_semaphore("tile_full")
        prob_full = nc.alloc_semaphore("prob_full")
        dve_chain = nc.alloc_semaphore("dve_chain")
        pool_chain = nc.alloc_semaphore("pool_chain")
        loaded = [nc.alloc_semaphore(f"loaded{s}") for s in range(STREAMS)]
        stacked = [nc.alloc_semaphore(f"stacked{s}") for s in range(STREAMS)]
        neg_row = [[nc.alloc_semaphore(f"neg_row{s}_{i}") for i in range(2)] for s in range(STREAMS)]
        stored = nc.alloc_semaphore("stored")
        of_round = [*sem.values(), wide_full, tile_full, prob_full, dve_chain, pool_chain, *loaded, *stacked,
                    *neg_row[0], *(neg_row[1] if STREAMS > 1 else []), stored]
        numbers = [h.num for h in of_round]
        assert sorted(numbers) == list(range(min(numbers), max(numbers) + 1))

        def mat(name, chunk=0, width=None):
            at, n = MAT_AT[name]
            width = width or n
            return MAT[:, at + chunk * width:at + (chunk + 1) * width]

        def col(name, i=0):
            at = COL_AT[name][0] + i
            return COL[:, at:at + 1]

        def row(name):
            at, n = ROW_AT[name]
            return ROW[:, at:at + n].unsqueeze(1).to_broadcast([128, TT, n])

        def attention_no(st, name):
            return int(name[1:])

        STACK_DMAS = 13

        with nc.Block() as block:
            @block.sync
            def _(sp):
                sp.dma_start(COL[:, :], cols).then_inc(consts_loaded, 16)
                sp.dma_start(mask_in[:, 0, :].rearrange("p (t k) -> p t k", t=QT),
                             mask0.rearrange("(t p) k -> p t k", p=128)).then_inc(consts_loaded, 16)
                sp.dma_start(mask_in[:, 1, :].rearrange("p (t k) -> p t k", t=QT),
                             mask1.rearrange("(t p) k -> p t k", p=128)).then_inc(consts_loaded, 16)
                sp.dma_start(ROW[:, :], rows.partition_broadcast(128)).then_inc(consts_loaded, 16)
                sp.dma_start(FC2B[:, :], fc2_bias).then_inc(consts_loaded, 16)
                for i, end in enumerate(PART_ENDS):
                    at = PART_ENDS[i - 1] if i else 0
                    sp.dma_start(MAT[:, at:end], mats[:, at:end]).then_inc(mats_loaded[i], 16)
                sp.wait_ge(consts_loaded, 80)

            @block.gpsimd
            def _(pool):
                made = [0]

                def link(ins):
                    made[0] += 1
                    ins.then_inc(pool_consts, 1)
                    pool.wait_ge(pool_consts, made[0])

                def select(dst, pattern, op, fill, base, per_partition):
                    link(pool.affine_select(out=dst, in_=dst, pattern=pattern, compare_op=op, fill=fill, base=base,
                                            channel_multiplier=per_partition))

                for t in (identf, identb):
                    link(pool.memset(t[:, :], 0.0))
                    select(t[:, :], [[-1, 128]], ALU.not_equal, 1.0, 0, 1)
                for t, shape in ((block_mask[:, :, :], [[-LHD, LHEADS], [0, LHD]]), (block_sum[:, :], [[-LHD, LHEADS]])):
                    link(pool.memset(t, 1.0))
                    select(t, shape, ALU.is_ge, 0.0, 0, 1)
                    select(t, [[LHD if s else 0, n] for s, n in shape], ALU.is_ge, 0.0, LHD - 1, -1)
                link(pool.memset(causal_q[:, :], 0.0))
                select(causal_q[:, :], [[-1, 128]], ALU.is_ge, MASKED, 0, 1)
                link(pool.memset(causal_k[:, :], 0.0))
                select(causal_k[:, :], [[1, 128]], ALU.is_ge, MASKED, 0, -1)
                link(pool.iota(mask_vis[:, 0, 0:EXPERTS].bitcast(i32), pattern=[[1, EXPERTS]], base=0,
                               channel_multiplier=0))
                link(pool.iota(mask_vis[0:HEADS, 1, 0:SEQ].bitcast(i32), pattern=[[1, SEQ]], base=0,
                               channel_multiplier=0))
                link(pool.tensor_copy(expert_no[:, :], mask_vis[:, 0, 0:EXPERTS].bitcast(i32)))
                link(pool.tensor_copy(key_no[:, :], mask_vis[0:HEADS, 1, 0:SEQ].bitcast(i32)))
                pool.sem_inc(pool_consts, 100)

            @block.vector
            def _(dve):
                made = [0]

                def link(ins):
                    made[0] += 1
                    ins.then_inc(dve_consts, 1)
                    dve.wait_ge(dve_consts, made[0])

                for s in range(STREAMS):
                    dve.memset(SQ[s][:, :, :], 0.0)
                    dve.memset(SK[s][:, :, :], 0.0)
                    dve.memset(V[s][:, :, :, :], 0.0)
                    dve.memset(LV[s][:, :, D:D + 1], 1.0)
                dve.memset(no_len[:, :], 0.0)
                link(dve.memset(minus_half[:, :], -0.5))
                for s in range(STREAMS):
                    dve.memset(SQ[s][LEN_ROW:LEN_ROW + 1, :, :], 1.0)
                    dve.memset(SK[s][MAX_ROW:MAX_ROW + 2, :, :], 1.0)
                    dve.memset(V[s][:, :, :, HD:HD + 1], 1.0)
                dve.wait_ge(pool_consts, 100)
                dve.tensor_reduce(head_mask[:, :], identf[:, :].rearrange("p (d h) -> p h d", h=HEADS), AX.X, ALU.add)
                dve.wait_ge(consts_loaded, 80)
                dve.tensor_scalar(mask_q[:, :, :, :].rearrange("p m t k -> p m (t k)"), mask_in[:, :, :], 0.0, MASKED,
                                  ALU.is_equal, ALU.mult)
                link(dve.tensor_scalar(mask_vis[:, :, :], mask_in[:, :, :], 0.0, None, ALU.not_equal))
                link(dve.tensor_reduce(mask_any[:, :, :], mask_vis[:, :, :].rearrange("p m (t k) -> p m t k", t=QT),
                                       AX.X, ALU.max))
                for b in range(NB):
                    link(dve.tensor_scalar(row_nan[:, :, b, :], mask_any[:, :, :], 0.0, HUGE, ALU.is_equal, ALU.mult))
                    link(dve.tensor_scalar(row_nan[:, :, b, :], row_nan[:, :, b, :], HUGE, 0.0, ALU.mult, ALU.mult))
                link(dve.memset(LZ[0][:, :, :], 0.0))
                dve.sem_inc(dve_consts, 100)
                for m in range(2):
                    dve.wait_ge(mask_turned, m + 1)
                    dve.tensor_copy(mask_k[:, m, :, :].rearrange("p t k -> p (t k)"), W[m][:, :].bitcast(bf16)[:, 0:QT * SEQ]) \
                       .then_inc(mask_copied, 1)
                dve.wait_ge(mask_copied, 2)

            @block.tensor
            def _(pe):
                pe.wait_ge(dve_consts, 100)
                for m in range(2):
                    for kt in range(QT):
                        for qt in range(QT):
                            at = kt * SEQ + qt * 128
                            last = pe.transpose(W[m][:, :].bitcast(bf16)[:, at:at + 128],
                                                mask_q[:, m, qt, kt * 128:(kt + 1) * 128], identb[:, :])
                    last.then_inc(mask_turned, 1)

        with nc.Fori(0, ROUNDS) as rnd:
            with nc.Block() as block:
                @block.sync
                def _(sp):
                    stacks = [0] * STREAMS

                    def load(st):
                        first = (rnd * STREAMS + st.s) * NB
                        sp.dma_start(X[st.s][:, :, :].rearrange("p (n t) d -> p n t d", n=NB),
                                     x_tok[:, bass.ds(first, NB), :, :]).then_inc(loaded[st.s], 16)
                        sp.dma_start(C[st.s][:, :, :].rearrange("p (n t) d -> p n t d", n=NB),
                                     ctx_tok[:, bass.ds(first, NB), :, :]).then_inc(loaded[st.s], 16)

                    def qkv(st):
                        s = st.s
                        sp.wait_ge(sem["q_split"], st.end["q_split"])
                        for r, part in enumerate((0, 0, 0, 1, 1, 2)):
                            sp.dma_start(SQ[s][HD * r:HD * r + HD, :, :], Q3[s][:, part, :]).then_inc(stacked[s], 16)
                        sp.wait_ge(sem["k_split"], st.end["k_split"])
                        for r, part in enumerate((0, 1, 2, 0, 1, 0)):
                            sp.dma_start(SK[s][HD * r:HD * r + HD, :, :], K3[s][:, part, :]).then_inc(stacked[s], 16)
                        if st.lengths:
                            sp.wait_ge(sem["len_row"], st.end["len_row"])
                        sp.dma_start(SK[s][LEN_ROW:LEN_ROW + 1, :, :], (LB[s] if st.lengths else no_len)[:, :]) \
                          .then_inc(stacked[s], 16)

                    def slot(st):
                        g = st.g - 1
                        if 0 <= g < GROUPS:
                            sp.wait_ge(sem["neg_turned"], st.end["neg_turned"])
                            sp.dma_start(SQ[st.s][MAX_ROW:MAX_ROW + 2, GROUP * g:GROUP * (g + 1), :],
                                         MT[st.s][:, g % 2, :]).then_inc(neg_row[st.s][g % 2], 16)

                    def store(st):
                        sp.wait_ge(sem["expert_mixed"], st.own["expert_mixed"])
                        first = (rnd * STREAMS + st.s) * NB
                        sp.dma_start(out_tok[:, bass.ds(first, NB), :, :],
                                     X[st.s][:, :, :].rearrange("p (n t) d -> p n t d", n=NB)).then_inc(stored, 16)

                    for st in steps:
                        if st.kind in ("load", "qkv", "slot", "store"):
                            {"load": load, "qkv": qkv, "slot": slot, "store": store}[st.kind](st)
                    sp.wait_ge(stored, 16 * STREAMS)

                @block.tensor
                def _(pe):
                    def wide(w):
                        if w >= 2:
                            what, value = released[w - 2]
                            pe.wait_ge(sem[what], value)
                        return W[w % 2]

                    def turn(st):
                        s = st.s
                        src = {"X": X, "C": C, "CC": CC, "CM": CM, "XH": XH}[st.src][s]
                        kind = st.after[0]
                        if kind == "load":
                            pe.wait_ge(loaded[s], 32)
                            if st.src == "CC":
                                pe.wait_ge(sem["doubled"], st.own["doubled"])
                        elif kind == "norm":
                            pe.wait_ge(sem["normed"], st.own["normed"])
                        elif kind == "affine":
                            pe.wait_ge(sem["summed"], st.own["summed"])
                        else:
                            pe.wait_ge(sem["row_kept"], st.own["row_kept"])
                        w = wide(st.w)
                        for t in range(TT):
                            last = pe.transpose(w[:, t * 128:(t + 1) * 128], src[:, t, :], identf[:, :])
                        last.then_inc(wide_full, 1)

                    def qkv(st):
                        s = st.s
                        xq, xk = ({"XT": XT, "CT": CT, "CMT": CMT}[n][s] for n in (st.q_from, st.kv_from))
                        pe.wait_ge(sem["turned"], st.own["turned"])
                        pe.wait_ge(mats_loaded[PART_OF[st.w_names[0]]], 16)
                        pe.matmul(wide(st.w)[:, 0:T], mat(st.w_names[0]), xq[:, :], start=True, stop=True) \
                          .then_inc(wide_full, 1)
                        pe.matmul(wide(st.w + 1)[:, 0:T], mat(st.w_names[1]), xk[:, :], start=True, stop=True) \
                          .then_inc(wide_full, 1)
                        w = wide(st.w + 2)
                        for t in range(TT):
                            last = pe.matmul(w[:, t * 128:(t + 1) * 128], xk[:, t * 128:(t + 1) * 128],
                                             mat(st.w_names[2]), start=True, stop=True)
                        last.then_inc(wide_full, 1)
                        if st.lengths:
                            pe.wait_ge(sem["q_first"], st.end["q_first"])
                            pe.wait_ge(sem["k_read"], st.end["k_read"])
                            w = wide(st.w + 3)
                            for b in range(NB):
                                last = pe.matmul(w[0:HEADS, b * SEQ:(b + 1) * SEQ], QF[s][:, b, :],
                                                 K32[s][:, b * SEQ:(b + 1) * SEQ], start=True, stop=True)
                            last.then_inc(wide_full, 1)

                    def max_scores(st, k):
                        s, n = st.s, st.base.get("stile", 0) + k
                        if n >= 2:
                            pe.wait_ge(sem["stile"], n - 1)
                        for j in range(2):
                            pair = st.g * PAIRS + 2 * k + j
                            h, b = pair // NB, pair % NB
                            bank = SA[n % 2][:, j * 2 * SEQ:(j + 1) * 2 * SEQ]
                            for qt in range(QT):
                                keys = (qt + 1) * 128 if st.mask == "causal" else SEQ
                                lhs = SQ[s][0:MAX_ROW, h, b * SEQ + qt * 128:b * SEQ + (qt + 1) * 128]
                                rhs = SK[s][0:MAX_ROW, h, b * SEQ:b * SEQ + keys]
                                at = qt * SEQ
                                if st.mask == "causal":
                                    last = pe.matmul(bank[:, at:at + keys], lhs, rhs, start=True, stop=False,
                                                     skip_group_check=True)
                                    last = pe.matmul(bank[:, at + keys - 128:at + keys], identb[:, :], causal_q[:, :],
                                                     start=False, stop=True, skip_group_check=True)
                                elif st.mask is None:
                                    last = pe.matmul(bank[:, at:at + keys], lhs, rhs, start=True, stop=True)
                                else:
                                    if qt == 0:
                                        pe.matmul(bank, identb[:, :], mask_q[:, st.mask, :, :].rearrange(
                                            "p t k -> p (t k)"), start=True, stop=False, skip_group_check=True)
                                    last = pe.matmul(bank[:, at:at + keys], lhs, rhs, start=False, stop=True,
                                                     skip_group_check=True)
                        last.then_inc(tile_full, 1)

                    def exp_scores(st, g, i):
                        s, n = st.s, st.base.get("prob", 0) + i
                        if n >= 2:
                            pe.wait_ge(sem["prob"], n - 1)
                        pair = g * PAIRS + i
                        h, b = pair // NB, pair % NB
                        bank = ST[n % 2]
                        for kt in range(QT):
                            lhs = SK[s][:, h, b * SEQ + kt * 128:b * SEQ + (kt + 1) * 128]
                            first = kt * 128 if st.mask == "causal" else 0
                            at = kt * SEQ
                            rhs = SQ[s][:, h, b * SEQ + first:(b + 1) * SEQ]
                            n_q = SEQ - first
                            if st.mask == "causal":
                                pe.matmul(bank[:, at:at + n_q], lhs, rhs, start=True, stop=False,
                                          skip_group_check=True)
                                last = pe.matmul(bank[:, at:at + 128], identb[:, :], causal_k[:, :], start=False,
                                                 stop=True, skip_group_check=True)
                            elif st.mask is None:
                                last = pe.matmul(bank[:, at:at + n_q], lhs, rhs, start=True, stop=True)
                            else:
                                if kt == 0:
                                    pe.matmul(bank[:, :], identb[:, :], mask_k[:, st.mask, :, :].rearrange(
                                        "p t k -> p (t k)"), start=True, stop=False, skip_group_check=True)
                                last = pe.matmul(bank[:, at:at + n_q], lhs, rhs, start=False, stop=True,
                                                 skip_group_check=True)
                        last.then_inc(prob_full, 1)

                    def slot(st):
                        s, w, a = st.s, st.w, st.attn
                        if 0 <= st.g - 4 < GROUPS:
                            g = st.g - 4
                            pe.wait_ge(sem["out_copied"], by[s, f"{a}/{g + 3}"].end["out_copied"])
                            bank = wide(w)
                            for t in range(TT):
                                last = pe.transpose(bank[:, t * 128:(t + 1) * 128],
                                                    OG[s][:, g % 2, t * 128:(t + 1) * 128], identf[:, :])
                            last.then_inc(wide_full, 1)
                            w += 1
                        for k in range(TILES):
                            if st.g < GROUPS:
                                if st.g == 0 and k == 0:
                                    pe.wait_ge(stacked[s], 16 * STACK_DMAS * (attention_no(st, a) + 1))
                                max_scores(st, k)
                            g = st.g - 2
                            if 0 <= g < GROUPS:
                                if k == 0:
                                    pe.wait_ge(neg_row[s][g % 2], 16 * (attention_no(st, a) * GROUPS // 2 + g // 2 + 1))
                                exp_scores(st, g, 2 * k)
                                exp_scores(st, g, 2 * k + 1)
                            if k == (TILES - 1) // 2 and 0 <= st.g - 1 < GROUPS:
                                g = st.g - 1
                                pe.wait_ge(sem["neg_parts"], st.end["neg_parts"])
                                bank = wide(w)[:, :].bitcast(bf16)
                                for t in range(TT):
                                    last = pe.transpose(bank[0:2 * GROUP, t * 128:(t + 1) * 128],
                                                        HL[s][:, g % 2, t, :], identb[:, :])
                                last.then_inc(wide_full, 1)
                                w += 1
                        g = st.g - 3
                        if 0 <= g < GROUPS:
                            pe.wait_ge(sem["prob"], by[s, f"{a}/{g + 2}"].end["prob"])
                            pe.wait_ge(sem["v_ready"], st.own["v_ready"])
                            bank = wide(w)
                            for b in range(NB):
                                for kt in range(QT):
                                    first = kt * 128 if st.mask == "causal" else 0
                                    for j in range(GROUP):
                                        last = pe.matmul(
                                            bank[32 * j:32 * j + 32, b * SEQ + first:(b + 1) * SEQ],
                                            V[s][:, b * QT + kt, GROUP * g + j, :],
                                            P[s][:, g % 2, j * NB + b, kt * SEQ:kt * SEQ + SEQ - first],
                                            start=(kt == 0), stop=(kt == QT - 1), skip_group_check=True)
                            last.then_inc(wide_full, 1)

                    def turn_rows(w, src):
                        bank = wide(w)
                        for t in range(TT):
                            last = pe.transpose(bank[:, t * 128:(t + 1) * 128], src[:, t, :], identf[:, :])
                        last.then_inc(wide_full, 1)

                    def times(w, left, right):
                        bank = wide(w)
                        for t in range(TT):
                            last = pe.matmul(bank[:, t * 128:(t + 1) * 128], left[:, t * 128:(t + 1) * 128], right,
                                             start=True, stop=True)
                        last.then_inc(wide_full, 1)

                    def project(st):
                        pe.wait_ge(sem["out_scaled"], st.own["out_scaled"])
                        turn_rows(st.w, OT[st.s])
                        pe.wait_ge(sem["turned"], st.end["turned"])
                        times(st.w + 1, OF[st.s], mat(st.wo))

                    def down(w, s, half, chunks, weight):
                        bank = wide(w)
                        for t in range(TT):
                            for c in range(chunks):
                                last = pe.matmul(bank[:, t * 128:(t + 1) * 128],
                                                 HB[s][:, half, c, t * 128:(t + 1) * 128], weight(c),
                                                 start=(c == 0), stop=(c == chunks - 1))
                        last.then_inc(wide_full, 1)

                    def ff(st):
                        src = {"XT": XT, "ET": ET}[st.x][st.s]
                        pe.wait_ge(sem["turned"], st.own["turned"])
                        pe.wait_ge(mats_loaded[PART_OF[st.w1]], 16)
                        for c in range(st.chunks):
                            pe.matmul(wide(st.w + c)[:, 0:T], mat(st.w1, c, 128), src[:, :], start=True, stop=True) \
                              .then_inc(wide_full, 1)
                        pe.wait_ge(sem["hidden"], st.end["hidden"])
                        down(st.w + st.chunks, st.s, 0, st.chunks, lambda c: mat(st.w2, c, 128))

                    def linear(st):
                        s, w = st.s, st.w
                        xq, xk = ({"XT": XT, "ET": ET}[n][s] for n in (st.q, st.kv))
                        pe.wait_ge(sem["turned"], st.own["turned"])
                        pe.wait_ge(mats_loaded[PART_OF[st.w_names[0]]], 16)
                        pe.matmul(wide(w)[:, 0:T], mat(st.w_names[0]), xq[:, :], start=True, stop=True) \
                          .then_inc(wide_full, 1)
                        times(w + 1, xk, mat(st.w_names[1]))
                        times(w + 2, xk, mat(st.w_names[2]))
                        pe.wait_ge(sem["lin_feature"], st.end["lin_feature"])
                        pe.wait_ge(sem["lin_v"], st.end["lin_v"])
                        for b in range(NB):
                            bank = wide(w + 3 + b)
                            for qt in range(QT):
                                last = pe.matmul(bank[:, 0:D + 1], LK[s][:, b * QT + qt, :], LV[s][:, b * QT + qt, :],
                                                 start=(qt == 0), stop=(qt == QT - 1))
                            last.then_inc(wide_full, 1)
                        for b in range(NB):
                            pe.wait_ge(sem["lin_kv"], st.base.get("lin_kv", 0) + b + 1)
                            bank = wide(w + 3 + NB + b)
                            for qt in range(QT):
                                at = (b * QT + qt) * 128
                                last = pe.matmul(bank[:, qt * (D + LHEADS):(qt + 1) * (D + LHEADS)],
                                                 LQ[s][:, at:at + 128], KVB[s][:, b, :], start=True, stop=True)
                            last.then_inc(wide_full, 1)
                        pe.wait_ge(sem["lin_out"], st.end["lin_out"])
                        turn_rows(w + 3 + 2 * NB, OT[s])
                        pe.wait_ge(sem["turned"], st.end["turned"])
                        times(w + 4 + 2 * NB, OF[s], mat(st.w_names[3]))

                    def route(st):
                        s = st.s
                        pe.wait_ge(sem["turned"], st.own["turned"])
                        bank = wide(st.w)
                        for t in range(TT):
                            last = pe.matmul(bank[:, t * EXPERTS:(t + 1) * EXPERTS], XT[s][:, t * 128:(t + 1) * 128],
                                             mat("L3_r"), start=True, stop=True)
                        last.then_inc(wide_full, 1)
                        pe.wait_ge(sem["gates"], st.end["gates"])
                        bank = wide(st.w + 1)
                        for t in range(TT):
                            last = pe.transpose(bank[0:EXPERTS, t * 128:(t + 1) * 128], G[s][:, t, :], identf[:, :])
                        last.then_inc(wide_full, 1)

                    def experts(st):
                        s = st.s
                        pe.wait_ge(sem["gates_turned"], st.own["gates_turned"])
                        pe.wait_ge(mats_loaded[PART_OF["M_f1"]], 16)
                        for i, (what, e, c) in enumerate(expert_uses()):
                            if what == "bias":
                                bank = wide(st.w + i)
                                for t in range(TT):
                                    last = pe.matmul(bank[:, t * 128:(t + 1) * 128], GT[s][:, t * 128:(t + 1) * 128],
                                                     FC2B[:, :], start=True, stop=True)
                                last.then_inc(wide_full, 1)
                            elif what == "up":
                                pe.matmul(wide(st.w + i)[:, 0:T], mat("M_f1", e * 4 + c, 128), XT[s][:, :], start=True,
                                          stop=True).then_inc(wide_full, 1)
                            else:
                                pe.wait_ge(sem["hidden"], st.base["hidden"] + 4 * e + 4)
                                down(st.w + i, s, e % 2, 4, lambda c: mat("M_f2", e * 4 + c, 128))

                    kinds = {"turn": turn, "qkv": qkv, "slot": slot, "project": project, "ff": ff, "linear": linear,
                             "route": route, "experts": experts}
                    for st in steps:
                        if st.kind in kinds:
                            kinds[st.kind](st)

                @block.scalar
                def _(act):
                    def wide(w):
                        act.wait_ge(wide_full, w + 1)
                        return W[w % 2]

                    def turn(st):
                        dst = {"XT": XT, "CT": CT, "CMT": CMT, "ET": ET}[st.dst][st.s]
                        w = wide(st.w)
                        if st.g:
                            act.activation(dst[:, :], w[:, 0:T], ACT.Identity, bias=col(st.g[1]), scale=col(st.g[0])) \
                               .then_inc(sem["turned"], 1)
                        else:
                            act.activation(dst[:, :], w[:, 0:T], ACT.Copy).then_inc(sem["turned"], 1)

                    def qkv(st):
                        s = st.s
                        w = wide(st.w + 1)
                        if st.bias[1]:
                            act.activation(K32[s][:, :], w[:, 0:T], ACT.Identity, bias=col(st.bias[1]))
                            act.activation(K3[s][:, 0, :], w[:, 0:T], ACT.Identity, bias=col(st.bias[1])) \
                               .then_inc(sem["k_read"], 1)
                        else:
                            act.activation(K32[s][:, :], w[:, 0:T], ACT.Copy)
                            act.activation(K3[s][:, 0, :], w[:, 0:T], ACT.Copy).then_inc(sem["k_read"], 1)
                        w = wide(st.w + 2)
                        act.activation(V[s][:, :, :, 0:HD].rearrange("p t h d -> p (t h) d"),
                                       w[:, 0:TT * 128].rearrange("p (a d) -> p a d", d=HD), ACT.Copy) \
                           .then_inc(sem["v_ready"], 1)
                        act.wait_ge(sem["k_rest"], st.end["k_rest"])
                        act.activation(K3[s][:, 1, :], KR[s][:, :], ACT.Copy).then_inc(sem["k_second"], 1)

                    def slot(st):
                        s, w = st.s, st.w + (0 <= st.g - 4 < GROUPS)
                        for k in range(TILES):
                            g = st.g - 2
                            if 0 <= g < GROUPS:
                                for i in (2 * k, 2 * k + 1):
                                    n = st.base.get("prob", 0) + i
                                    used = 2 * SEQ - (128 if st.mask == "causal" else 0)
                                    act.wait_ge(prob_full, n + 1)
                                    act.activation(P[s][:, g % 2, i, 0:used], ST[n % 2][:, 0:used], ACT.Exp) \
                                       .then_inc(sem["prob"], 1)
                            if k == (TILES - 1) // 2 and 0 <= st.g - 1 < GROUPS:
                                bank = wide(w)[:, :].bitcast(bf16)
                                act.activation(MT[s][:, (st.g - 1) % 2, :], bank[0:2 * GROUP, 0:T], ACT.Copy) \
                                   .then_inc(sem["neg_turned"], 1)
                                w += 1
                        if 0 <= st.g - 3 < GROUPS:
                            act.activation(OG[s][:, (st.g - 3) % 2, :], wide(w)[:, 0:T], ACT.Copy) \
                               .then_inc(sem["out_copied"], 1)

                    def project(st):
                        act.activation(OF[st.s][:, :], wide(st.w)[:, 0:T], ACT.Identity, bias=col(st.bv)) \
                           .then_inc(sem["turned"], 1)

                    def ff(st):
                        for c in range(st.chunks):
                            w = wide(st.w + c)
                            dst = HB[st.s][:, 0, c, :]
                            if st.b1:
                                act.activation(dst, w[:, 0:T], ACT.Relu, bias=col(st.b1, c)).then_inc(sem["hidden"], 1)
                            else:
                                act.activation(dst, w[:, 0:T], ACT.Relu).then_inc(sem["hidden"], 1)

                    def linear(st):
                        s = st.s
                        for i in range(2):
                            act.wait_ge(sem["lin_min"], st.base.get("lin_min", 0) + i + 1)
                            act.activation(LE[s][:, i, :], LM[s][:, i, :], ACT.Exp).then_inc(sem["lin_exp"], 1)
                        act.activation(LV[s][:, :, 0:D], wide(st.w + 2)[:, 0:TT * 128].rearrange(
                            "p (t d) -> p t d", d=D), ACT.Copy).then_inc(sem["lin_v"], 1)
                        act.activation(OF[s][:, :], wide(st.w + 3 + 2 * NB)[:, 0:T], ACT.Copy) \
                           .then_inc(sem["turned"], 1)

                    def route(st):
                        s = st.s
                        act.wait_ge(sem["gate_diff"], st.end["gate_diff"])
                        act.activation(GE[s][:, :], GD[s][:, :], ACT.Exp).then_inc(sem["gate_exp"], 1)
                        act.activation(GT[s][:, :], wide(st.w + 1)[0:EXPERTS, 0:T], ACT.Copy) \
                           .then_inc(sem["gates_turned"], 1)

                    def experts(st):
                        for i, (what, e, c) in enumerate(expert_uses()):
                            if what == "up":
                                act.activation(HB[st.s][:, e % 2, c, :], wide(st.w + i)[:, 0:T], ACT.Gelu,
                                               bias=col("M_fb1", e * 4 + c)).then_inc(sem["hidden"], 1)

                    kinds = {"turn": turn, "qkv": qkv, "slot": slot, "project": project, "ff": ff, "linear": linear,
                             "route": route, "experts": experts}
                    for st in steps:
                        if st.kind in kinds:
                            kinds[st.kind](st)

                @block.gpsimd
                def _(pool):
                    chain = [0]

                    def link(ins):
                        chain[0] += 1
                        ins.then_inc(pool_chain, 1)
                        pool.wait_ge(pool_chain, chain[0])

                    def norm(st):
                        s = st.s
                        pool.wait_ge(sem["variance"], st.end["variance"])
                        link(pool.tensor_scalar(RS[s][:, :], MV[s][:, :, 1], EPS, None, ALU.add))
                        pool.tensor_tensor(RS[s][:, :], RS[s][:, :], minus_half[:, :], ALU.pow) \
                            .then_inc(sem["rstd"], 1)

                    def affine(st):
                        if st.plus:
                            return
                        s = st.s
                        pool.wait_ge(sem["normed"], st.own["normed"])
                        link(pool.tensor_tensor(AF[s][:, :, :], XH[s][:, :, :], row(st.g), ALU.mult))
                        pool.tensor_tensor(X[s][:, :, :], AF[s][:, :, :], row(st.b), ALU.add) \
                            .then_inc(sem["affined"], 1)

                    def qkv(st):
                        s = st.s
                        pool.wait_ge(sem["k_read"], st.end["k_read"])
                        pool.tensor_tensor(KR[s][:, :], K32[s][:, :], K3[s][:, 0, :], ALU.subtract) \
                            .then_inc(sem["k_rest"], 1)
                        pool.wait_ge(sem["k_rest"], st.end["k_rest"])
                        pool.wait_ge(sem["k_second"], st.end["k_second"])
                        pool.tensor_tensor(K3[s][:, 2, :], KR[s][:, :], K3[s][:, 1, :], ALU.subtract) \
                            .then_inc(sem["k_split"], 1)

                    def slot(st):
                        g = st.g - 1
                        if not 0 <= g < GROUPS:
                            return
                        s = st.s
                        pool.wait_ge(sem["stile"], by[s, f"{st.attn}/{g}"].end["stile"])
                        neg = NEG[s][:, g * PAIRS * QT:(g + 1) * PAIRS * QT].rearrange("p (h t) -> p t h", t=TT)
                        src = neg
                        if st.mask in (0, 1):
                            src = HF[s][:, :, :]
                            nan = row_nan[:, st.mask, :, :].rearrange("p b t -> p (b t)")
                            link(pool.tensor_tensor(src, neg, nan.unsqueeze(2).to_broadcast([128, TT, GROUP]), ALU.add))
                        high, low = HL[s][:, g % 2, :, 0:GROUP], HL[s][:, g % 2, :, GROUP:2 * GROUP]
                        link(pool.tensor_scalar(high, src, 1.0, None, ALU.mult))
                        pool.tensor_tensor(low, src, high, ALU.subtract).then_inc(sem["neg_parts"], 1)

                    kinds = {"norm": norm, "affine": affine, "qkv": qkv, "slot": slot}
                    for st in steps:
                        if st.kind in kinds:
                            kinds[st.kind](st)

                @block.vector
                def _(dve):
                    chain = [0]

                    def link(ins):
                        chain[0] += 1
                        ins.then_inc(dve_chain, 1)
                        dve.wait_ge(dve_chain, chain[0])

                    def own(st, *names):
                        for n in names:
                            if st.own.get(n, 0):
                                dve.wait_ge(sem[n], st.own[n])

                    def wide(w):
                        dve.wait_ge(wide_full, w + 1)
                        return W[w % 2]

                    def tokens(bank):
                        return bank[:, 0:TT * 128].rearrange("p (t d) -> p t d", d=128)

                    def load(st):
                        dve.wait_ge(loaded[st.s], 32)
                        dve.tensor_tensor(CC[st.s][:, :, :], C[st.s][:, :, :], C[st.s][:, :, :], ALU.add) \
                           .then_inc(sem["doubled"], 1)

                    def norm(st):
                        s = st.s
                        src = {"R": R, "X": X, "C": C}[st.src][s]
                        own(st, "residual", "summed")
                        for t in range(TT):
                            ins = dve.bn_stats(BN[s][:, t, :], src[:, t, :])
                        link(ins)
                        for t in range(TT):
                            ins = dve.bn_aggr(MV[s][:, t, :], BN[s][:, t, :])
                        ins.then_inc(sem["variance"], 1)
                        dve.wait_ge(sem["rstd"], st.end["rstd"])
                        dve.wait_ge(sem["variance"], st.end["variance"])
                        own(st, "turned", "affined")
                        for t in range(TT):
                            ins = dve.tensor_scalar(XH[s][:, t, :], src[:, t, :], MV[s][:, t, 0:1], RS[s][:, t:t + 1],
                                                    ALU.subtract, ALU.mult)
                        ins.then_inc(sem["normed"], 1)

                    def affine(st):
                        if not st.plus:
                            return
                        s = st.s
                        dst = {"X": X, "CC": CC}[st.dst][s]
                        own(st, "normed", "doubled")
                        link(dve.tensor_tensor(AF[s][:, :, :], XH[s][:, :, :], row(st.g), ALU.mult))
                        own(st, "affined")
                        link(dve.tensor_tensor(AF[s][:, :, :], AF[s][:, :, :], row(st.b), ALU.add))
                        dve.tensor_tensor(dst[:, :, :], AF[s][:, :, :], dst[:, :, :], ALU.add) \
                           .then_inc(sem["summed"], 1)

                    def rowmask(st):
                        s = st.s
                        m = {"M0": M0, "M1": M1}[st.dst][s]
                        own(st, "affined")
                        link(dve.tensor_reduce(AM[s][:, :], X[s][:, :, :], AX.X, ALU.max, apply_absolute_value=True))
                        dve.tensor_scalar(m[:, :], AM[s][:, :], 0.0, None, ALU.not_equal).then_inc(sem["rowmask"], 1)
                        dve.wait_ge(sem["rowmask"], st.end["rowmask"])
                        if st.kv:
                            for t in range(TT):
                                ins = dve.tensor_scalar(CM[s][:, t, :], C[s][:, t, :], m[:, t:t + 1], None, ALU.mult)
                            ins.then_inc(sem["row_kept"], 1)

                    def qkv(st):
                        s = st.s
                        w = wide(st.w)
                        if st.bias[0]:
                            ins = dve.tensor_scalar(Q32[s][:, :], w[:, 0:T], col(st.bias[0]), ATTN_SCALE, ALU.add,
                                                    ALU.mult)
                        else:
                            ins = dve.tensor_scalar(Q32[s][:, :], w[:, 0:T], ATTN_SCALE, None, ALU.mult)
                        ins.then_inc(sem["q_read"], 1)
                        dve.wait_ge(sem["q_read"], st.end["q_read"])
                        if st.lengths:
                            for b in range(NB):
                                ins = dve.tensor_scalar(QF[s][:, b, :], head_mask[:, :],
                                                        Q32[s][:, b * SEQ:b * SEQ + 1], None, ALU.mult)
                            ins.then_inc(sem["q_first"], 1)
                        link(dve.tensor_copy(Q3[s][:, 0, :], Q32[s][:, :]))
                        link(dve.tensor_tensor(QR[s][:, :], Q32[s][:, :], Q3[s][:, 0, :], ALU.subtract))
                        link(dve.tensor_copy(Q3[s][:, 1, :], QR[s][:, :]))
                        dve.tensor_tensor(Q3[s][:, 2, :], QR[s][:, :], Q3[s][:, 1, :], ALU.subtract) \
                           .then_inc(sem["q_split"], 1)
                        if st.lengths:
                            w = wide(st.w + 3)
                            dve.tensor_scalar(NZ[s][:, :, :].rearrange("h b k -> h (b k)"), w[0:HEADS, 0:T], 0.0, None,
                                              ALU.not_equal).then_inc(sem["len_read"], 1)
                            dve.wait_ge(sem["len_read"], st.end["len_read"])
                            link(dve.tensor_reduce(LEN[s][:, :], NZ[s][:, :, :], AX.X, ALU.add))
                            link(dve.tensor_scalar(LNAN[s][:, :], LEN[s][:, :], 0.0, HUGE, ALU.is_equal, ALU.mult))
                            link(dve.tensor_scalar(LNAN[s][:, :], LNAN[s][:, :], HUGE, 0.0, ALU.mult, ALU.mult))
                            for b in range(NB):
                                ins = dve.tensor_scalar(NZ[s][:, b, :], key_no[:, :], LEN[s][:, b:b + 1], MASKED,
                                                        ALU.is_ge, ALU.mult)
                            link(ins)
                            for b in range(NB):
                                ins = dve.tensor_scalar(LB[s][:, b * SEQ:(b + 1) * SEQ], NZ[s][:, b, :],
                                                        LNAN[s][:, b:b + 1], None, ALU.add)
                            ins.then_inc(sem["len_row"], 1)

                    def slot(st):
                        s = st.s
                        g = st.g - 4
                        if 0 <= g < GROUPS:
                            w = wide(st.w)[:, 0:TT * 128].rearrange("p (t j m) -> p t j m", t=TT, j=GROUP)
                            link(dve.reciprocal(RC[s][:, :, :], w[:, :, :, HD]))
                            if st.lengths:
                                own(st, "rowmask")
                                m = (M0 if st.mask == "causal" else M1)[s]
                                link(dve.tensor_tensor(RC[s][:, :, :], RC[s][:, :, :],
                                                       m[:, :].unsqueeze(2).to_broadcast([128, TT, GROUP]), ALU.mult))
                            dst = OT[s][:, :, GROUP * HD * g:GROUP * HD * (g + 1)].rearrange("p t (j d) -> p t j d", d=HD)
                            dve.tensor_tensor(dst, w[:, :, :, 0:HD],
                                              RC[s][:, :, :].unsqueeze(3).to_broadcast([128, TT, GROUP, HD]), ALU.mult) \
                               .then_inc(sem["out_scaled"], 1)
                        if st.g < GROUPS:
                            for k in range(TILES):
                                n = st.base.get("stile", 0) + k
                                dve.wait_ge(tile_full, n + 1)
                                at = (st.g * TILES + k) * 2 * QT
                                dst = NEG[s][:, at:at + 2 * QT]
                                tile = SA[n % 2][:, :].rearrange("p (j t k) -> p j t k", j=2, t=QT)
                                if st.mask == "causal":
                                    dst = dst.rearrange("p (j t) -> p j t", t=QT)
                                    for qt in range(QT):
                                        ins = dve.tensor_reduce(dst[:, :, qt], tile[:, :, qt, 0:(qt + 1) * 128], AX.X,
                                                                ALU.max, negate=True)
                                else:
                                    ins = dve.tensor_reduce(dst, tile.rearrange("p j t k -> p (j t) k"), AX.X, ALU.max,
                                                            negate=True)
                                ins.then_inc(sem["stile"], 1)

                    def project(st):
                        s = st.s
                        own(st, "affined")
                        dst = {"R": R, "X": X}[st.acc][s]
                        dve.wait_ge(wide_full, st.w + 2)
                        dve.tensor_tensor(AF[s][:, :, :], tokens(W[(st.w + 1) % 2]), row(st.bo), ALU.add) \
                           .then_inc(sem["out_read"], 1)
                        dve.wait_ge(sem["out_read"], st.end["out_read"])
                        dve.tensor_tensor(dst[:, :, :], AF[s][:, :, :], X[s][:, :, :], ALU.add) \
                           .then_inc(sem["residual"], 1)

                    def addz(st):
                        s = st.s
                        own(st, "affined", "out_scaled")
                        dve.tensor_tensor(R[s][:, :, :], OT[s][:, :, :], X[s][:, :, :], ALU.add) \
                           .then_inc(sem["residual"], 1)

                    def ff(st):
                        s = st.s
                        w = wide(st.w + st.chunks)
                        if not st.b2:
                            dve.tensor_copy(R[s][:, :, :], tokens(w)).then_inc(sem["residual"], 1)
                            return
                        dve.tensor_tensor(R[s][:, :, :], tokens(w), row(st.b2), ALU.add).then_inc(sem["ff_read"], 1)
                        dve.wait_ge(sem["ff_read"], st.end["ff_read"])
                        if st.mask:
                            for t in range(TT):
                                ins = dve.tensor_scalar(R[s][:, t, :], R[s][:, t, :], M0[s][:, t:t + 1], None, ALU.mult)
                            link(ins)
                        own(st, "affined")
                        dve.tensor_tensor(R[s][:, :, :], R[s][:, :, :], X[s][:, :, :], ALU.add) \
                           .then_inc(sem["residual"], 1)

                    def linear(st):
                        s = st.s
                        for i in range(2):
                            dve.tensor_scalar(LM[s][:, i, :], wide(st.w + i)[:, 0:T], 0.0, None, ALU.min) \
                               .then_inc(sem["lin_min"], 1)
                        for i, dst in enumerate((LQ[s][:, :], LK[s][:, :, :].rearrange("p t d -> p (t d)"))):
                            dve.wait_ge(sem["lin_exp"], st.base.get("lin_exp", 0) + i + 1)
                            dve.scalar_tensor_tensor(out=dst, in0=W[(st.w + i) % 2][:, 0:T], scalar=0.0,
                                                     in1=LE[s][:, i, :], op0=ALU.max, op1=ALU.add) \
                               .then_inc(sem["lin_feature"], 1)
                        for b in range(NB):
                            w = wide(st.w + 3 + b)
                            dve.tensor_tensor(KVB[s][:, b, 0:D], w[:, 0:D],
                                              block_mask[:, :, :].rearrange("p h d -> p (h d)"), ALU.mult)
                            dve.tensor_scalar(KVB[s][:, b, D:D + LHEADS], block_sum[:, :], w[:, D:D + 1], None,
                                              ALU.mult).then_inc(sem["lin_kv"], 1)
                        for b in range(NB):
                            w = wide(st.w + 3 + NB + b)[:, 0:QT * (D + LHEADS)].rearrange("p (t n) -> p t n", t=QT)
                            link(dve.tensor_scalar(LZ[s][:, :, :], w[:, :, D:D + LHEADS], 1e-6, None, ALU.add))
                            link(dve.reciprocal(LZ[s][:, :, :], LZ[s][:, :, :]))
                            dve.tensor_tensor(
                                OT[s][:, b * QT:(b + 1) * QT, :].rearrange("p t (h d) -> p t h d", d=LHD),
                                w[:, :, 0:D].rearrange("p t (h d) -> p t h d", d=LHD),
                                LZ[s][:, :, :].unsqueeze(3).to_broadcast([128, QT, LHEADS, LHD]), ALU.mult) \
                               .then_inc(sem["lin_out"], 1)
                        dve.tensor_copy(R[s][:, :, :], tokens(wide(st.w + 4 + 2 * NB))).then_inc(sem["residual"], 1)

                    def route(st):
                        s = st.s
                        w = wide(st.w)[:, 0:TT * EXPERTS].rearrange("p (t e) -> p t e", t=TT)
                        dve.tensor_tensor(LG[s][:, :, :], w, row("L3_rb"), ALU.add).then_inc(sem["route_read"], 1)
                        dve.wait_ge(sem["route_read"], st.end["route_read"])
                        for t in range(TT):
                            ins = dve.max(MX[s][:, t, :], LG[s][:, t, :])
                        link(ins)
                        dve.tensor_tensor(GD[s][:, :], MX[s][:, :, 1], MX[s][:, :, 0], ALU.subtract) \
                           .then_inc(sem["gate_diff"], 1)
                        for t in range(TT):
                            ins = dve.max_index(IX[s][:, t, :], MX[s][:, t, :], LG[s][:, t, :])
                        link(ins)
                        dve.tensor_copy(IXF[s][:, :, :], IX[s][:, :, 0:2])
                        dve.wait_ge(sem["gate_exp"], st.end["gate_exp"])
                        link(dve.tensor_scalar(GP[s][:, :], GE[s][:, :], 1.0, None, ALU.add))
                        link(dve.reciprocal(GP[s][:, :], GP[s][:, :]))
                        link(dve.tensor_tensor(GQ[s][:, :], GE[s][:, :], GP[s][:, :], ALU.mult))
                        for t in range(TT):
                            dve.tensor_scalar(G[s][:, t, :], expert_no[:, :], IXF[s][:, t, 0:1], GP[s][:, t:t + 1],
                                              ALU.is_equal, ALU.mult)
                            ins = dve.tensor_scalar(G2[s][:, t, :], expert_no[:, :], IXF[s][:, t, 1:2],
                                                    GQ[s][:, t:t + 1], ALU.is_equal, ALU.mult)
                        link(ins)
                        dve.tensor_tensor(G[s][:, :, :], G[s][:, :, :], G2[s][:, :, :], ALU.add) \
                           .then_inc(sem["gates"], 1)

                    def experts(st):
                        s, base, n = st.s, st.base.get("expert_mixed", 0), 0
                        own(st, "gates", "residual")
                        for i, (what, e, c) in enumerate(expert_uses()):
                            if what == "bias":
                                dve.tensor_tensor(X[s][:, :, :], tokens(wide(st.w + i)), X[s][:, :, :], ALU.add) \
                                   .then_inc(sem["expert_mixed"], 1)
                                n += 1
                            elif what == "down":
                                w = tokens(wide(st.w + i))
                                dve.wait_ge(sem["expert_mixed"], base + n)
                                for t in range(TT):
                                    ins = dve.scalar_tensor_tensor(out=X[s][:, t, :], in0=w[:, t, :],
                                                                   scalar=G[s][:, t, e:e + 1], in1=X[s][:, t, :],
                                                                   op0=ALU.mult, op1=ALU.add)
                                ins.then_inc(sem["expert_mixed"], 1)
                                n += 1

                    kinds = {"load": load, "norm": norm, "affine": affine, "rowmask": rowmask, "qkv": qkv,
                             "slot": slot, "project": project, "addz": addz, "ff": ff, "linear": linear,
                             "route": route, "experts": experts}
                    for st in steps:
                        if st.kind in kinds:
                            kinds[st.kind](st)
            nc.all_engine_barrier()
            nc.gpsimd.sem_clear(range(min(numbers), max(numbers) + 1))
            nc.all_engine_barrier()


def _by_dim(w):
    import numpy as np
    return np.transpose(w, (1, 2, 0)).reshape(D, D)


def _cols_by_dim(w):
    import numpy as np
    return np.swapaxes(w.reshape(*w.shape[:-1], HEADS, HD), -1, -2).reshape(w.shape)


def _down(w):
    import numpy as np
    return np.transpose(w.reshape(-1, 128, w.shape[1]), (1, 0, 2)).reshape(128, -1)


def kernel(**inputs):
    import numpy as np
    import concourse.bacc as bacc
    from concourse.bass_utils import run_bass_kernel_spmd

    a = {k: np.asarray(v) for k, v in inputs.items()}
    L = [{k[len(f"L{i}_xattn_"):]: v for k, v in a.items() if k.startswith(f"L{i}_xattn_")} for i in range(4)]
    sa, ca = L[3]["sa_in_w"], L[3]["ca_in_w"]
    m = {
        "L0_q": _cols_by_dim(L[0]["wq_s"]), "L0_k": _cols_by_dim(L[0]["wk_s"]), "L0_v": L[0]["wv_s"], "L0_o": L[0]["wo_s"],
        "L0_cq": _cols_by_dim(L[0]["wq_c"]), "L0_ck": _cols_by_dim(L[0]["wk_c"]), "L0_cv": L[0]["wv_c"],
        "L0_co": L[0]["wo_c"], "L0_f1": L[0]["ff1_w"], "L0_f2": _down(L[0]["ff2_w"]),
        "L1_q": _by_dim(L[1]["Wq1"]), "L1_k": _by_dim(L[1]["Wk1"]),
        "L1_v": np.transpose(L[1]["Wv1"], (1, 0, 2)).reshape(D, D),
        "L1_cq": _by_dim(L[1]["Wq2"]), "L1_ck": _by_dim(L[1]["Wk2"]),
        "L1_cv": np.transpose(L[1]["Wv2"], (1, 0, 2)).reshape(D, D),
        "L1_f1": L[1]["fc1_w"].T, "L1_f2": L[1]["fc2_w"].T,
        "E_q": L[2]["e_wq"], "E_k": L[2]["e_wk"], "E_v": L[2]["e_wv"], "E_m": L[2]["e_wm"], "E_f1": L[2]["e_w1"],
        "E_f2": _down(L[2]["e_w2"]),
        "S_q": L[2]["d_wq0"], "S_k": L[2]["d_wk0"], "S_v": L[2]["d_wv0"], "S_m": L[2]["d_wm0"],
        "C_q": L[2]["d_wq1"], "C_k": L[2]["d_wk1"], "C_v": L[2]["d_wv1"], "C_m": L[2]["d_wm1"],
        "D_f1": L[2]["d_w1"], "D_f2": _down(L[2]["d_w2"]),
        "L3_q": _cols_by_dim(sa[0:D].T), "L3_k": _cols_by_dim(sa[D:2 * D].T), "L3_v": sa[2 * D:].T,
        "L3_o": L[3]["sa_out_w"].T,
        "L3_cq": _cols_by_dim(ca[0:D].T), "L3_ck": _cols_by_dim(ca[D:2 * D].T), "L3_cv": ca[2 * D:].T,
        "L3_co": L[3]["ca_out_w"].T, "L3_r": L[3]["router_w"].T,
        "M_f1": np.transpose(L[3]["e_fc1_w"], (2, 0, 1)).reshape(D, -1),
        "M_f2": np.transpose(L[3]["e_fc2_w"].reshape(EXPERTS, D, DFF // 128, 128), (3, 0, 2, 1)).reshape(128, -1),
    }
    sb_, cb_ = L[3]["sa_in_b"], L[3]["ca_in_b"]
    c = {
        "L0_bq": _cols_by_dim(L[0]["bq_s"]), "L0_bk": _cols_by_dim(L[0]["bk_s"]), "L0_bv": L[0]["bv_s"],
        "L0_cbq": _cols_by_dim(L[0]["bq_c"]), "L0_cbk": _cols_by_dim(L[0]["bk_c"]), "L0_cbv": L[0]["bv_c"],
        "L0_fb1": L[0]["ff1_b"], "L1_fb1": L[1]["fc1_b"],
        "L3_bq": _cols_by_dim(sb_[0:D]), "L3_bk": _cols_by_dim(sb_[D:2 * D]), "L3_bv": sb_[2 * D:],
        "L3_cbq": _cols_by_dim(cb_[0:D]), "L3_cbk": _cols_by_dim(cb_[D:2 * D]), "L3_cbv": cb_[2 * D:],
        "L3_g1": L[3]["sa_ln_g"], "L3_b1": L[3]["sa_ln_b"], "L3_g2": L[3]["ca_q_ln_g"], "L3_b2": L[3]["ca_q_ln_b"],
        "L3_gk": L[3]["ca_kv_ln_g"], "L3_bkv": L[3]["ca_kv_ln_b"], "L3_g3": L[3]["moe_ln_g"], "L3_b3": L[3]["moe_ln_b"],
        "M_fb1": L[3]["e_fc1_b"].reshape(-1),
    }
    r = {"L0_bo": L[0]["bo_s"], "L0_cbo": L[0]["bo_c"], "L0_fb2": L[0]["ff2_b"], "L1_fb2": L[1]["fc2_b"],
         "L3_bo": L[3]["sa_out_b"], "L3_cbo": L[3]["ca_out_b"], "L3_rb": L[3]["router_b"]}
    for i in (0, 1):
        for n in (1, 2, 3):
            for kind in "gb":
                c[f"L{i}_{kind}{n}"] = r[f"L{i}_{kind}{n}"] = L[i][f"ln{n}_{kind}"]
    for kind in "gb":
        for n in (1, 2):
            r[f"E_{kind}{n}"] = L[2][f"e_{kind}{n}"]
        for n in (0, 1, 2):
            r[f"D_{kind}{n}"] = L[2][f"d_{kind}{n}"]

    arrays = {
        "x": a["x"], "ctx": a["ctx_1024"],
        "mask0": a["mask_1x1xSxS2_ik0"].reshape(SEQ, SEQ), "mask1": a["mask_1x1xSxS2_if1"].reshape(SEQ, SEQ),
        "mats": np.concatenate([m[n] for n in MAT_AT], axis=1),
        "cols": np.concatenate([c[n].reshape(-1, 128) for n in COL_AT], axis=0).T,
        "rows": np.concatenate([r[n] for n in ROW_AT]),
        "fc2_bias": L[3]["e_fc2_b"],
    }
    arrays = {k: np.ascontiguousarray(v) for k, v in arrays.items()}
    nc = bacc.Bacc("TRN2", target_bir_lowering=False, num_devices=1)
    args = [nc.dram_tensor(f"in_{k}", v.shape, mybir.dt.from_np(v.dtype), kind="ExternalInput").ap()
            for k, v in arrays.items()]
    out = nc.dram_tensor("out", (BATCHES, SEQ, D), mybir.dt.float32, kind="ExternalOutput").ap()
    build(nc, *args, out)
    got = run_bass_kernel_spmd(nc, [{f"in_{k}": v for k, v in arrays.items()}], core_ids=[0])
    return got.results[0]["out"]
```

```python
import concourse.bass as bass
from concourse import mybir
from contextlib import ExitStack
import numpy as np

BATCHES, SEQ, D = 8, 256, 128
HEADS, HD = 16, 8
LHEADS, LHD = 8, 16
EXPERTS, DFF = 8, 512
CHUNKS = DFF // 128
QT = SEQ // 128
NB = 1
STREAMS = 2
T = NB * SEQ
TT = NB * QT
ROUNDS = BATCHES // (NB * STREAMS)
GROUP = 4
GROUPS = HEADS // GROUP
PAIRS = GROUP * NB
TILES = PAIRS // 2
EPS = 1e-5
MASKED = -1e30
HUGE = 3e38
ATTN_SCALE = 1.0 / float(np.sqrt(HD))
SPLIT_ROWS, LEN_ROW, MAX_ROW = 48, 64, 96

WITH_LENGTHS, CLEARS_LENGTHS = ("a2", "a3"), "a4"

MATS = [
    [("L0_q", 128), ("L0_k", 128), ("L0_v", 128), ("L0_o", 128), ("L0_cq", 128), ("L0_ck", 128), ("L0_cv", 128),
     ("L0_co", 128), ("L0_f1", 512), ("L0_f2", 512)],
    [("L1_q", 128), ("L1_k", 128), ("L1_v", 128), ("L1_cq", 128), ("L1_ck", 128), ("L1_cv", 128), ("L1_f1", 128),
     ("L1_f2", 128)],
    [("E_q", 128), ("E_k", 128), ("E_v", 128), ("E_m", 128), ("E_f1", 256), ("E_f2", 256),
     ("S_q", 128), ("S_k", 128), ("S_v", 128), ("S_m", 128), ("C_q", 128), ("C_k", 128), ("C_v", 128), ("C_m", 128),
     ("D_f1", 256), ("D_f2", 256)],
    [("L3_q", 128), ("L3_k", 128), ("L3_v", 128), ("L3_o", 128), ("L3_cq", 128), ("L3_ck", 128), ("L3_cv", 128),
     ("L3_co", 128), ("L3_r", 8)],
    [("M_f1", EXPERTS * DFF), ("M_f2", EXPERTS * DFF)],
]
COLS = [("L0_bq", 1), ("L0_bk", 1), ("L0_bv", 1), ("L0_cbq", 1), ("L0_cbk", 1), ("L0_cbv", 1), ("L0_fb1", 4),
        ("L0_g1", 1), ("L0_b1", 1), ("L0_g2", 1), ("L0_b2", 1), ("L0_g3", 1), ("L0_b3", 1),
        ("L1_g1", 1), ("L1_b1", 1), ("L1_g2", 1), ("L1_b2", 1), ("L1_g3", 1), ("L1_b3", 1), ("L1_fb1", 1),
        ("L3_bq", 1), ("L3_bk", 1), ("L3_bv", 1), ("L3_cbq", 1), ("L3_cbk", 1), ("L3_cbv", 1),
        ("L3_g1", 1), ("L3_b1", 1), ("L3_g2", 1), ("L3_b2", 1), ("L3_gk", 1), ("L3_bkv", 1), ("L3_g3", 1), ("L3_b3", 1),
        ("M_fb1", EXPERTS * DFF // 128)]
ROWS = [("L0_bo", 128), ("L0_cbo", 128), ("L0_fb2", 128), ("L0_g1", 128), ("L0_b1", 128), ("L0_g2", 128),
        ("L0_b2", 128), ("L0_g3", 128), ("L0_b3", 128),
        ("L1_g1", 128), ("L1_b1", 128), ("L1_g2", 128), ("L1_b2", 128), ("L1_g3", 128), ("L1_b3", 128), ("L1_fb2", 128),
        ("E_g1", 128), ("E_b1", 128), ("E_g2", 128), ("E_b2", 128), ("D_g0", 128), ("D_b0", 128),
        ("D_g1", 128), ("D_b1", 128), ("D_g2", 128), ("D_b2", 128),
        ("L3_bo", 128), ("L3_cbo", 128), ("L3_rb", 8)]

LASTS = {
    "load": [("SP", 0.5), ("WAIT", 2.0)], "turn": [("PE", 0.4), ("ACT", 0.5)], "stats": [("DVE", 0.7), ("POOL", 0.9)],
    "normalise": [("DVE", 0.5)], "affine": [("POOL", 1.5)], "plus": [("DVE", 1.2)], "rowmask": [("DVE", 0.7)],
    "qkv": [("PE", 1.4), ("DVE", 1.5), ("DMA", 6.5), ("WAIT", 1.7)], "lengths": [("PE", 0.5), ("DVE", 1.6), ("DMA", 0.6), ("WAIT", 1.7)],
    "maxima": [("PE", 0.45), ("DVE", 1.15)], "negatives": [("POOL", 0.7), ("PE", 0.1), ("ACT", 0.4), ("DMA", 0.6), ("WAIT", 1.7)],
    "exps": [("PE", 0.45), ("ACT", 1.1)], "values": [("PE", 1.05), ("ACT", 0.35)], "out_rows": [("PE", 0.3), ("DVE", 0.4)],
    "out_turn": [("PE", 0.4), ("ACT", 0.5)], "out_product": [("PE", 0.5), ("DVE", 0.8)], "addz": [("DVE", 0.3)],
    "up": [("PE", 1.0), ("ACT", 0.5)], "down": [("PE", 1.0), ("DVE", 0.8)],
    "lin_qkv": [("PE", 1.4), ("DVE", 0.7), ("ACT", 0.6), ("DVE", 0.7)], "lin_kv": [("PE", 0.6), ("DVE", 0.4)],
    "lin_out": [("PE", 0.8), ("DVE", 0.8)], "logits": [("PE", 0.3), ("DVE", 1.0), ("ACT", 0.3)],
    "gates": [("DVE", 1.0), ("PE", 0.3), ("ACT", 0.5)], "expert_bias": [("PE", 0.5), ("DVE", 0.4)],
    "expert": [("PE", 3.6), ("DVE", 0.5)], "store": [],
}
HOP = 0.15
LAG = 30


def hops_of(kind, p):
    hops = LASTS["plus" if kind == "affine" and p["plus"] else kind]
    if kind in ("maxima", "exps") and p["mask"] in (0, 1):
        return [(hops[0][0], 2 * hops[0][1]), *hops[1:]]
    return hops


def lasts(kind, p):
    return sum(t + HOP for _, t in hops_of(kind, p))


def places(entries):
    at, out = 0, {}
    for name, n in entries:
        out[name] = (at, n)
        at += n
    return out, at


MAT_AT, MAT_COLS = places([e for part in MATS for e in part])
PART_ENDS = [sum(n for part in MATS[:i + 1] for _, n in part) for i in range(len(MATS))]
COL_AT, COL_COLS = places(COLS)
ROW_AT, ROW_COLS = places(ROWS)
PART_OF = {name: i for i, part in enumerate(MATS) for name, _ in part}


def uses(kind, p):
    if kind == "turn":
        return {"turned": 1}, [("turned", 1)]
    if kind == "stats":
        return {"variance": 1, "rstd": 1}, []
    if kind == "normalise":
        return {"normed": 1}, []
    if kind == "affine":
        return ({"summed": 1} if p["plus"] else {"affined": 1}), []
    if kind == "rowmask":
        return ({"rowmask": 1, "row_kept": 1} if p["kv"] else {"rowmask": 1}), []
    if kind == "qkv":
        n = {"q_read": 1, "q_one": 1, "q_two": 1, "q_three": 1, "k_read": 1, "k_one": 1, "k_two": 1, "k_three": 1,
             "v_ready": 1}
        if p["lengths"]:
            n["q_first"] = 1
        return n, [("q_read", 1), ("k_read", 1), ("v_ready", 1)]
    if kind == "lengths":
        return {"len_read": 1, "len_row": 1}, [("len_read", 1)]
    if kind == "maxima":
        return {"stile": 1}, []
    if kind == "negatives":
        return {"neg_parts": 1, "neg_turned": 1}, [("neg_turned", 1)]
    if kind == "exps":
        return {"prob": 2}, []
    if kind == "values":
        return {"out_copied": 1}, [("out_copied", 1)]
    if kind == "out_rows":
        return {"out_scaled": 1}, [("out_scaled", 1)]
    if kind == "out_turn":
        return {"turned": 1}, [("turned", 1)]
    if kind == "out_product":
        if p["acc"]:
            return {"out_read": 1, "residual": 1}, [("out_read", 1)]
        return {"residual": 1}, [("residual", 1)]
    if kind == "addz":
        return {"residual": 1}, []
    if kind == "up":
        return {"hidden": p["chunks"]}, [("hidden", i + 1) for i in range(p["chunks"])]
    if kind == "down":
        if p["b2"]:
            return {"ff_read": 1, "residual": 1}, [("ff_read", 1)]
        return {"residual": 1}, [("residual", 1)]
    if kind == "lin_qkv":
        return ({"lin_min": 2, "lin_exp": 2, "lin_feature": 2, "lin_v": 1},
                [("lin_feature", 1), ("lin_feature", 2), ("lin_v", 1)])
    if kind == "lin_kv":
        return {"lin_kv": NB}, [("lin_kv", b + 1) for b in range(NB)]
    if kind == "lin_out":
        return {"lin_out": NB}, [("lin_out", b + 1) for b in range(NB)]
    if kind == "logits":
        return {"route_read": 1, "gate_diff": 1, "gate_exp": 1}, [("route_read", 1)]
    if kind == "gates":
        return {"gates": 1, "gates_turned": 1}, [("gates_turned", 1)]
    if kind == "expert_bias":
        return {"expert_mixed": 1}, [("expert_mixed", 1)]
    if kind == "expert":
        n, w = {}, []
        if p["e"] < EXPERTS:
            n["prob"] = CHUNKS
        if p["e"] >= 1:
            n["expert_mixed"] = 1
            w.append(("expert_mixed", 1))
        return n, w
    if kind == "load":
        return {"doubled": 1}, []
    return {}, []


def stream_steps():
    out = []

    def add(kind, name, needs=None, **p):
        out.append((kind, name, p, needs if needs is not None else [out[-1][1]] if out else []))

    def attention(n, q_from, kv_from, w, bias, mask, lengths, needs, rows=()):
        add("qkv", n, needs, q_from=q_from, kv_from=kv_from, w_names=w, bias=bias, lengths=lengths, mask=mask)
        if lengths:
            add("lengths", f"{n}l")
        before = [f"{n}l"] if lengths else [n]
        for g in range(GROUPS + 4):
            for k in range(TILES):
                if g < GROUPS:
                    add("maxima", f"{n}m{g}/{k}", before, attn=n, g=g, k=k, mask=mask, lengths=lengths)
                    before = [f"{n}m{g}/{k}"]
                    if k == TILES - 2 and g >= 2:
                        before = [*before, f"{n}n{g - 2}"]
                e = g - 2
                if 0 <= e < GROUPS:
                    needs = [f"{n}e{e}/{k - 1}"] if k else [f"{n}n{e}"] + [f"{n}v{e - 2}"] * (e >= 2)
                    add("exps", f"{n}e{e}/{k}", needs, attn=n, g=e, k=k, mask=mask)
                e = g - 1
                if k == 0 and 0 <= e < GROUPS:
                    needs = [f"{n}m{e}/{TILES - 1}"] + [f"{n}e{e - 2}/0"] * (e >= 2) + [f"{n}n{e - 1}"] * (e >= 1)
                    add("negatives", f"{n}n{e}", needs, attn=n, g=e, mask=mask)
            e = g - 4
            if 0 <= e < GROUPS:
                needs = [f"{n}v{e}"] + ([f"{n}r{e - 1}"] if e else list(rows))
                add("out_rows", f"{n}r{e}", needs, attn=n, g=e, mask=mask, lengths=lengths)
            e = g - 3
            if 0 <= e < GROUPS:
                needs = [f"{n}e{e}/{TILES - 1}"] + [f"{n}r{e - 2}"] * (e >= 2) + [f"{n}v{e - 1}"] * (e >= 1)
                add("values", f"{n}v{e}", needs, attn=n, g=e, mask=mask)

    def norm(n, src, needs=None):
        add("stats", f"{n}s", needs, src=src)
        add("normalise", n, src=src)

    def project(n, wo, bv, bo, acc):
        add("out_turn", f"{n}t", [f"a{n[1:]}r{GROUPS - 1}"], bv=bv, of="out_scaled")
        add("out_product", n, wo=wo, bo=bo, acc=acc)

    def feed_forward(n, x, needs, w1, b1, w2, b2, chunks, mask):
        add("up", f"{n}u", needs, x=x, w1=w1, b1=b1, chunks=chunks)
        add("down", n, w2=w2, b2=b2, chunks=chunks, mask=mask)

    def linear(n, q, kv, w_names, needs):
        add("lin_qkv", f"{n}q", needs, q=q, kv=kv, w_names=w_names)
        add("lin_kv", f"{n}k")
        add("lin_out", f"{n}o")
        add("out_turn", f"{n}t", bv=None, of="lin_out")
        add("out_product", n, wo=w_names[3], bo=None, acc=None)

    add("load", "load")
    add("turn", "x", src="X", dst="XT", g=None, after=("load",))
    attention("a0", "XT", "XT", ("L0_q", "L0_k", "L0_v"), ("L0_bq", "L0_bk"), 0, False, ["x"])
    add("turn", "c", ["x"], src="C", dst="CT", g=None, after=("load",))
    project("o0", wo="L0_o", bv="L0_bv", bo="L0_bo", acc="R")
    norm("n0", "R")
    add("turn", "h1", src="XH", dst="XT", g=("L0_g1", "L0_b1"), after=("norm", "n0"))
    add("affine", "f0", ["n0"], g="L0_g1", b="L0_b1", dst="X", plus=None)
    attention("a1", "XT", "CT", ("L0_cq", "L0_ck", "L0_cv"), ("L0_cbq", "L0_cbk"), 1, False, ["h1", "c"], ["f0"])
    project("o1", wo="L0_co", bv="L0_cbv", bo="L0_cbo", acc="R")
    norm("n1", "R")
    add("turn", "h2", src="XH", dst="XT", g=("L0_g2", "L0_b2"), after=("norm", "n1"))
    add("affine", "f1", ["n1"], g="L0_g2", b="L0_b2", dst="X", plus=None)
    feed_forward("ff0", "XT", ["h2"], w1="L0_f1", b1="L0_fb1", w2="L0_f2", b2="L0_fb2", chunks=4, mask=None)
    norm("n2", "R", ["ff0", "f1"])
    add("turn", "x1", src="XH", dst="XT", g=("L0_g3", "L0_b3"), after=("norm", "n2"))
    add("affine", "f2", ["n2"], g="L0_g3", b="L0_b3", dst="X", plus=None)
    add("rowmask", "m0", ["f2"], dst="M0", kv=False)
    attention("a2", "XT", "XT", ("L1_q", "L1_k", "L1_v"), (None, None), "causal", True, ["x1"], ["m0"])
    add("addz", "z0", [f"a2r{GROUPS - 1}"])
    norm("n3", "R")
    add("turn", "y1", src="XH", dst="XT", g=("L1_g1", "L1_b1"), after=("norm", "n3"))
    add("affine", "f3", ["n3"], g="L1_g1", b="L1_b1", dst="X", plus=None)
    add("rowmask", "m1", dst="M1", kv=True)
    add("turn", "cm", src="CM", dst="CMT", g=None, after=("rowmask", "m1"))
    attention("a3", "XT", "CMT", ("L1_cq", "L1_ck", "L1_cv"), (None, None), None, True, ["y1", "cm"])
    add("addz", "z1", [f"a3r{GROUPS - 1}"])
    norm("n4", "R")
    add("turn", "y2", src="XH", dst="XT", g=("L1_g2", "L1_b2"), after=("norm", "n4"))
    add("affine", "f4", ["n4"], g="L1_g2", b="L1_b2", dst="X", plus=None)
    feed_forward("ff1", "XT", ["y2"], w1="L1_f1", b1="L1_fb1", w2="L1_f2", b2="L1_fb2", chunks=1, mask="M0")
    norm("n5", "R", ["ff1", "f4"])
    add("turn", "x2", src="XH", dst="XT", g=("L1_g3", "L1_b3"), after=("norm", "n5"))
    add("affine", "f5", ["n5"], g="L1_g3", b="L1_b3", dst="X", plus=None)
    add("turn", "e0", ["n5"], src="CC", dst="ET", g=None, after=("load",))
    linear("le", q="ET", kv="ET", w_names=("E_q", "E_k", "E_v", "E_m"), needs=["e0"])
    norm("n6", "R", ["le", "x2", "f5"])
    add("affine", "f6", g="E_g1", b="E_b1", dst="CC", plus="CC")
    add("turn", "e1", src="CC", dst="ET", g=None, after=("affine", "f6"))
    feed_forward("ffe", "ET", ["e1"], w1="E_f1", b1=None, w2="E_f2", b2=None, chunks=2, mask=None)
    norm("n7", "R")
    add("affine", "f7", g="E_g2", b="E_b2", dst="CC", plus="CC")
    add("turn", "e2", src="CC", dst="ET", g=None, after=("affine", "f7"))
    linear("ls", q="XT", kv="XT", w_names=("S_q", "S_k", "S_v", "S_m"), needs=["f7"])
    norm("n8", "R")
    add("affine", "f8", g="D_g0", b="D_b0", dst="X", plus="X")
    add("turn", "d0", src="X", dst="XT", g=None, after=("affine", "f8"))
    linear("lc", q="XT", kv="ET", w_names=("C_q", "C_k", "C_v", "C_m"), needs=["d0", "e2"])
    norm("n9", "R")
    add("affine", "f9", g="D_g1", b="D_b1", dst="X", plus="X")
    add("turn", "d1", src="X", dst="XT", g=None, after=("affine", "f9"))
    feed_forward("ffd", "XT", ["d1"], w1="D_f1", b1=None, w2="D_f2", b2=None, chunks=2, mask=None)
    norm("n10", "R")
    add("affine", "f10", g="D_g2", b="D_b2", dst="X", plus="X")
    norm("n11", "X")
    add("turn", "q3", src="XH", dst="XT", g=("L3_g1", "L3_b1"), after=("norm", "n11"))
    attention("a4", "XT", "XT", ("L3_q", "L3_k", "L3_v"), ("L3_bq", "L3_bk"), None, False, ["q3"])
    norm("n12", "C", ["a4"])
    add("turn", "k3", src="XH", dst="CT", g=("L3_gk", "L3_bkv"), after=("norm", "n12"))
    project("o4", wo="L3_o", bv="L3_bv", bo="L3_bo", acc="X")
    norm("n13", "X", ["o4", "k3"])
    add("turn", "q4", src="XH", dst="XT", g=("L3_g2", "L3_b2"), after=("norm", "n13"))
    attention("a5", "XT", "CT", ("L3_cq", "L3_ck", "L3_cv"), ("L3_cbq", "L3_cbk"), None, False, ["q4", "k3"])
    project("o5", wo="L3_co", bv="L3_cbv", bo="L3_cbo", acc="X")
    norm("n14", "X")
    add("turn", "h3", src="XH", dst="XT", g=("L3_g3", "L3_b3"), after=("norm", "n14"))
    add("logits", "r")
    add("gates", "g")
    add("expert_bias", "bias")
    for e in range(EXPERTS + 1):
        add("expert", f"mix{e}", e=e)
    add("store", "store")
    return out


class Step:

    def __init__(self, kind, s, name, p, base, end, own, w):
        self.kind, self.s, self.name, self.base, self.end, self.own, self.w = kind, s, name, base, end, own, w
        self.src, self.dst, self.after, self.plus, self.kv = (p.get(n) for n in ("src", "dst", "after", "plus", "kv"))
        self.acc, self.mask, self.b = p.get("acc"), p.get("mask"), p.get("b")
        self.g, self.k = p.get("g"), p.get("k")
        self.attn, self.lengths, self.bias, self.w_names = (p.get(n) for n in ("attn", "lengths", "bias", "w_names"))
        self.q_from, self.kv_from, self.q = (p.get(n) for n in ("q_from", "kv_from", "q"))
        self.wo, self.bv, self.bo, self.of = p.get("wo"), p.get("bv"), p.get("bo"), p.get("of")
        self.x, self.w1, self.b1, self.w2, self.b2, self.chunks = (
            p.get(n) for n in ("x", "w1", "b1", "w2", "b2", "chunks"))
        self.e = p.get("e")


def plan():
    entries = stream_steps()
    left = {}
    for kind, name, p, needs in reversed(entries):
        left[name] = lasts(kind, p) + max((left[m] for _, m, _, n in entries if name in n), default=0)
    done, free, unplaced = {}, {}, [list(entries) for _ in range(STREAMS)]
    banks = {"wide": [0, 0], "maxima": [0, 0], "exps": [0]}
    count, steps, by, released = {}, [], {}, []
    own = [{} for _ in range(STREAMS)]

    def earliest(s, kind, p, needs):
        t = max((done[s, n] for n in needs), default=0)
        for what, banks_of in banks.items():
            if what == ("exps" if kind == "expert" else kind) or (what == "wide" and uses(kind, p)[1]):
                t = max(t, banks_of[-2] if len(banks_of) > 1 and what != "exps" else banks_of[-1])
        hops = hops_of(kind, p)
        return max(t, free.get(hops[0][0], 0)) if hops else t

    while any(unplaced):
        ready = [(s, e) for s in range(STREAMS) for e in unplaced[s] if all((s, n) in done for n in e[3])]
        starts = {(s, e[1]): earliest(s, e[0], e[2], e[3]) for s, e in ready}
        s, (kind, name, p, needs) = min(ready, key=lambda c: (starts[c[0], c[1][1]], -left[c[1][1]] + LAG * c[0]))
        unplaced[s] = [e for e in unplaced[s] if e[1] != name]
        t, read = starts[s, name], 0
        for engine, duration in hops_of(kind, p):
            if engine != "WAIT":
                t = max(t, free.get(engine, 0))
            t += duration
            if engine != "WAIT":
                free[engine] = t
            t += HOP
            if engine != "PE" and not read:
                read = t
        done[s, name] = t
        n, wide = uses(kind, p)
        if kind == "maxima":
            banks["maxima"].append(t)
        elif kind in ("exps", "expert"):
            banks["exps"].append(t - 0.8)
        elif wide:
            banks["wide"] += [read or t] * len(wide)
        base = dict(count)
        for what, k in n.items():
            count[what] = count.get(what, 0) + k
        st = Step(kind, s, name, p, base, dict(count), dict(own[s]), len(released))
        own[s] |= {what: count[what] for what in n}
        released += [(what, base.get(what, 0) + k) for what, k in wide]
        steps.append(st)
        by[s, name] = st
    return steps, by, released, sorted(count)


def build(nc, x, ctx, mask0, mask1, mats, cols, rows, fc2_bias, out):
    f32, bf16, i32, u32 = mybir.dt.float32, mybir.dt.bfloat16, mybir.dt.int32, mybir.dt.uint32
    ALU, ACT, AX = mybir.AluOpType, mybir.ActivationFunctionType, mybir.AxisListType
    steps, by, released, counted = plan()
    x_tok = x.rearrange("n (t p) d -> p n t d", p=128)
    ctx_tok = ctx.rearrange("n (t p) d -> p n t d", p=128)
    out_tok = out.rearrange("n (t p) d -> p n t d", p=128)

    with ExitStack() as stack:
        def sb(name, shape, dt=f32):
            return stack.enter_context(nc.sbuf_tensor(name, shape, dt))

        def psum(name, shape):
            return stack.enter_context(nc.psum_tensor(name, shape, f32))

        def per_stream(name, shape, dt=f32):
            return [sb(f"{name}{s}", shape, dt) for s in range(STREAMS)]

        MAT = sb("MAT", [128, MAT_COLS])
        COL = sb("COL", [128, COL_COLS])
        ROW = sb("ROW", [128, ROW_COLS])
        FC2B = sb("FC2B", [EXPERTS, D])
        identf = sb("identf", [128, 128])
        identb = sb("identb", [128, 128], bf16)
        head_mask = sb("head_mask", [128, HEADS])
        block_mask = sb("block_mask", [128, LHEADS, LHD])
        block_sum = sb("block_sum", [128, LHEADS])
        expert_no = sb("expert_no", [128, EXPERTS])
        key_no = sb("key_no", [HEADS, SEQ])
        minus_half = sb("minus_half", [128, TT])
        no_len = sb("no_len", [HEADS, T], bf16)
        causal_q = sb("causal_q", [128, 128], bf16)
        causal_k = sb("causal_k", [128, 128], bf16)
        mask_any = sb("mask_any", [128, 2, QT])
        mask_q = sb("mask_q", [128, 2, QT, SEQ], bf16)
        mask_k = sb("mask_k", [128, 2, QT, SEQ], bf16)
        row_nan = sb("row_nan", [128, 2, NB, QT])

        X, C, CC, CM = (per_stream(n, [128, TT, D]) for n in ("X", "C", "CC", "CM"))
        R, XH, AF, OT = (per_stream(n, [128, TT, D]) for n in ("R", "XH", "AF", "OT"))
        XT, CT, ET, OF = (per_stream(n, [128, T]) for n in ("XT", "CT", "ET", "OF"))
        CMT = ET
        BN = per_stream("BN", [128, TT, 6])
        MV = per_stream("MV", [128, TT, 2])
        RS = per_stream("RS", [128, TT])
        AM = per_stream("AM", [128, TT])
        M0, M1 = per_stream("M0", [128, TT]), per_stream("M1", [128, TT])
        Q32, K32, QR, KR = (per_stream(n, [128, T]) for n in ("Q32", "K32", "QR", "KR"))
        Q3, K3 = per_stream("Q3", [128, 3, T], bf16), per_stream("K3", [128, 3, T], bf16)
        SQ, SK = per_stream("SQ", [128, HEADS, T], bf16), per_stream("SK", [128, HEADS, T], bf16)
        V = per_stream("V", [128, TT, HEADS, 32])
        QF = per_stream("QF", [128, NB, HEADS])
        NZ = per_stream("NZ", [HEADS, NB, SEQ])
        LEN, LNAN = per_stream("LEN", [HEADS, NB]), per_stream("LNAN", [HEADS, NB])
        LB = per_stream("LB", [HEADS, T], bf16)
        NEG = per_stream("NEG", [128, HEADS * TT])
        HL = per_stream("HL", [128, 2, TT, 2 * GROUP], bf16)
        HF = per_stream("HF", [128, TT, GROUP])
        MT = per_stream("MT", [2 * GROUP, 2, T], bf16)
        P = per_stream("P", [128, 2, PAIRS, 2 * SEQ])
        OG = per_stream("OG", [128, 2, T])
        RC = per_stream("RC", [128, TT, GROUP])
        room = [P[s][:, :, :, :].rearrange("p a i k -> p a (i k)") for s in range(STREAMS)]
        HB = [r[:, :, 0:4 * T].rearrange("p a (c t) -> p a c t", c=4) for r in room]
        LM = [r[:, 0, 4 * T:6 * T].rearrange("p (i t) -> p i t", i=2) for r in room]
        LE = [r[:, 0, 6 * T:8 * T].rearrange("p (i t) -> p i t", i=2) for r in room]
        LQ = [r[:, 1, 4 * T:5 * T] for r in room]
        LK = [r[:, 1, 5 * T:6 * T].rearrange("p (t d) -> p t d", d=D) for r in room]
        mask_in = room[0][:, 0, 0:2 * QT * SEQ].rearrange("p (m k) -> p m k", m=2).bitcast(i32)
        mask_vis = room[0][:, 1, 0:2 * QT * SEQ].rearrange("p (m k) -> p m k", m=2)
        LV = per_stream("LV", [128, TT, D + 1])
        KVB = per_stream("KVB", [128, NB, D + LHEADS])
        LZ = per_stream("LZ", [128, 2, LHEADS])
        LG, MX = per_stream("LG", [128, TT, EXPERTS]), per_stream("MX", [128, TT, 8])
        IX, IXF = per_stream("IX", [128, TT, 8], u32), per_stream("IXF", [128, TT, 2])
        GD, GE, GP, GQ = (per_stream(n, [128, TT]) for n in ("GD", "GE", "GP", "GQ"))
        G, G2 = per_stream("G", [128, TT, EXPERTS]), per_stream("G2", [128, TT, EXPERTS])
        GT = per_stream("GT", [EXPERTS, T])

        SA = [psum(f"SA{i}", [128, 4 * SEQ]) for i in range(2)]
        ST = [psum(f"ST{i}", [128, 2 * SEQ]) for i in range(2)]
        W = [psum(f"W{i}", [128, 512]) for i in range(2)]

        consts_loaded = nc.alloc_semaphore("consts_loaded")
        pool_consts = nc.alloc_semaphore("pool_consts")
        dve_consts = nc.alloc_semaphore("dve_consts")
        mask_turned = nc.alloc_semaphore("mask_turned")
        mask_copied = nc.alloc_semaphore("mask_copied")
        mats_loaded = [nc.alloc_semaphore(f"mats_loaded{i}") for i in range(len(MATS))]
        sem = {n: nc.alloc_semaphore(n) for n in counted}
        wide_full = nc.alloc_semaphore("wide_full")
        tile_full = nc.alloc_semaphore("tile_full")
        prob_full = nc.alloc_semaphore("prob_full")
        dve_chain = nc.alloc_semaphore("dve_chain")
        pool_chain = nc.alloc_semaphore("pool_chain")
        loaded = [nc.alloc_semaphore(f"loaded{s}") for s in range(STREAMS)]
        stacked = [nc.alloc_semaphore(f"stacked{s}") for s in range(STREAMS)]
        neg_row = [[nc.alloc_semaphore(f"neg_row{s}_{i}") for i in range(2)] for s in range(STREAMS)]
        stored = nc.alloc_semaphore("stored")
        of_round = [*sem.values(), wide_full, tile_full, prob_full, dve_chain, pool_chain, *loaded, *stacked,
                    *neg_row[0], *(neg_row[1] if STREAMS > 1 else []), stored]
        numbers = [h.num for h in of_round]
        assert sorted(numbers) == list(range(min(numbers), max(numbers) + 1))

        def mat(name, chunk=0, width=None):
            at, n = MAT_AT[name]
            width = width or n
            return MAT[:, at + chunk * width:at + (chunk + 1) * width]

        def col(name, i=0):
            at = COL_AT[name][0] + i
            return COL[:, at:at + 1]

        def row(name):
            at, n = ROW_AT[name]
            return ROW[:, at:at + n].unsqueeze(1).to_broadcast([128, TT, n])

        def attention_no(st, name):
            return int(name[1:])

        def stack_dmas(st):
            upto = range(attention_no(st, st.attn) + 1)
            return 12 * len(upto) + sum(f"a{n}" in (*WITH_LENGTHS, CLEARS_LENGTHS) for n in upto)

        with nc.Block() as block:
            @block.sync
            def _(sp):
                sp.dma_start(COL[:, :], cols).then_inc(consts_loaded, 16)
                sp.dma_start(mask_in[:, 0, :].rearrange("p (t k) -> p t k", t=QT),
                             mask0.rearrange("(t p) k -> p t k", p=128)).then_inc(consts_loaded, 16)
                sp.dma_start(mask_in[:, 1, :].rearrange("p (t k) -> p t k", t=QT),
                             mask1.rearrange("(t p) k -> p t k", p=128)).then_inc(consts_loaded, 16)
                sp.dma_start(ROW[:, :], rows.partition_broadcast(128)).then_inc(consts_loaded, 16)
                sp.dma_start(FC2B[:, :], fc2_bias).then_inc(consts_loaded, 16)
                for i, end in enumerate(PART_ENDS):
                    at = PART_ENDS[i - 1] if i else 0
                    sp.dma_start(MAT[:, at:end], mats[:, at:end]).then_inc(mats_loaded[i], 16)
                sp.wait_ge(consts_loaded, 80)

            @block.gpsimd
            def _(pool):
                made = [0]

                def link(ins):
                    made[0] += 1
                    ins.then_inc(pool_consts, 1)
                    pool.wait_ge(pool_consts, made[0])

                def select(dst, pattern, op, fill, base, per_partition):
                    link(pool.affine_select(out=dst, in_=dst, pattern=pattern, compare_op=op, fill=fill, base=base,
                                            channel_multiplier=per_partition))

                for t in (identf, identb):
                    link(pool.memset(t[:, :], 0.0))
                    select(t[:, :], [[-1, 128]], ALU.not_equal, 1.0, 0, 1)
                for t, shape in ((block_mask[:, :, :], [[-LHD, LHEADS], [0, LHD]]), (block_sum[:, :], [[-LHD, LHEADS]])):
                    link(pool.memset(t, 1.0))
                    select(t, shape, ALU.is_ge, 0.0, 0, 1)
                    select(t, [[LHD if s else 0, n] for s, n in shape], ALU.is_ge, 0.0, LHD - 1, -1)
                link(pool.memset(causal_q[:, :], 0.0))
                select(causal_q[:, :], [[-1, 128]], ALU.is_ge, MASKED, 0, 1)
                link(pool.memset(causal_k[:, :], 0.0))
                select(causal_k[:, :], [[1, 128]], ALU.is_ge, MASKED, 0, -1)
                link(pool.iota(mask_vis[:, 0, 0:EXPERTS].bitcast(i32), pattern=[[1, EXPERTS]], base=0,
                               channel_multiplier=0))
                link(pool.iota(mask_vis[0:HEADS, 1, 0:SEQ].bitcast(i32), pattern=[[1, SEQ]], base=0,
                               channel_multiplier=0))
                link(pool.tensor_copy(expert_no[:, :], mask_vis[:, 0, 0:EXPERTS].bitcast(i32)))
                link(pool.tensor_copy(key_no[:, :], mask_vis[0:HEADS, 1, 0:SEQ].bitcast(i32)))
                pool.sem_inc(pool_consts, 100)

            @block.vector
            def _(dve):
                made = [0]

                def link(ins):
                    made[0] += 1
                    ins.then_inc(dve_consts, 1)
                    dve.wait_ge(dve_consts, made[0])

                for s in range(STREAMS):
                    dve.memset(SQ[s][:, :, :], 0.0)
                    dve.memset(SK[s][:, :, :], 0.0)
                    dve.memset(V[s][:, :, :, :], 0.0)
                    dve.memset(LV[s][:, :, D:D + 1], 1.0)
                dve.memset(no_len[:, :], 0.0)
                link(dve.memset(minus_half[:, :], -0.5))
                for s in range(STREAMS):
                    dve.memset(SQ[s][LEN_ROW:LEN_ROW + 1, :, :], 1.0)
                    dve.memset(SK[s][MAX_ROW:MAX_ROW + 2, :, :], 1.0)
                    dve.memset(V[s][:, :, :, HD:HD + 1], 1.0)
                dve.wait_ge(pool_consts, 100)
                dve.tensor_reduce(head_mask[:, :], identf[:, :].rearrange("p (d h) -> p h d", h=HEADS), AX.X, ALU.add)
                dve.wait_ge(consts_loaded, 80)
                dve.tensor_scalar(mask_q[:, :, :, :].rearrange("p m t k -> p m (t k)"), mask_in[:, :, :], 0.0, MASKED,
                                  ALU.is_equal, ALU.mult)
                link(dve.tensor_scalar(mask_vis[:, :, :], mask_in[:, :, :], 0.0, None, ALU.not_equal))
                link(dve.tensor_reduce(mask_any[:, :, :], mask_vis[:, :, :].rearrange("p m (t k) -> p m t k", t=QT),
                                       AX.X, ALU.max))
                for b in range(NB):
                    link(dve.tensor_scalar(row_nan[:, :, b, :], mask_any[:, :, :], 0.0, HUGE, ALU.is_equal, ALU.mult))
                    link(dve.tensor_scalar(row_nan[:, :, b, :], row_nan[:, :, b, :], HUGE, 0.0, ALU.mult, ALU.mult))
                link(dve.memset(LZ[0][:, :, :], 0.0))
                dve.sem_inc(dve_consts, 100)
                for m in range(2):
                    dve.wait_ge(mask_turned, m + 1)
                    dve.tensor_copy(mask_k[:, m, :, :].rearrange("p t k -> p (t k)"), W[m][:, :].bitcast(bf16)[:, 0:QT * SEQ]) \
                       .then_inc(mask_copied, 1)
                dve.wait_ge(mask_copied, 2)

            @block.tensor
            def _(pe):
                pe.wait_ge(dve_consts, 100)
                for m in range(2):
                    for kt in range(QT):
                        for qt in range(QT):
                            at = kt * SEQ + qt * 128
                            last = pe.transpose(W[m][:, :].bitcast(bf16)[:, at:at + 128],
                                                mask_q[:, m, qt, kt * 128:(kt + 1) * 128], identb[:, :])
                    last.then_inc(mask_turned, 1)

        with nc.Fori(0, ROUNDS) as rnd:
            with nc.Block() as block:
                @block.sync
                def _(sp):
                    stacks = [0] * STREAMS

                    def load(st):
                        first = (rnd * STREAMS + st.s) * NB
                        sp.dma_start(X[st.s][:, :, :].rearrange("p (n t) d -> p n t d", n=NB),
                                     x_tok[:, bass.ds(first, NB), :, :]).then_inc(loaded[st.s], 16)
                        sp.dma_start(C[st.s][:, :, :].rearrange("p (n t) d -> p n t d", n=NB),
                                     ctx_tok[:, bass.ds(first, NB), :, :]).then_inc(loaded[st.s], 16)

                    def qkv(st):
                        s = st.s
                        for stack, parts, part, what, at in (
                                (SQ, Q3, 0, "q_one", (0, 1, 2)), (SK, K3, 0, "k_one", (0, 3, 5)),
                                (SQ, Q3, 1, "q_two", (3, 4)), (SQ, Q3, 2, "q_three", (5,)),
                                (SK, K3, 1, "k_two", (1, 4)), (SK, K3, 2, "k_three", (2,))):
                            sp.wait_ge(sem[what], st.end[what])
                            for r in at:
                                sp.dma_start(stack[s][HD * r:HD * r + HD, :, :], parts[s][:, part, :]) \
                                  .then_inc(stacked[s], 16)
                        if st.name == CLEARS_LENGTHS:
                            sp.dma_start(SK[s][LEN_ROW:LEN_ROW + 1, :, :], no_len[:, :]).then_inc(stacked[s], 16)

                    def lengths(st):
                        sp.wait_ge(sem["len_row"], st.end["len_row"])
                        sp.dma_start(SK[st.s][LEN_ROW:LEN_ROW + 1, :, :], LB[st.s][:, :]).then_inc(stacked[st.s], 16)

                    def store(st):
                        sp.wait_ge(sem["expert_mixed"], st.own["expert_mixed"])
                        first = (rnd * STREAMS + st.s) * NB
                        sp.dma_start(out_tok[:, bass.ds(first, NB), :, :],
                                     X[st.s][:, :, :].rearrange("p (n t) d -> p n t d", n=NB)).then_inc(stored, 16)

                    for st in steps:
                        if st.kind in ("load", "qkv", "lengths", "store"):
                            {"load": load, "qkv": qkv, "lengths": lengths, "store": store}[st.kind](st)
                    sp.wait_ge(stored, 16 * STREAMS)

                @block.tensor
                def _(pe):
                    def wide(w):
                        if w >= 2:
                            what, value = released[w - 2]
                            pe.wait_ge(sem[what], value)
                        return W[w % 2]

                    def turn(st):
                        s = st.s
                        src = {"X": X, "C": C, "CC": CC, "CM": CM, "XH": XH}[st.src][s]
                        kind = st.after[0]
                        if kind == "load":
                            pe.wait_ge(loaded[s], 32)
                            if st.src == "CC":
                                pe.wait_ge(sem["doubled"], st.own["doubled"])
                        elif kind == "norm":
                            pe.wait_ge(sem["normed"], st.own["normed"])
                        elif kind == "affine":
                            pe.wait_ge(sem["summed"], st.own["summed"])
                        else:
                            pe.wait_ge(sem["row_kept"], st.own["row_kept"])
                        w = wide(st.w)
                        for t in range(TT):
                            last = pe.transpose(w[:, t * 128:(t + 1) * 128], src[:, t, :], identf[:, :])
                        last.then_inc(wide_full, 1)

                    def qkv(st):
                        s = st.s
                        xq, xk = ({"XT": XT, "CT": CT, "CMT": CMT}[n][s] for n in (st.q_from, st.kv_from))
                        pe.wait_ge(sem["turned"], st.own["turned"])
                        pe.wait_ge(mats_loaded[PART_OF[st.w_names[0]]], 16)
                        pe.matmul(wide(st.w)[:, 0:T], mat(st.w_names[0]), xq[:, :], start=True, stop=True) \
                          .then_inc(wide_full, 1)
                        pe.matmul(wide(st.w + 1)[:, 0:T], mat(st.w_names[1]), xk[:, :], start=True, stop=True) \
                          .then_inc(wide_full, 1)
                        w = wide(st.w + 2)
                        for t in range(TT):
                            last = pe.matmul(w[:, t * 128:(t + 1) * 128], xk[:, t * 128:(t + 1) * 128],
                                             mat(st.w_names[2]), start=True, stop=True)
                        last.then_inc(wide_full, 1)

                    def lengths(st):
                        s = st.s
                        pe.wait_ge(sem["q_first"], st.own["q_first"])
                        pe.wait_ge(sem["k_read"], st.own["k_read"])
                        w = wide(st.w)
                        for b in range(NB):
                            last = pe.matmul(w[0:HEADS, b * SEQ:(b + 1) * SEQ], QF[s][:, b, :],
                                             K32[s][:, b * SEQ:(b + 1) * SEQ], start=True, stop=True)
                        last.then_inc(wide_full, 1)

                    def maxima(st):
                        s, k, n = st.s, st.k, st.base.get("stile", 0)
                        if st.g == 0 and k == 0:
                            pe.wait_ge(stacked[s], 16 * stack_dmas(st))
                        if n >= 2:
                            pe.wait_ge(sem["stile"], n - 1)
                        for j in range(2):
                            pair = st.g * PAIRS + 2 * k + j
                            h, b = pair // NB, pair % NB
                            bank = SA[n % 2][:, j * 2 * SEQ:(j + 1) * 2 * SEQ]
                            for qt in range(QT):
                                keys = (qt + 1) * 128 if st.mask == "causal" else SEQ
                                lhs = SQ[s][0:MAX_ROW, h, b * SEQ + qt * 128:b * SEQ + (qt + 1) * 128]
                                rhs = SK[s][0:MAX_ROW, h, b * SEQ:b * SEQ + keys]
                                at = qt * SEQ
                                if st.mask == "causal":
                                    last = pe.matmul(bank[:, at:at + keys], lhs, rhs, start=True, stop=False,
                                                     skip_group_check=True)
                                    last = pe.matmul(bank[:, at + keys - 128:at + keys], identb[:, :], causal_q[:, :],
                                                     start=False, stop=True, skip_group_check=True)
                                elif st.mask is None:
                                    last = pe.matmul(bank[:, at:at + keys], lhs, rhs, start=True, stop=True)
                                else:
                                    if qt == 0:
                                        pe.matmul(bank, identb[:, :], mask_q[:, st.mask, :, :].rearrange(
                                            "p t k -> p (t k)"), start=True, stop=False, skip_group_check=True)
                                    last = pe.matmul(bank[:, at:at + keys], lhs, rhs, start=False, stop=True,
                                                     skip_group_check=True)
                        last.then_inc(tile_full, 1)

                    def exp_scores(st, i):
                        s, g, n = st.s, st.g, st.base.get("prob", 0) + i
                        if n >= 2:
                            pe.wait_ge(sem["prob"], n - 1)
                        pair = g * PAIRS + 2 * st.k + i
                        h, b = pair // NB, pair % NB
                        bank = ST[n % 2]
                        for kt in range(QT):
                            lhs = SK[s][:, h, b * SEQ + kt * 128:b * SEQ + (kt + 1) * 128]
                            first = kt * 128 if st.mask == "causal" else 0
                            at = kt * SEQ
                            rhs = SQ[s][:, h, b * SEQ + first:(b + 1) * SEQ]
                            n_q = SEQ - first
                            if st.mask == "causal":
                                pe.matmul(bank[:, at:at + n_q], lhs, rhs, start=True, stop=False,
                                          skip_group_check=True)
                                last = pe.matmul(bank[:, at:at + 128], identb[:, :], causal_k[:, :], start=False,
                                                 stop=True, skip_group_check=True)
                            elif st.mask is None:
                                last = pe.matmul(bank[:, at:at + n_q], lhs, rhs, start=True, stop=True)
                            else:
                                if kt == 0:
                                    pe.matmul(bank[:, :], identb[:, :], mask_k[:, st.mask, :, :].rearrange(
                                        "p t k -> p (t k)"), start=True, stop=False, skip_group_check=True)
                                last = pe.matmul(bank[:, at:at + n_q], lhs, rhs, start=False, stop=True,
                                                 skip_group_check=True)
                        last.then_inc(prob_full, 1)

                    def exps(st):
                        s, g = st.s, st.g
                        if st.k == 0:
                            pe.wait_ge(neg_row[s][g % 2], 16 * (attention_no(st, st.attn) * GROUPS // 2 + g // 2 + 1))
                        exp_scores(st, 0)
                        exp_scores(st, 1)

                    def negatives(st):
                        pe.wait_ge(sem["neg_parts"], st.end["neg_parts"])
                        bank = wide(st.w)[:, :].bitcast(bf16)
                        for t in range(TT):
                            last = pe.transpose(bank[0:2 * GROUP, t * 128:(t + 1) * 128],
                                                HL[st.s][:, st.g % 2, t, :], identb[:, :])
                        last.then_inc(wide_full, 1)

                    def out_rows(st):
                        s, g = st.s, st.g
                        pe.wait_ge(sem["out_copied"], by[s, f"{st.attn}v{g}"].end["out_copied"])
                        bank = wide(st.w)
                        for t in range(TT):
                            last = pe.transpose(bank[:, t * 128:(t + 1) * 128],
                                                OG[s][:, g % 2, t * 128:(t + 1) * 128], identf[:, :])
                        last.then_inc(wide_full, 1)

                    def values(st):
                        s, g = st.s, st.g
                        pe.wait_ge(sem["prob"], by[s, f"{st.attn}e{g}/{TILES - 1}"].end["prob"])
                        pe.wait_ge(sem["v_ready"], st.own["v_ready"])
                        bank = wide(st.w)
                        for b in range(NB):
                            for kt in range(QT):
                                first = kt * 128 if st.mask == "causal" else 0
                                for j in range(GROUP):
                                    last = pe.matmul(
                                        bank[32 * j:32 * j + 32, b * SEQ + first:(b + 1) * SEQ],
                                        V[s][:, b * QT + kt, GROUP * g + j, :],
                                        P[s][:, g % 2, j * NB + b, kt * SEQ:kt * SEQ + SEQ - first],
                                        start=(kt == 0), stop=(kt == QT - 1), skip_group_check=True)
                        last.then_inc(wide_full, 1)

                    def turn_rows(w, src):
                        bank = wide(w)
                        for t in range(TT):
                            last = pe.transpose(bank[:, t * 128:(t + 1) * 128], src[:, t, :], identf[:, :])
                        last.then_inc(wide_full, 1)

                    def times(w, left, right):
                        bank = wide(w)
                        for t in range(TT):
                            last = pe.matmul(bank[:, t * 128:(t + 1) * 128], left[:, t * 128:(t + 1) * 128], right,
                                             start=True, stop=True)
                        last.then_inc(wide_full, 1)

                    def out_turn(st):
                        pe.wait_ge(sem[st.of], st.own[st.of])
                        turn_rows(st.w, OT[st.s])

                    def out_product(st):
                        pe.wait_ge(sem["turned"], st.own["turned"])
                        times(st.w, OF[st.s], mat(st.wo))

                    def product_down(w, s, half, chunks, weight):
                        bank = wide(w)
                        for t in range(TT):
                            for c in range(chunks):
                                last = pe.matmul(bank[:, t * 128:(t + 1) * 128],
                                                 HB[s][:, half, c, t * 128:(t + 1) * 128], weight(c),
                                                 start=(c == 0), stop=(c == chunks - 1))
                        last.then_inc(wide_full, 1)

                    def up(st):
                        src = {"XT": XT, "ET": ET}[st.x][st.s]
                        pe.wait_ge(sem["turned"], st.own["turned"])
                        pe.wait_ge(mats_loaded[PART_OF[st.w1]], 16)
                        for c in range(st.chunks):
                            pe.matmul(wide(st.w + c)[:, 0:T], mat(st.w1, c, 128), src[:, :], start=True, stop=True) \
                              .then_inc(wide_full, 1)

                    def down(st):
                        pe.wait_ge(sem["hidden"], st.own["hidden"])
                        product_down(st.w, st.s, 0, st.chunks, lambda c: mat(st.w2, c, 128))

                    def lin_qkv(st):
                        s, w = st.s, st.w
                        xq, xk = ({"XT": XT, "ET": ET}[n][s] for n in (st.q, st.kv))
                        pe.wait_ge(sem["turned"], st.own["turned"])
                        pe.wait_ge(mats_loaded[PART_OF[st.w_names[0]]], 16)
                        pe.matmul(wide(w)[:, 0:T], mat(st.w_names[0]), xq[:, :], start=True, stop=True) \
                          .then_inc(wide_full, 1)
                        times(w + 1, xk, mat(st.w_names[1]))
                        times(w + 2, xk, mat(st.w_names[2]))

                    def lin_kv(st):
                        s = st.s
                        pe.wait_ge(sem["lin_feature"], st.own["lin_feature"])
                        pe.wait_ge(sem["lin_v"], st.own["lin_v"])
                        for b in range(NB):
                            bank = wide(st.w + b)
                            for qt in range(QT):
                                last = pe.matmul(bank[:, 0:D + 1], LK[s][:, b * QT + qt, :], LV[s][:, b * QT + qt, :],
                                                 start=(qt == 0), stop=(qt == QT - 1))
                            last.then_inc(wide_full, 1)

                    def lin_out(st):
                        s = st.s
                        for b in range(NB):
                            pe.wait_ge(sem["lin_kv"], st.own["lin_kv"] - NB + b + 1)
                            bank = wide(st.w + b)
                            for qt in range(QT):
                                at = (b * QT + qt) * 128
                                last = pe.matmul(bank[:, qt * (D + LHEADS):(qt + 1) * (D + LHEADS)],
                                                 LQ[s][:, at:at + 128], KVB[s][:, b, :], start=True, stop=True)
                            last.then_inc(wide_full, 1)

                    def logits(st):
                        s = st.s
                        pe.wait_ge(sem["turned"], st.own["turned"])
                        bank = wide(st.w)
                        for t in range(TT):
                            last = pe.matmul(bank[:, t * EXPERTS:(t + 1) * EXPERTS], XT[s][:, t * 128:(t + 1) * 128],
                                             mat("L3_r"), start=True, stop=True)
                        last.then_inc(wide_full, 1)

                    def gates(st):
                        s = st.s
                        pe.wait_ge(sem["gates"], st.end["gates"])
                        bank = wide(st.w)
                        for t in range(TT):
                            last = pe.transpose(bank[0:EXPERTS, t * 128:(t + 1) * 128], G[s][:, t, :], identf[:, :])
                        last.then_inc(wide_full, 1)

                    def expert_bias(st):
                        s = st.s
                        pe.wait_ge(sem["gates_turned"], st.own["gates_turned"])
                        bank = wide(st.w)
                        for t in range(TT):
                            last = pe.matmul(bank[:, t * 128:(t + 1) * 128], GT[s][:, t * 128:(t + 1) * 128],
                                             FC2B[:, :], start=True, stop=True)
                        last.then_inc(wide_full, 1)

                    def expert(st):
                        s, w, e = st.s, st.w, st.e
                        pe.wait_ge(mats_loaded[PART_OF["M_f1"]], 16)
                        if e >= 1:
                            pe.wait_ge(sem["prob"], st.own["prob"])
                            bank = wide(w)
                        for c in range(CHUNKS):
                            if e < EXPERTS:
                                n = st.base["prob"] + c
                                pe.wait_ge(sem["prob"], n - 1)
                                pe.matmul(ST[n % 2][:, 0:T], mat("M_f1", e * CHUNKS + c, 128), XT[s][:, :],
                                          start=True, stop=True).then_inc(prob_full, 1)
                            if e >= 1:
                                for i in range(c * TT, (c + 1) * TT):
                                    t, d = i // CHUNKS, i % CHUNKS
                                    last = pe.matmul(bank[:, t * 128:(t + 1) * 128],
                                                     HB[s][:, (e - 1) % 2, d, t * 128:(t + 1) * 128],
                                                     mat("M_f2", (e - 1) * CHUNKS + d, 128),
                                                     start=(d == 0), stop=(d == CHUNKS - 1), skip_group_check=True)
                        if e >= 1:
                            last.then_inc(wide_full, 1)

                    kinds = {"turn": turn, "qkv": qkv, "lengths": lengths, "maxima": maxima,
                             "negatives": negatives, "exps": exps, "values": values, "out_rows": out_rows,
                             "out_turn": out_turn,
                             "out_product": out_product, "up": up, "down": down, "lin_qkv": lin_qkv, "lin_kv": lin_kv,
                             "lin_out": lin_out, "logits": logits, "gates": gates, "expert_bias": expert_bias,
                             "expert": expert}
                    for st in steps:
                        if st.kind in kinds:
                            kinds[st.kind](st)

                @block.scalar
                def _(act):
                    def wide(w):
                        act.wait_ge(wide_full, w + 1)
                        return W[w % 2]

                    def turn(st):
                        dst = {"XT": XT, "CT": CT, "CMT": CMT, "ET": ET}[st.dst][st.s]
                        w = wide(st.w)
                        if st.g:
                            act.activation(dst[:, :], w[:, 0:T], ACT.Identity, bias=col(st.g[1]), scale=col(st.g[0])) \
                               .then_inc(sem["turned"], 1)
                        else:
                            act.activation(dst[:, :], w[:, 0:T], ACT.Copy).then_inc(sem["turned"], 1)

                    def qkv(st):
                        s = st.s
                        w = wide(st.w + 2)
                        act.activation(V[s][:, :, :, 0:HD].rearrange("p t h d -> p (t h) d"),
                                       w[:, 0:TT * 128].rearrange("p (a d) -> p a d", d=HD), ACT.Copy) \
                           .then_inc(sem["v_ready"], 1)

                    def exps(st):
                        s, g = st.s, st.g
                        for i in range(2):
                            n = st.base.get("prob", 0) + i
                            used = 2 * SEQ - (128 if st.mask == "causal" else 0)
                            act.wait_ge(prob_full, n + 1)
                            act.activation(P[s][:, g % 2, 2 * st.k + i, 0:used], ST[n % 2][:, 0:used], ACT.Exp) \
                               .then_inc(sem["prob"], 1)

                    def negatives(st):
                        s, g = st.s, st.g
                        bank = wide(st.w)[:, :].bitcast(bf16)
                        act.activation(MT[s][:, g % 2, :], bank[0:2 * GROUP, 0:T], ACT.Copy) \
                           .then_inc(sem["neg_turned"], 1)
                        act.wait_ge(sem["neg_turned"], st.end["neg_turned"])
                        act.dma_start(SQ[s][MAX_ROW:MAX_ROW + 2, GROUP * g:GROUP * (g + 1), :], MT[s][:, g % 2, :]) \
                           .then_inc(neg_row[s][g % 2], 16)

                    def values(st):
                        act.activation(OG[st.s][:, st.g % 2, :], wide(st.w)[:, 0:T], ACT.Copy) \
                           .then_inc(sem["out_copied"], 1)

                    def out_turn(st):
                        if st.bv:
                            act.activation(OF[st.s][:, :], wide(st.w)[:, 0:T], ACT.Identity, bias=col(st.bv)) \
                               .then_inc(sem["turned"], 1)
                        else:
                            act.activation(OF[st.s][:, :], wide(st.w)[:, 0:T], ACT.Copy).then_inc(sem["turned"], 1)

                    def up(st):
                        for c in range(st.chunks):
                            w = wide(st.w + c)
                            dst = HB[st.s][:, 0, c, :]
                            if st.b1:
                                act.activation(dst, w[:, 0:T], ACT.Relu, bias=col(st.b1, c)).then_inc(sem["hidden"], 1)
                            else:
                                act.activation(dst, w[:, 0:T], ACT.Relu).then_inc(sem["hidden"], 1)

                    def lin_qkv(st):
                        s = st.s
                        for i in range(2):
                            act.wait_ge(sem["lin_min"], st.base.get("lin_min", 0) + i + 1)
                            act.activation(LE[s][:, i, :], LM[s][:, i, :], ACT.Exp).then_inc(sem["lin_exp"], 1)
                        act.activation(LV[s][:, :, 0:D], wide(st.w + 2)[:, 0:TT * 128].rearrange(
                            "p (t d) -> p t d", d=D), ACT.Copy).then_inc(sem["lin_v"], 1)

                    def logits(st):
                        s = st.s
                        act.wait_ge(sem["gate_diff"], st.end["gate_diff"])
                        act.activation(GE[s][:, :], GD[s][:, :], ACT.Exp).then_inc(sem["gate_exp"], 1)

                    def gates(st):
                        act.activation(GT[st.s][:, :], wide(st.w)[0:EXPERTS, 0:T], ACT.Copy) \
                           .then_inc(sem["gates_turned"], 1)

                    def expert(st):
                        if st.e < EXPERTS:
                            for c in range(CHUNKS):
                                n = st.base["prob"] + c
                                act.wait_ge(prob_full, n + 1)
                                act.activation(HB[st.s][:, st.e % 2, c, :], ST[n % 2][:, 0:T], ACT.Gelu,
                                               bias=col("M_fb1", st.e * CHUNKS + c)).then_inc(sem["prob"], 1)

                    kinds = {"turn": turn, "qkv": qkv, "exps": exps, "negatives": negatives, "values": values,
                             "out_turn": out_turn, "up": up,
                             "lin_qkv": lin_qkv, "logits": logits, "gates": gates, "expert": expert}
                    for st in steps:
                        if st.kind in kinds:
                            kinds[st.kind](st)

                @block.gpsimd
                def _(pool):
                    chain = [0]

                    def link(ins):
                        chain[0] += 1
                        ins.then_inc(pool_chain, 1)
                        pool.wait_ge(pool_chain, chain[0])

                    def stats(st):
                        s = st.s
                        pool.wait_ge(sem["variance"], st.end["variance"])
                        link(pool.tensor_scalar(RS[s][:, :], MV[s][:, :, 1], EPS, None, ALU.add))
                        pool.tensor_tensor(RS[s][:, :], RS[s][:, :], minus_half[:, :], ALU.pow) \
                            .then_inc(sem["rstd"], 1)

                    def affine(st):
                        if st.plus:
                            return
                        s = st.s
                        pool.wait_ge(sem["normed"], st.own["normed"])
                        link(pool.tensor_tensor(AF[s][:, :, :], XH[s][:, :, :], row(st.g), ALU.mult))
                        pool.tensor_tensor(X[s][:, :, :], AF[s][:, :, :], row(st.b), ALU.add) \
                            .then_inc(sem["affined"], 1)

                    def negatives(st):
                        s, g = st.s, st.g
                        pool.wait_ge(sem["stile"], by[s, f"{st.attn}m{g}/{TILES - 1}"].end["stile"])
                        neg = NEG[s][:, g * PAIRS * QT:(g + 1) * PAIRS * QT].rearrange("p (h t) -> p t h", t=TT)
                        src = neg
                        if st.mask in (0, 1):
                            src = HF[s][:, :, :]
                            nan = row_nan[:, st.mask, :, :].rearrange("p b t -> p (b t)")
                            link(pool.tensor_tensor(src, neg, nan.unsqueeze(2).to_broadcast([128, TT, GROUP]), ALU.add))
                        high, low = HL[s][:, g % 2, :, 0:GROUP], HL[s][:, g % 2, :, GROUP:2 * GROUP]
                        link(pool.tensor_scalar(high, src, 1.0, None, ALU.mult))
                        pool.tensor_tensor(low, src, high, ALU.subtract).then_inc(sem["neg_parts"], 1)

                    kinds = {"stats": stats, "affine": affine, "negatives": negatives}
                    for st in steps:
                        if st.kind in kinds:
                            kinds[st.kind](st)

                @block.vector
                def _(dve):
                    chain = [0]

                    def link(ins):
                        chain[0] += 1
                        ins.then_inc(dve_chain, 1)
                        dve.wait_ge(dve_chain, chain[0])

                    def own(st, *names):
                        for n in names:
                            if st.own.get(n, 0):
                                dve.wait_ge(sem[n], st.own[n])

                    def wide(w):
                        dve.wait_ge(wide_full, w + 1)
                        return W[w % 2]

                    def tokens(bank):
                        return bank[:, 0:TT * 128].rearrange("p (t d) -> p t d", d=128)

                    def load(st):
                        dve.wait_ge(loaded[st.s], 32)
                        dve.tensor_tensor(CC[st.s][:, :, :], C[st.s][:, :, :], C[st.s][:, :, :], ALU.add) \
                           .then_inc(sem["doubled"], 1)

                    def stats(st):
                        s = st.s
                        src = {"R": R, "X": X, "C": C}[st.src][s]
                        own(st, "residual", "summed")
                        for t in range(TT):
                            ins = dve.bn_stats(BN[s][:, t, :], src[:, t, :])
                        link(ins)
                        for t in range(TT):
                            ins = dve.bn_aggr(MV[s][:, t, :], BN[s][:, t, :])
                        ins.then_inc(sem["variance"], 1)

                    def normalise(st):
                        s = st.s
                        src = {"R": R, "X": X, "C": C}[st.src][s]
                        own(st, "rstd", "variance", "turned", "affined")
                        for t in range(TT):
                            ins = dve.tensor_scalar(XH[s][:, t, :], src[:, t, :], MV[s][:, t, 0:1], RS[s][:, t:t + 1],
                                                    ALU.subtract, ALU.mult)
                        ins.then_inc(sem["normed"], 1)

                    def affine(st):
                        if not st.plus:
                            return
                        s = st.s
                        dst = {"X": X, "CC": CC}[st.dst][s]
                        own(st, "normed", "doubled")
                        link(dve.tensor_tensor(AF[s][:, :, :], XH[s][:, :, :], row(st.g), ALU.mult))
                        own(st, "affined")
                        link(dve.tensor_tensor(AF[s][:, :, :], AF[s][:, :, :], row(st.b), ALU.add))
                        dve.tensor_tensor(dst[:, :, :], AF[s][:, :, :], dst[:, :, :], ALU.add) \
                           .then_inc(sem["summed"], 1)

                    def rowmask(st):
                        s = st.s
                        m = {"M0": M0, "M1": M1}[st.dst][s]
                        own(st, "affined")
                        link(dve.tensor_reduce(AM[s][:, :], X[s][:, :, :], AX.X, ALU.max, apply_absolute_value=True))
                        dve.tensor_scalar(m[:, :], AM[s][:, :], 0.0, None, ALU.not_equal).then_inc(sem["rowmask"], 1)
                        dve.wait_ge(sem["rowmask"], st.end["rowmask"])
                        if st.kv:
                            for t in range(TT):
                                ins = dve.tensor_scalar(CM[s][:, t, :], C[s][:, t, :], m[:, t:t + 1], None, ALU.mult)
                            ins.then_inc(sem["row_kept"], 1)

                    def qkv(st):
                        s = st.s
                        w = wide(st.w)
                        if st.bias[0]:
                            ins = dve.tensor_scalar(Q32[s][:, :], w[:, 0:T], col(st.bias[0]), ATTN_SCALE, ALU.add,
                                                    ALU.mult)
                        else:
                            ins = dve.tensor_scalar(Q32[s][:, :], w[:, 0:T], ATTN_SCALE, None, ALU.mult)
                        ins.then_inc(sem["q_read"], 1)
                        dve.wait_ge(sem["q_read"], st.end["q_read"])
                        if st.lengths:
                            for b in range(NB):
                                ins = dve.tensor_scalar(QF[s][:, b, :], head_mask[:, :],
                                                        Q32[s][:, b * SEQ:b * SEQ + 1], None, ALU.mult)
                            ins.then_inc(sem["q_first"], 1)
                        dve.tensor_copy(Q3[s][:, 0, :], Q32[s][:, :]).then_inc(sem["q_one"], 1)
                        dve.wait_ge(sem["q_one"], st.end["q_one"])
                        link(dve.tensor_tensor(QR[s][:, :], Q32[s][:, :], Q3[s][:, 0, :], ALU.subtract))
                        w = wide(st.w + 1)
                        if st.bias[1]:
                            ins = dve.tensor_scalar(K32[s][:, :], w[:, 0:T], col(st.bias[1]), None, ALU.add)
                        else:
                            ins = dve.tensor_copy(K32[s][:, :], w[:, 0:T])
                        ins.then_inc(sem["k_read"], 1)
                        dve.wait_ge(sem["k_read"], st.end["k_read"])
                        dve.tensor_copy(K3[s][:, 0, :], K32[s][:, :]).then_inc(sem["k_one"], 1)
                        dve.tensor_copy(Q3[s][:, 1, :], QR[s][:, :]).then_inc(sem["q_two"], 1)
                        dve.wait_ge(sem["q_two"], st.end["q_two"])
                        dve.tensor_tensor(Q3[s][:, 2, :], QR[s][:, :], Q3[s][:, 1, :], ALU.subtract) \
                           .then_inc(sem["q_three"], 1)
                        dve.wait_ge(sem["k_one"], st.end["k_one"])
                        link(dve.tensor_tensor(KR[s][:, :], K32[s][:, :], K3[s][:, 0, :], ALU.subtract))
                        dve.tensor_copy(K3[s][:, 1, :], KR[s][:, :]).then_inc(sem["k_two"], 1)
                        dve.wait_ge(sem["k_two"], st.end["k_two"])
                        dve.tensor_tensor(K3[s][:, 2, :], KR[s][:, :], K3[s][:, 1, :], ALU.subtract) \
                           .then_inc(sem["k_three"], 1)

                    def lengths(st):
                        s = st.s
                        w = wide(st.w)
                        dve.tensor_scalar(NZ[s][:, :, :].rearrange("h b k -> h (b k)"), w[0:HEADS, 0:T], 0.0, None,
                                          ALU.not_equal).then_inc(sem["len_read"], 1)
                        dve.wait_ge(sem["len_read"], st.end["len_read"])
                        link(dve.tensor_reduce(LEN[s][:, :], NZ[s][:, :, :], AX.X, ALU.add))
                        link(dve.tensor_scalar(LNAN[s][:, :], LEN[s][:, :], 0.0, HUGE, ALU.is_equal, ALU.mult))
                        link(dve.tensor_scalar(LNAN[s][:, :], LNAN[s][:, :], HUGE, 0.0, ALU.mult, ALU.mult))
                        for b in range(NB):
                            ins = dve.tensor_scalar(NZ[s][:, b, :], key_no[:, :], LEN[s][:, b:b + 1], MASKED,
                                                    ALU.is_ge, ALU.mult)
                        link(ins)
                        for b in range(NB):
                            ins = dve.tensor_scalar(LB[s][:, b * SEQ:(b + 1) * SEQ], NZ[s][:, b, :],
                                                    LNAN[s][:, b:b + 1], None, ALU.add)
                        ins.then_inc(sem["len_row"], 1)

                    def maxima(st):
                        s, n = st.s, st.base.get("stile", 0)
                        dve.wait_ge(tile_full, n + 1)
                        at = (st.g * TILES + st.k) * 2 * QT
                        dst = NEG[s][:, at:at + 2 * QT]
                        tile = SA[n % 2][:, :].rearrange("p (j t k) -> p j t k", j=2, t=QT)
                        if st.mask == "causal":
                            dst = dst.rearrange("p (j t) -> p j t", t=QT)
                            for qt in range(QT):
                                ins = dve.tensor_reduce(dst[:, :, qt], tile[:, :, qt, 0:(qt + 1) * 128], AX.X,
                                                        ALU.max, negate=True)
                        else:
                            ins = dve.tensor_reduce(dst, tile.rearrange("p j t k -> p (j t) k"), AX.X, ALU.max,
                                                    negate=True)
                        ins.then_inc(sem["stile"], 1)

                    def out_rows(st):
                        s, g = st.s, st.g
                        w = wide(st.w)[:, 0:TT * 128].rearrange("p (t j m) -> p t j m", t=TT, j=GROUP)
                        own(st, "out_scaled")
                        link(dve.reciprocal(RC[s][:, :, :], w[:, :, :, HD]))
                        if st.lengths:
                            own(st, "rowmask")
                            m = (M0 if st.mask == "causal" else M1)[s]
                            link(dve.tensor_tensor(RC[s][:, :, :], RC[s][:, :, :],
                                                   m[:, :].unsqueeze(2).to_broadcast([128, TT, GROUP]), ALU.mult))
                        dst = OT[s][:, :, GROUP * HD * g:GROUP * HD * (g + 1)].rearrange("p t (j d) -> p t j d", d=HD)
                        dve.tensor_tensor(dst, w[:, :, :, 0:HD],
                                          RC[s][:, :, :].unsqueeze(3).to_broadcast([128, TT, GROUP, HD]), ALU.mult) \
                           .then_inc(sem["out_scaled"], 1)

                    def out_product(st):
                        s = st.s
                        bank = tokens(wide(st.w))
                        if not st.acc:
                            dve.tensor_copy(R[s][:, :, :], bank).then_inc(sem["residual"], 1)
                            return
                        own(st, "affined")
                        dve.tensor_tensor(AF[s][:, :, :], bank, row(st.bo), ALU.add).then_inc(sem["out_read"], 1)
                        dve.wait_ge(sem["out_read"], st.end["out_read"])
                        dve.tensor_tensor({"R": R, "X": X}[st.acc][s][:, :, :], AF[s][:, :, :], X[s][:, :, :],
                                          ALU.add).then_inc(sem["residual"], 1)

                    def addz(st):
                        s = st.s
                        own(st, "affined", "out_scaled")
                        dve.tensor_tensor(R[s][:, :, :], OT[s][:, :, :], X[s][:, :, :], ALU.add) \
                           .then_inc(sem["residual"], 1)

                    def down(st):
                        s = st.s
                        w = wide(st.w)
                        if not st.b2:
                            dve.tensor_copy(R[s][:, :, :], tokens(w)).then_inc(sem["residual"], 1)
                            return
                        dve.tensor_tensor(R[s][:, :, :], tokens(w), row(st.b2), ALU.add).then_inc(sem["ff_read"], 1)
                        dve.wait_ge(sem["ff_read"], st.end["ff_read"])
                        if st.mask:
                            for t in range(TT):
                                ins = dve.tensor_scalar(R[s][:, t, :], R[s][:, t, :], M0[s][:, t:t + 1], None, ALU.mult)
                            link(ins)
                        own(st, "affined")
                        dve.tensor_tensor(R[s][:, :, :], R[s][:, :, :], X[s][:, :, :], ALU.add) \
                           .then_inc(sem["residual"], 1)

                    def lin_qkv(st):
                        s = st.s
                        for i in range(2):
                            dve.tensor_scalar(LM[s][:, i, :], wide(st.w + i)[:, 0:T], 0.0, None, ALU.min) \
                               .then_inc(sem["lin_min"], 1)
                        for i, dst in enumerate((LQ[s][:, :], LK[s][:, :, :].rearrange("p t d -> p (t d)"))):
                            dve.wait_ge(sem["lin_exp"], st.base.get("lin_exp", 0) + i + 1)
                            dve.scalar_tensor_tensor(out=dst, in0=W[(st.w + i) % 2][:, 0:T], scalar=0.0,
                                                     in1=LE[s][:, i, :], op0=ALU.max, op1=ALU.add) \
                               .then_inc(sem["lin_feature"], 1)

                    def lin_kv(st):
                        s = st.s
                        for b in range(NB):
                            w = wide(st.w + b)
                            dve.tensor_tensor(KVB[s][:, b, 0:D], w[:, 0:D],
                                              block_mask[:, :, :].rearrange("p h d -> p (h d)"), ALU.mult)
                            dve.tensor_scalar(KVB[s][:, b, D:D + LHEADS], block_sum[:, :], w[:, D:D + 1], None,
                                              ALU.mult).then_inc(sem["lin_kv"], 1)

                    def lin_out(st):
                        s = st.s
                        for b in range(NB):
                            w = wide(st.w + b)[:, 0:QT * (D + LHEADS)].rearrange("p (t n) -> p t n", t=QT)
                            link(dve.tensor_scalar(LZ[s][:, :, :], w[:, :, D:D + LHEADS], 1e-6, None, ALU.add))
                            link(dve.reciprocal(LZ[s][:, :, :], LZ[s][:, :, :]))
                            dve.tensor_tensor(
                                OT[s][:, b * QT:(b + 1) * QT, :].rearrange("p t (h d) -> p t h d", d=LHD),
                                w[:, :, 0:D].rearrange("p t (h d) -> p t h d", d=LHD),
                                LZ[s][:, :, :].unsqueeze(3).to_broadcast([128, QT, LHEADS, LHD]), ALU.mult) \
                               .then_inc(sem["lin_out"], 1)

                    def logits(st):
                        s = st.s
                        w = wide(st.w)[:, 0:TT * EXPERTS].rearrange("p (t e) -> p t e", t=TT)
                        dve.tensor_tensor(LG[s][:, :, :], w, row("L3_rb"), ALU.add).then_inc(sem["route_read"], 1)
                        dve.wait_ge(sem["route_read"], st.end["route_read"])
                        for t in range(TT):
                            ins = dve.max(MX[s][:, t, :], LG[s][:, t, :])
                        link(ins)
                        dve.tensor_tensor(GD[s][:, :], MX[s][:, :, 1], MX[s][:, :, 0], ALU.subtract) \
                           .then_inc(sem["gate_diff"], 1)
                        for t in range(TT):
                            ins = dve.max_index(IX[s][:, t, :], MX[s][:, t, :], LG[s][:, t, :])
                        link(ins)
                        link(dve.tensor_copy(IXF[s][:, :, :], IX[s][:, :, 0:2]))

                    def gates(st):
                        s = st.s
                        dve.wait_ge(sem["gate_exp"], st.own["gate_exp"])
                        link(dve.tensor_scalar(GP[s][:, :], GE[s][:, :], 1.0, None, ALU.add))
                        link(dve.reciprocal(GP[s][:, :], GP[s][:, :]))
                        link(dve.tensor_tensor(GQ[s][:, :], GE[s][:, :], GP[s][:, :], ALU.mult))
                        for t in range(TT):
                            dve.tensor_scalar(G[s][:, t, :], expert_no[:, :], IXF[s][:, t, 0:1], GP[s][:, t:t + 1],
                                              ALU.is_equal, ALU.mult)
                            ins = dve.tensor_scalar(G2[s][:, t, :], expert_no[:, :], IXF[s][:, t, 1:2],
                                                    GQ[s][:, t:t + 1], ALU.is_equal, ALU.mult)
                        link(ins)
                        dve.tensor_tensor(G[s][:, :, :], G[s][:, :, :], G2[s][:, :, :], ALU.add) \
                           .then_inc(sem["gates"], 1)

                    def expert_bias(st):
                        s = st.s
                        own(st, "gates", "residual")
                        dve.tensor_tensor(X[s][:, :, :], tokens(wide(st.w)), X[s][:, :, :], ALU.add) \
                           .then_inc(sem["expert_mixed"], 1)

                    def expert(st):
                        s, e = st.s, st.e - 1
                        if e < 0:
                            return
                        w = tokens(wide(st.w))
                        own(st, "expert_mixed")
                        for t in range(TT):
                            ins = dve.scalar_tensor_tensor(out=X[s][:, t, :], in0=w[:, t, :],
                                                           scalar=G[s][:, t, e:e + 1], in1=X[s][:, t, :],
                                                           op0=ALU.mult, op1=ALU.add)
                        ins.then_inc(sem["expert_mixed"], 1)

                    kinds = {"load": load, "stats": stats, "normalise": normalise, "affine": affine,
                             "rowmask": rowmask, "qkv": qkv, "lengths": lengths, "maxima": maxima, "out_rows": out_rows,
                             "out_product": out_product, "addz": addz, "down": down, "lin_qkv": lin_qkv,
                             "lin_kv": lin_kv, "lin_out": lin_out, "logits": logits, "gates": gates,
                             "expert_bias": expert_bias, "expert": expert}
                    for st in steps:
                        if st.kind in kinds:
                            kinds[st.kind](st)
            nc.all_engine_barrier()
            nc.gpsimd.sem_clear(range(min(numbers), max(numbers) + 1))
            nc.all_engine_barrier()


def _by_dim(w):
    import numpy as np
    return np.transpose(w, (1, 2, 0)).reshape(D, D)


def _cols_by_dim(w):
    import numpy as np
    return np.swapaxes(w.reshape(*w.shape[:-1], HEADS, HD), -1, -2).reshape(w.shape)


def _down(w):
    import numpy as np
    return np.transpose(w.reshape(-1, 128, w.shape[1]), (1, 0, 2)).reshape(128, -1)


def kernel(**inputs):
    import numpy as np
    import concourse.bacc as bacc
    from concourse.bass_utils import run_bass_kernel_spmd

    a = {k: np.asarray(v) for k, v in inputs.items()}
    L = [{k[len(f"L{i}_xattn_"):]: v for k, v in a.items() if k.startswith(f"L{i}_xattn_")} for i in range(4)]
    sa, ca = L[3]["sa_in_w"], L[3]["ca_in_w"]
    m = {
        "L0_q": _cols_by_dim(L[0]["wq_s"]), "L0_k": _cols_by_dim(L[0]["wk_s"]), "L0_v": L[0]["wv_s"], "L0_o": L[0]["wo_s"],
        "L0_cq": _cols_by_dim(L[0]["wq_c"]), "L0_ck": _cols_by_dim(L[0]["wk_c"]), "L0_cv": L[0]["wv_c"],
        "L0_co": L[0]["wo_c"], "L0_f1": L[0]["ff1_w"], "L0_f2": _down(L[0]["ff2_w"]),
        "L1_q": _by_dim(L[1]["Wq1"]), "L1_k": _by_dim(L[1]["Wk1"]),
        "L1_v": np.transpose(L[1]["Wv1"], (1, 0, 2)).reshape(D, D),
        "L1_cq": _by_dim(L[1]["Wq2"]), "L1_ck": _by_dim(L[1]["Wk2"]),
        "L1_cv": np.transpose(L[1]["Wv2"], (1, 0, 2)).reshape(D, D),
        "L1_f1": L[1]["fc1_w"].T, "L1_f2": L[1]["fc2_w"].T,
        "E_q": L[2]["e_wq"], "E_k": L[2]["e_wk"], "E_v": L[2]["e_wv"], "E_m": L[2]["e_wm"], "E_f1": L[2]["e_w1"],
        "E_f2": _down(L[2]["e_w2"]),
        "S_q": L[2]["d_wq0"], "S_k": L[2]["d_wk0"], "S_v": L[2]["d_wv0"], "S_m": L[2]["d_wm0"],
        "C_q": L[2]["d_wq1"], "C_k": L[2]["d_wk1"], "C_v": L[2]["d_wv1"], "C_m": L[2]["d_wm1"],
        "D_f1": L[2]["d_w1"], "D_f2": _down(L[2]["d_w2"]),
        "L3_q": _cols_by_dim(sa[0:D].T), "L3_k": _cols_by_dim(sa[D:2 * D].T), "L3_v": sa[2 * D:].T,
        "L3_o": L[3]["sa_out_w"].T,
        "L3_cq": _cols_by_dim(ca[0:D].T), "L3_ck": _cols_by_dim(ca[D:2 * D].T), "L3_cv": ca[2 * D:].T,
        "L3_co": L[3]["ca_out_w"].T, "L3_r": L[3]["router_w"].T,
        "M_f1": np.transpose(L[3]["e_fc1_w"], (2, 0, 1)).reshape(D, -1),
        "M_f2": np.transpose(L[3]["e_fc2_w"].reshape(EXPERTS, D, DFF // 128, 128), (3, 0, 2, 1)).reshape(128, -1),
    }
    sb_, cb_ = L[3]["sa_in_b"], L[3]["ca_in_b"]
    c = {
        "L0_bq": _cols_by_dim(L[0]["bq_s"]), "L0_bk": _cols_by_dim(L[0]["bk_s"]), "L0_bv": L[0]["bv_s"],
        "L0_cbq": _cols_by_dim(L[0]["bq_c"]), "L0_cbk": _cols_by_dim(L[0]["bk_c"]), "L0_cbv": L[0]["bv_c"],
        "L0_fb1": L[0]["ff1_b"], "L1_fb1": L[1]["fc1_b"],
        "L3_bq": _cols_by_dim(sb_[0:D]), "L3_bk": _cols_by_dim(sb_[D:2 * D]), "L3_bv": sb_[2 * D:],
        "L3_cbq": _cols_by_dim(cb_[0:D]), "L3_cbk": _cols_by_dim(cb_[D:2 * D]), "L3_cbv": cb_[2 * D:],
        "L3_g1": L[3]["sa_ln_g"], "L3_b1": L[3]["sa_ln_b"], "L3_g2": L[3]["ca_q_ln_g"], "L3_b2": L[3]["ca_q_ln_b"],
        "L3_gk": L[3]["ca_kv_ln_g"], "L3_bkv": L[3]["ca_kv_ln_b"], "L3_g3": L[3]["moe_ln_g"], "L3_b3": L[3]["moe_ln_b"],
        "M_fb1": L[3]["e_fc1_b"].reshape(-1),
    }
    r = {"L0_bo": L[0]["bo_s"], "L0_cbo": L[0]["bo_c"], "L0_fb2": L[0]["ff2_b"], "L1_fb2": L[1]["fc2_b"],
         "L3_bo": L[3]["sa_out_b"], "L3_cbo": L[3]["ca_out_b"], "L3_rb": L[3]["router_b"]}
    for i in (0, 1):
        for n in (1, 2, 3):
            for kind in "gb":
                c[f"L{i}_{kind}{n}"] = r[f"L{i}_{kind}{n}"] = L[i][f"ln{n}_{kind}"]
    for kind in "gb":
        for n in (1, 2):
            r[f"E_{kind}{n}"] = L[2][f"e_{kind}{n}"]
        for n in (0, 1, 2):
            r[f"D_{kind}{n}"] = L[2][f"d_{kind}{n}"]

    arrays = {
        "x": a["x"], "ctx": a["ctx_1024"],
        "mask0": a["mask_1x1xSxS2_ik0"].reshape(SEQ, SEQ), "mask1": a["mask_1x1xSxS2_if1"].reshape(SEQ, SEQ),
        "mats": np.concatenate([m[n] for n in MAT_AT], axis=1),
        "cols": np.concatenate([c[n].reshape(-1, 128) for n in COL_AT], axis=0).T,
        "rows": np.concatenate([r[n] for n in ROW_AT]),
        "fc2_bias": L[3]["e_fc2_b"],
    }
    arrays = {k: np.ascontiguousarray(v) for k, v in arrays.items()}
    nc = bacc.Bacc("TRN2", target_bir_lowering=False, num_devices=1)
    args = [nc.dram_tensor(f"in_{k}", v.shape, mybir.dt.from_np(v.dtype), kind="ExternalInput").ap()
            for k, v in arrays.items()]
    out = nc.dram_tensor("out", (BATCHES, SEQ, D), mybir.dt.float32, kind="ExternalOutput").ap()
    build(nc, *args, out)
    got = run_bass_kernel_spmd(nc, [{f"in_{k}": v for k, v in arrays.items()}], core_ids=[0])
    return got.results[0]["out"]
```

```python
import concourse.bass as bass
from concourse import mybir
from contextlib import ExitStack
import numpy as np

BATCHES, SEQ, D = 8, 256, 128
HEADS, HD = 16, 8
LHEADS, LHD = 8, 16
EXPERTS, DFF = 8, 512
CHUNKS = DFF // 128
QT = SEQ // 128
NB = 1
STREAMS = 4
T = NB * SEQ
TT = NB * QT
ROUNDS = BATCHES // (NB * STREAMS)
LAST_STREAMS = BATCHES // NB - ROUNDS * STREAMS
GROUP = 4
GROUPS = HEADS // GROUP
PV_ROWS = 32
PAIRS = GROUP * NB
P_TILES = 3
TILES = PAIRS // 2
EPS = 1e-5
MASKED = -1e30
HUGE = 3e38
TWO_ONES = float(np.array([0x3F803F80], np.uint32).view(np.float32)[0])
ATTN_SCALE = 1.0 / float(np.sqrt(HD))
SPLIT_ROWS, LEN_ROW, MAX_ROW = 48, 64, 96

WITH_LENGTHS, CLEARS_LENGTHS = ("a2", "a3"), "a4"

MATS = [
    [("L0_q", 128), ("L0_k", 128), ("L0_v", 128), ("L0_o", 128), ("L0_cq", 128), ("L0_ck", 128), ("L0_cv", 128),
     ("L0_co", 128), ("L0_f1", 512), ("L0_f2", 512)],
    [("L1_q", 128), ("L1_k", 128), ("L1_v", 128), ("L1_cq", 128), ("L1_ck", 128), ("L1_cv", 128), ("L1_f1", 128),
     ("L1_f2", 128)],
    [("E_q", 128), ("E_k", 128), ("E_v", 128), ("E_m", 128), ("E_f1", 256), ("E_f2", 256),
     ("S_q", 128), ("S_k", 128), ("S_v", 128), ("S_m", 128), ("C_q", 128), ("C_k", 128), ("C_v", 128), ("C_m", 128),
     ("D_f1", 256), ("D_f2", 256)],
    [("L3_q", 128), ("L3_k", 128), ("L3_v", 128), ("L3_o", 128), ("L3_cq", 128), ("L3_ck", 128), ("L3_cv", 128),
     ("L3_co", 128), ("L3_r", 8)],
]
EXPERT_MATS = ("M_f1", "M_f2")
COLS = [("L0_bq", 1), ("L0_bk", 1), ("L0_bv", 1), ("L0_cbq", 1), ("L0_cbk", 1), ("L0_cbv", 1), ("L0_fb1", 4),
        ("L0_g1", 1), ("L0_b1", 1), ("L0_g2", 1), ("L0_b2", 1), ("L0_g3", 1), ("L0_b3", 1),
        ("L1_g1", 1), ("L1_b1", 1), ("L1_g2", 1), ("L1_b2", 1), ("L1_g3", 1), ("L1_b3", 1), ("L1_fb1", 1),
        ("L3_bq", 1), ("L3_bk", 1), ("L3_bv", 1), ("L3_cbq", 1), ("L3_cbk", 1), ("L3_cbv", 1),
        ("L3_g1", 1), ("L3_b1", 1), ("L3_g2", 1), ("L3_b2", 1), ("L3_gk", 1), ("L3_bkv", 1), ("L3_g3", 1), ("L3_b3", 1),
        ("M_fb1", EXPERTS * DFF // 128)]
ROWS = [("L0_bo", 128), ("L0_cbo", 128), ("L0_fb2", 128), ("L0_g1", 128), ("L0_b1", 128), ("L0_g2", 128),
        ("L0_b2", 128), ("L0_g3", 128), ("L0_b3", 128),
        ("L1_g1", 128), ("L1_b1", 128), ("L1_g2", 128), ("L1_b2", 128), ("L1_g3", 128), ("L1_b3", 128), ("L1_fb2", 128),
        ("E_g1", 128), ("E_b1", 128), ("E_g2", 128), ("E_b2", 128), ("D_g0", 128), ("D_b0", 128),
        ("D_g1", 128), ("D_b1", 128), ("D_g2", 128), ("D_b2", 128),
        ("L3_bo", 128), ("L3_cbo", 128), ("L3_rb", 8)]

LASTS = {
    "load": [("DMA", 0.9), ("WAIT", 2.0)], "turn": [("PE", 0.25), ("ACT", 0.4)], "stats": [("DVE", 0.7), ("POOL", 0.9)],
    "normalise": [("DVE", 0.5)], "affine": [("POOL", 1.5)], "plus": [("DVE", 1.2)], "rowmask": [("DVE", 0.7)],
    "qkv": [("PE", 1.4), ("WAIT", -0.9), ("DVE", 2.7), ("WAIT", -2.3), ("DMA", 7.6), ("WAIT", 1.8)],
    "lengths": [("PE", 0.5), ("DVE", 1.6), ("DMA", 0.6), ("WAIT", 1.7)],
    "maxima": [("PE", 0.45), ("DVE", 1.15)], "neg_split": [("POOL", 0.8)],
    "negatives": [("PE", 0.1), ("ACT", 0.4), ("DMA", 0.6), ("WAIT", 1.7)],
    "exps": [("PE", 0.45), ("ACT", 0.95)], "values": [("PE", 1.05), ("ACT", 0.35)],
    "out_rows": [("PE", 0.22), ("DVE", 0.4)],
    "out_turn": [("PE", 0.25), ("ACT", 0.4)], "out_product": [("PE", 0.5), ("DVE", 0.8)], "addz": [("DVE", 0.3)],
    "up": [("PE", 1.0), ("ACT", 0.5)], "down": [("PE", 1.0), ("DVE", 0.8)],
    "lin_qkv": [("PE", 1.5), ("DVE", 0.7), ("ACT", 0.6), ("DVE", 0.7)], "lin_kv": [("PE", 0.6), ("DVE", 0.4)],
    "lin_out": [("PE", 0.8), ("DVE", 0.8)], "logits": [("PE", 0.3), ("DVE", 1.0), ("ACT", 0.3)],
    "gates": [("DVE", 1.2)], "gates_turn": [("PE", 0.3), ("ACT", 0.5)], "expert_bias": [("PE", 0.5), ("DVE", 0.4)],
    "expert": [("PE", 3.55), ("WAIT", -2.5), ("ACT", 2.4), ("DVE", 0.5)], "store": [],
    "double": [("DVE", 0.4)], "restore": [("POOL", 3.6)], "fetch": [("DMA", 0.9), ("WAIT", 2.5)],
}
TABLE_OF = {"exps": "Exp", "lin_qkv": "Exp", "logits": "Exp", "expert": "Gelu"}
TABLE_LOAD = 1.3
HOP = 0.15
URGENCY = 0.01562
AHEAD = {
    "logits": -0.2, "neg_split": 0.2, "normalise": 0.5, "negatives": 0.5, "stats": 0.5, "restore": 0.2,
    "double": 1, "expert": -1, "load": -1, "affine": 0.5, "addz": 0.2, "turn": 0.2, "lengths": 0.2,
}
LAG = 20


def hops_of(kind, p):
    hops = LASTS["plus" if kind == "affine" and p["plus"] else kind]
    if kind in ("maxima", "exps") and p["mask"] in (0, 1):
        return [(hops[0][0], 2 * hops[0][1]), *hops[1:]]
    return hops


def lasts(kind, p):
    return sum(t + HOP for _, t in hops_of(kind, p))


def places(entries):
    at, out = 0, {}
    for name, n in entries:
        out[name] = (at, n)
        at += n
    return out, at


MAT_AT, MAT_COLS = places([e for part in MATS for e in part])
PART_ENDS = [sum(n for part in MATS[:i + 1] for _, n in part) for i in range(len(MATS))]
COL_AT, COL_COLS = places(COLS)
ROW_AT, ROW_COLS = places(ROWS)
PART_OF = {name: i for i, part in enumerate(MATS) for name, _ in part}


def uses(kind, p):
    if kind == "turn":
        return {"turned": 1}, [("turned", 1)]
    if kind == "stats":
        return {"variance": 1, "rstd": 1}, []
    if kind == "normalise":
        return {"normed": 1}, []
    if kind == "affine":
        return ({"summed": 1} if p["plus"] else {"affined": 1}), []
    if kind == "rowmask":
        return ({"rowmask": 1, "row_kept": 1} if p["kv"] else {"rowmask": 1}), []
    if kind == "qkv":
        n = {"q_read": 1, "q_one": 1, "q_two": 1, "q_three": 1, "k_read": 1, "k_one": 1, "k_two": 1, "k_three": 1,
             "v_ready": 1}
        if p["lengths"]:
            n["q_first"] = 1
        return n, [("q_read", 1), ("k_read", 1), ("v_ready", 1)]
    if kind == "lengths":
        return {"len_read": 1, "len_row": 1}, [("len_read", 1)]
    if kind == "maxima":
        return {"stile": 1}, []
    if kind == "neg_split":
        return {"neg_parts": 1}, []
    if kind == "negatives":
        return {"neg_turned": 1}, [("neg_turned", 1)]
    if kind == "exps":
        return {"prob": 2}, []
    if kind == "values":
        return {"out_copied": 1}, [("out_copied", 1)]
    if kind == "out_rows":
        return {"out_scaled": 1}, [("out_scaled", 1)]
    if kind == "out_turn":
        return {"turned": 1}, [("turned", 1)]
    if kind == "out_product":
        if p["acc"]:
            return {"out_read": 1, "residual": 1}, [("out_read", 1)]
        return {"residual": 1}, [("residual", 1)]
    if kind == "addz":
        return {"residual": 1}, []
    if kind == "up":
        return {"hidden": p["chunks"]}, [("hidden", i + 1) for i in range(p["chunks"])]
    if kind == "down":
        if p["b2"]:
            return {"ff_read": 1, "residual": 1}, [("ff_read", 1)]
        return {"residual": 1}, [("residual", 1)]
    if kind == "lin_qkv":
        return ({"lin_min": 2, "lin_exp": 2, "lin_feature": 2, "lin_v": 1},
                [("lin_v", 1), ("lin_feature", 1), ("lin_feature", 2)])
    if kind == "lin_kv":
        return {"lin_kv": NB}, [("lin_kv", b + 1) for b in range(NB)]
    if kind == "lin_out":
        return {"lin_out": NB}, [("lin_out", b + 1) for b in range(NB)]
    if kind == "logits":
        return {"route_read": 1, "gate_diff": 1, "gate_exp": 1}, [("route_read", 1)]
    if kind == "gates":
        return {"gates": 1}, []
    if kind == "gates_turn":
        return {"gates_turned": 1}, [("gates_turned", 1)]
    if kind == "restore":
        return {"restored": 1}, []
    if kind == "expert_bias":
        return {"expert_mixed": 1}, [("expert_mixed", 1)]
    if kind == "expert":
        n, w = {}, []
        if p["e"] < EXPERTS:
            n["prob"] = CHUNKS
        if p["e"] >= 1:
            n["expert_mixed"] = 1
            w.append(("expert_mixed", 1))
        return n, w
    if kind == "double":
        return {"doubled": 1}, []
    return {}, []


def stream_steps():
    out = []

    def add(kind, name, needs=None, **p):
        out.append((kind, name, p, needs if needs is not None else [out[-1][1]] if out else []))

    def attention(n, q_from, kv_from, w, bias, mask, lengths, needs, rows=()):
        add("qkv", n, needs, q_from=q_from, kv_from=kv_from, w_names=w, bias=bias, lengths=lengths, mask=mask)
        if lengths:
            add("lengths", f"{n}l")
        before = [f"{n}l"] if lengths else [n]
        for g in range(GROUPS + 4):
            for k in range(TILES):
                if g < GROUPS:
                    add("maxima", f"{n}m{g}/{k}", before, attn=n, g=g, k=k, mask=mask, lengths=lengths)
                    before = [f"{n}m{g}/{k}"]
                    if k == TILES - 2 and g >= 2:
                        before = [*before, f"{n}n{g - 2}"]
                e = g - 2
                if 0 <= e < GROUPS:
                    needs = [f"{n}e{e}/{k - 1}"] if k else [f"{n}n{e}"]
                    former = (e * TILES + k - P_TILES) // TILES
                    if former >= 0:
                        needs.append(f"{n}v{former}")
                    add("exps", f"{n}e{e}/{k}", needs, attn=n, g=e, k=k, mask=mask)
                e = g - 1
                if k == 0 and 0 <= e < GROUPS:
                    add("neg_split", f"{n}s{e}", [f"{n}m{e}/{TILES - 1}"], attn=n, g=e, mask=mask)
                    needs = [f"{n}s{e}"] + [f"{n}e{e - 2}/0"] * (e >= 2) + [f"{n}n{e - 1}"] * (e >= 1)
                    add("negatives", f"{n}n{e}", needs, attn=n, g=e, mask=mask)
            e = g - 4
            if 0 <= e < GROUPS:
                needs = [f"{n}v{e}"] + ([f"{n}r{e - 1}"] if e else list(rows))
                add("out_rows", f"{n}r{e}", needs, attn=n, g=e, mask=mask, lengths=lengths)
            e = g - 3
            if 0 <= e < GROUPS:
                needs = [f"{n}e{e}/{TILES - 1}"] + [f"{n}r{e - 1}"] * (e >= 1) + [f"{n}v{e - 1}"] * (e >= 1)
                add("values", f"{n}v{e}", needs, attn=n, g=e, mask=mask)

    def norm(n, src, needs=None):
        add("stats", f"{n}s", needs, src=src)
        add("normalise", n, src=src)

    def project(n, wo, bv, bo, acc, target=()):
        add("out_turn", f"{n}t", [f"a{n[1:]}r{GROUPS - 1}"], bv=bv, of="out_scaled")
        add("out_product", n, [f"{n}t", *target], wo=wo, bo=bo, acc=acc)

    def feed_forward(n, x, needs, w1, b1, w2, b2, chunks, mask, target=()):
        add("up", f"{n}u", needs, x=x, w1=w1, b1=b1, chunks=chunks)
        add("down", n, [f"{n}u", *target], w2=w2, b2=b2, chunks=chunks, mask=mask)

    def linear(n, q, kv, w_names, needs, room=(), target=()):
        add("lin_qkv", f"{n}q", needs, q=q, kv=kv, w_names=w_names)
        add("lin_kv", f"{n}k")
        add("lin_out", f"{n}o")
        add("out_turn", f"{n}t", [f"{n}o", *room], bv=None, of="lin_out")
        add("out_product", n, [f"{n}t", *target], wo=w_names[3], bo=None, acc=None)

    add("load", "load")
    add("restore", "clean", ["load"])
    add("turn", "x", ["load"], src="X", dst="XT", g=None, after=("load",))
    attention("a0", "XT", "XT", ("L0_q", "L0_k", "L0_v"), ("L0_bq", "L0_bk"), 0, False, ["x", "clean"])
    add("turn", "c", ["x"], src="C", dst="CT", g=None, after=("load",))
    project("o0", wo="L0_o", bv="L0_bv", bo="L0_bo", acc="R")
    norm("n0", "R")
    add("turn", "h1", src="XH", dst="XT", g=("L0_g1", "L0_b1"), after=("norm", "n0"))
    add("affine", "f0", ["n0"], g="L0_g1", b="L0_b1", dst="X", plus=None)
    attention("a1", "XT", "CT", ("L0_cq", "L0_ck", "L0_cv"), ("L0_cbq", "L0_cbk"), 1, False, ["h1", "c"], ["f0"])
    project("o1", wo="L0_co", bv="L0_cbv", bo="L0_cbo", acc="R")
    norm("n1", "R")
    add("turn", "h2", src="XH", dst="XT", g=("L0_g2", "L0_b2"), after=("norm", "n1"))
    add("affine", "f1", ["n1"], g="L0_g2", b="L0_b2", dst="X", plus=None)
    feed_forward("ff0", "XT", ["h2"], w1="L0_f1", b1="L0_fb1", w2="L0_f2", b2="L0_fb2", chunks=4, mask=None,
                 target=["f1"])
    norm("n2", "R", ["ff0", "f1"])
    add("turn", "x1", src="XH", dst="XT", g=("L0_g3", "L0_b3"), after=("norm", "n2"))
    add("affine", "f2", ["n2"], g="L0_g3", b="L0_b3", dst="X", plus=None)
    add("rowmask", "m0", ["f2"], dst="M0", kv=False)
    attention("a2", "XT", "XT", ("L1_q", "L1_k", "L1_v"), (None, None), "causal", True, ["x1"], ["m0"])
    add("addz", "z0", [f"a2r{GROUPS - 1}"])
    norm("n3", "R")
    add("turn", "y1", src="XH", dst="XT", g=("L1_g1", "L1_b1"), after=("norm", "n3"))
    add("affine", "f3", ["n3"], g="L1_g1", b="L1_b1", dst="X", plus=None)
    add("rowmask", "m1", dst="M1", kv=True)
    add("turn", "cm", src="CM", dst="CMT", g=None, after=("rowmask", "m1"))
    attention("a3", "XT", "CMT", ("L1_cq", "L1_ck", "L1_cv"), (None, None), None, True, ["y1", "cm"])
    add("addz", "z1", [f"a3r{GROUPS - 1}"])
    norm("n4", "R")
    add("turn", "y2", src="XH", dst="XT", g=("L1_g2", "L1_b2"), after=("norm", "n4"))
    add("affine", "f4", ["n4"], g="L1_g2", b="L1_b2", dst="X", plus=None)
    feed_forward("ff1", "XT", ["y2"], w1="L1_f1", b1="L1_fb1", w2="L1_f2", b2="L1_fb2", chunks=1, mask="M0",
                 target=["f4"])
    norm("n5", "R", ["ff1", "f4"])
    add("affine", "f5", ["n5"], g="L1_g3", b="L1_b3", dst="X", plus=None)
    add("double", "cc", ["a3"])
    add("turn", "e0", ["cc"], src="CC", dst="ET", g=None, after=("double",))
    linear("le", q="ET", kv="ET", w_names=("E_q", "E_k", "E_v", "E_m"), needs=["e0", "z1"],
           room=["ff1u"], target=["f5"])
    add("turn", "x2", ["le", "f5"], src="X", dst="XT", g=None, after=("pool affine",))
    norm("n6", "R", ["le"])
    add("affine", "f6", g="E_g1", b="E_b1", dst="CC", plus="CC")
    add("turn", "e1", src="CC", dst="ET", g=None, after=("affine", "f6"))
    feed_forward("ffe", "ET", ["e1"], w1="E_f1", b1=None, w2="E_f2", b2=None, chunks=2, mask=None)
    norm("n7", "R")
    add("affine", "f7", g="E_g2", b="E_b2", dst="CC", plus="CC")
    add("turn", "e2", src="CC", dst="ET", g=None, after=("affine", "f7"))
    linear("ls", q="XT", kv="XT", w_names=("S_q", "S_k", "S_v", "S_m"), needs=["f7", "x2"])
    norm("n8", "R")
    add("affine", "f8", g="D_g0", b="D_b0", dst="X", plus="X")
    add("turn", "d0", src="X", dst="XT", g=None, after=("affine", "f8"))
    linear("lc", q="XT", kv="ET", w_names=("C_q", "C_k", "C_v", "C_m"), needs=["d0", "e2"])
    norm("n9", "R")
    add("affine", "f9", g="D_g1", b="D_b1", dst="X", plus="X")
    add("turn", "d1", src="X", dst="XT", g=None, after=("affine", "f9"))
    feed_forward("ffd", "XT", ["d1"], w1="D_f1", b1=None, w2="D_f2", b2=None, chunks=2, mask=None)
    norm("n10", "R")
    add("affine", "f10", g="D_g2", b="D_b2", dst="X", plus="X")
    norm("n11", "X")
    add("turn", "q3", src="XH", dst="XT", g=("L3_g1", "L3_b1"), after=("norm", "n11"))
    attention("a4", "XT", "XT", ("L3_q", "L3_k", "L3_v"), ("L3_bq", "L3_bk"), None, False, ["q3"])
    norm("n12", "C", ["a4"])
    add("turn", "k3", src="XH", dst="CT", g=("L3_gk", "L3_bkv"), after=("norm", "n12"))
    project("o4", wo="L3_o", bv="L3_bv", bo="L3_bo", acc="X", target=["k3"])
    norm("n13", "X", ["o4", "k3"])
    add("turn", "q4", src="XH", dst="XT", g=("L3_g2", "L3_b2"), after=("norm", "n13"))
    attention("a5", "XT", "CT", ("L3_cq", "L3_ck", "L3_cv"), ("L3_cbq", "L3_cbk"), None, False, ["q4", "k3"])
    project("o5", wo="L3_co", bv="L3_cbv", bo="L3_cbo", acc="X")
    norm("n14", "X")
    add("turn", "h3", src="XH", dst="XT", g=("L3_g3", "L3_b3"), after=("norm", "n14"))
    add("fetch", "fetch0", [f"a5e{GROUPS - 1}/{TILES - 1}"], e=0)
    add("fetch", "fetch1", ["fetch0"], e=1)
    add("logits", "r", ["h3"])
    add("gates", "g")
    add("gates_turn", "gt")
    add("expert_bias", "bias")
    for e in range(EXPERTS + 1):
        if e >= 2:
            add("fetch", f"fetch{e}", [f"mix{e - 2}"], e=e)
        add("expert", f"mix{e}", [f"mix{e - 1}" if e else "bias", f"fetch{e}"], e=e)
    add("store", "store")
    return out


class Step:

    def __init__(self, kind, s, name, p, base, end, own, w):
        self.kind, self.s, self.name, self.base, self.end, self.own, self.w = kind, s, name, base, end, own, w
        self.src, self.dst, self.after, self.plus, self.kv = (p.get(n) for n in ("src", "dst", "after", "plus", "kv"))
        self.acc, self.mask, self.b = p.get("acc"), p.get("mask"), p.get("b")
        self.g, self.k = p.get("g"), p.get("k")
        self.attn, self.lengths, self.bias, self.w_names = (p.get(n) for n in ("attn", "lengths", "bias", "w_names"))
        self.q_from, self.kv_from, self.q = (p.get(n) for n in ("q_from", "kv_from", "q"))
        self.wo, self.bv, self.bo, self.of = p.get("wo"), p.get("bv"), p.get("bo"), p.get("of")
        self.x, self.w1, self.b1, self.w2, self.b2, self.chunks = (
            p.get(n) for n in ("x", "w1", "b1", "w2", "b2", "chunks"))
        self.e = p.get("e")


def plan(streams):
    entries = stream_steps()
    own_time = {name: lasts(kind, p) for kind, name, p, _ in entries}
    followers = {name: [m for _, m, _, needs in entries if name in needs] for name in own_time}
    left = dict(own_time)
    changed = True
    while changed:
        longer = {name: t + max((left[m] for m in followers[name]), default=0) for name, t in own_time.items()}
        changed, left = longer != left, longer
    done, free, unplaced = {}, {}, [list(entries) for _ in range(streams)]
    banks = {"wide": [0, 0], "maxima": [0, 0], "exps": [0]}
    count, steps, by, released, table = {}, [], {}, [], "Exp"
    own = [{} for _ in range(streams)]

    def earliest(s, kind, p, needs):
        t = max((done[s, n] for n in needs), default=0)
        for what, banks_of in banks.items():
            if what == ("exps" if kind == "expert" else kind) or (what == "wide" and uses(kind, p)[1]):
                t = max(t, banks_of[-2] if len(banks_of) > 1 and what != "exps" else banks_of[-1])
        hops = hops_of(kind, p)
        return max(t, free.get(hops[0][0], 0)) if hops else t

    while any(unplaced):
        ready = [(s, e) for s in range(streams) for e in unplaced[s] if all((s, n) in done for n in e[3])]
        starts = {(s, e[1]): earliest(s, e[0], e[2], e[3]) for s, e in ready}
        s, (kind, name, p, needs) = min(ready, key=lambda c: (
            starts[c[0], c[1][1]] - URGENCY * (left[c[1][1]] - LAG * c[0]) - AHEAD.get(c[1][0], 0)))
        unplaced[s] = [e for e in unplaced[s] if e[1] != name]
        t, read = starts[s, name], 0
        for engine, duration in hops_of(kind, p):
            if engine != "WAIT":
                t = max(t, free.get(engine, 0))
            if engine == "ACT" and TABLE_OF.get(kind, table) != table:
                table, t = TABLE_OF[kind], t + TABLE_LOAD
            t += duration
            if engine != "WAIT":
                free[engine] = t
            t += HOP
            if engine not in ("PE", "WAIT") and not read:
                read = t
        done[s, name] = t
        n, wide = uses(kind, p)
        if kind == "maxima":
            banks["maxima"].append(t)
        elif kind in ("exps", "expert"):
            banks["exps"].append(t - 0.8)
        elif wide:
            banks["wide"] += [read or t] * len(wide)
        base = dict(count)
        for what, k in n.items():
            count[what] = count.get(what, 0) + k
        st = Step(kind, s, name, p, base, dict(count), dict(own[s]), len(released))
        own[s] |= {what: count[what] for what in n}
        released += [(what, base.get(what, 0) + k) for what, k in wide]
        steps.append(st)
        by[s, name] = st
    return steps, by, released, sorted(count)


def build(nc, x, ctx, mask0, mask1, mats, expert_mats, cols, rows, fc2_bias, out):
    f32, bf16, i32, u32 = mybir.dt.float32, mybir.dt.bfloat16, mybir.dt.int32, mybir.dt.uint32
    ALU, ACT, AX = mybir.AluOpType, mybir.ActivationFunctionType, mybir.AxisListType
    counted = plan(1)[3]
    x_tok = x.rearrange("n (t p) d -> p n t d", p=128)
    ctx_tok = ctx.rearrange("n (t p) d -> p n t d", p=128)
    out_tok = out.rearrange("n (t p) d -> p n t d", p=128)

    with ExitStack() as stack:
        def sb(name, shape, dt=f32):
            return stack.enter_context(nc.sbuf_tensor(name, shape, dt))

        def psum(name, shape):
            return stack.enter_context(nc.psum_tensor(name, shape, f32))

        def per_stream(name, shape, dt=f32):
            return [sb(f"{name}{s}", shape, dt) for s in range(STREAMS)]

        MAT = sb("MAT", [128, MAT_COLS])
        COL = sb("COL", [128, COL_COLS])
        ROW = sb("ROW", [128, ROW_COLS])
        FC2B = sb("FC2B", [EXPERTS, D])
        identf = sb("identf", [128, 128])
        identb = sb("identb", [128, 128], bf16)
        head_mask = sb("head_mask", [128, HEADS])
        block_mask = sb("block_mask", [128, LHEADS, LHD])
        block_sum = sb("block_sum", [128, LHEADS])
        expert_no = sb("expert_no", [128, EXPERTS])
        key_no = sb("key_no", [HEADS, SEQ])
        minus_half = sb("minus_half", [128, TT])
        no_len = sb("no_len", [HEADS, T], bf16)
        causal_q = sb("causal_q", [128, 128], bf16)
        causal_k = sb("causal_k", [128, 128], bf16)
        mask_any = sb("mask_any", [128, 2, QT])
        mask_q = sb("mask_q", [128, 2, QT, SEQ], bf16)
        mask_k = sb("mask_k", [128, 2, QT, SEQ], bf16)
        row_nan = sb("row_nan", [128, 2, NB, QT])

        X, C, CC, R, OT = (per_stream(n, [128, TT, D]) for n in ("X", "C", "CC", "R", "OT"))
        XT, CT = per_stream("XT", [128, T]), per_stream("CT", [128, T])
        XH, CM, OF, ET, CMT = R, CC, XT, CT, CT
        BN = per_stream("BN", [128, TT, 6])
        MV = per_stream("MV", [128, TT, 2])
        RS = per_stream("RS", [128, TT])
        AM = per_stream("AM", [128, TT])
        M0, M1 = per_stream("M0", [128, TT]), per_stream("M1", [128, TT])
        SQ, SK = per_stream("SQ", [128, HEADS, T], bf16), per_stream("SK", [128, HEADS, T], bf16)
        V_COLS = HEADS * (HD + 1)
        V = per_stream("V", [128, TT, V_COLS + PV_ROWS])
        QF = per_stream("QF", [128, NB, HEADS])
        LEN, LNAN = per_stream("LEN", [HEADS, NB]), per_stream("LNAN", [HEADS, NB])
        NEG = per_stream("NEG", [128, HEADS * TT])
        HL = per_stream("HL", [128, 2, TT, 2 * GROUP], bf16)
        HF = per_stream("HF", [128, TT, GROUP])
        MT = per_stream("MT", [2 * GROUP, 2, T], bf16)
        P = per_stream("P", [128, P_TILES, 2 * 2 * SEQ])
        OG = per_stream("OG", [128, T])
        RC = per_stream("RC", [128, TT, GROUP])
        LZ = per_stream("LZ", [128, 2, LHEADS])
        LG, MX = per_stream("LG", [128, TT, EXPERTS]), per_stream("MX", [128, TT, 8])
        IX, IXF = per_stream("IX", [128, TT, 8], u32), per_stream("IXF", [128, TT, 2])
        GD, GE, GP, GQ = (per_stream(n, [128, TT]) for n in ("GD", "GE", "GP", "GQ"))
        G, G2 = per_stream("G", [128, TT, EXPERTS]), per_stream("G2", [128, TT, EXPERTS])
        room = [P[s][:, :, :].rearrange("p a k -> p (a k)") for s in range(STREAMS)]
        HB = [r[:, 0:8 * T].rearrange("p (a c t) -> p a c t", a=2, c=4) for r in room]
        LM = [r[:, 4 * T:6 * T].rearrange("p (i t) -> p i t", i=2) for r in room]
        LE = [r[:, 6 * T:8 * T].rearrange("p (i t) -> p i t", i=2) for r in room]
        LQ = [r[:, 8 * T:9 * T] for r in room]
        LK = [r[:, 9 * T:10 * T].rearrange("p (t d) -> p t d", d=D) for r in room]
        LV = [r[:, 10 * T:10 * T + TT * (D + 1)].rearrange("p (t d) -> p t d", d=D + 1) for r in room]
        KVB = [r[:, 12 * T - NB * (D + LHEADS):12 * T].rearrange("p (b d) -> p b d", b=NB) for r in room]
        GT = [r[0:EXPERTS, 8 * T:9 * T] for r in room]
        Q32, K32 = [r[:, T:2 * T] for r in room], [r[:, 2 * T:3 * T] for r in room]
        Q3, K3 = ([r[:, at:at + 3 * T // 2].bitcast(bf16).rearrange("p (i t) -> p i t", i=3) for r in room]
                  for at in (5 * T, 13 * T // 2))
        KR = [r[:, 4 * T:5 * T] for r in room]
        LB = [r[0:HEADS, 3 * T:4 * T].bitcast(bf16)[:, 0:T] for r in room]
        NZ = [r[0:HEADS, 0:T].rearrange("p (b k) -> p b k", b=NB) for r in room]
        expert_room = [SQ[s][:, :, :].rearrange("p h t -> p (h t)").bitcast(f32)[:, 0:4 * DFF].rearrange(
            "p (m e k) -> p m e k", m=2, e=2) for s in range(STREAMS)]
        mask_in = room[0][:, 0:2 * QT * SEQ].rearrange("p (m k) -> p m k", m=2).bitcast(i32)
        mask_vis = room[0][:, 2 * QT * SEQ:4 * QT * SEQ].rearrange("p (m k) -> p m k", m=2)

        SA = [psum(f"SA{i}", [128, 4 * SEQ]) for i in range(2)]
        ST = [psum(f"ST{i}", [128, 2 * SEQ]) for i in range(2)]
        W = [psum(f"W{i}", [128, 512]) for i in range(2)]

        consts_loaded = nc.alloc_semaphore("consts_loaded")
        pool_consts = nc.alloc_semaphore("pool_consts")
        dve_consts = nc.alloc_semaphore("dve_consts")
        mask_turned = nc.alloc_semaphore("mask_turned")
        mask_copied = nc.alloc_semaphore("mask_copied")
        mats_loaded = [nc.alloc_semaphore(f"mats_loaded{i}") for i in range(len(MATS))]
        sem = {n: nc.alloc_semaphore(n) for n in counted}
        wide_full = nc.alloc_semaphore("wide_full")
        tile_full = nc.alloc_semaphore("tile_full")
        prob_full = nc.alloc_semaphore("prob_full")
        dve_chain = nc.alloc_semaphore("dve_chain")
        pool_chain = nc.alloc_semaphore("pool_chain")
        fetched = [[nc.alloc_semaphore(f"fetched{s}_{i}") for i in range(2)] for s in range(STREAMS)]
        loaded = [nc.alloc_semaphore(f"loaded{s}") for s in range(STREAMS)]
        stacked = [nc.alloc_semaphore(f"stacked{s}") for s in range(STREAMS)]
        neg_row = [[nc.alloc_semaphore(f"neg_row{s}_{i}") for i in range(2)] for s in range(STREAMS)]
        stored = nc.alloc_semaphore("stored")
        of_round = [*sem.values(), wide_full, tile_full, prob_full, dve_chain, pool_chain, *loaded, *stacked,
                    *(h for pair in (*neg_row, *fetched) for h in pair), stored]
        numbers = [h.num for h in of_round]
        assert sorted(numbers) == list(range(min(numbers), max(numbers) + 1))

        def mat(name, chunk=0, width=None):
            at, n = MAT_AT[name]
            width = width or n
            return MAT[:, at + chunk * width:at + (chunk + 1) * width]

        def col(name, i=0):
            at = COL_AT[name][0] + i
            return COL[:, at:at + 1]

        def row(name):
            at, n = ROW_AT[name]
            return ROW[:, at:at + n].unsqueeze(1).to_broadcast([128, TT, n])

        def probs(g, pair, first, n):
            at = (pair % 2) * 2 * SEQ + first
            return (g * TILES + pair // 2) % P_TILES, slice(at, at + n)

        def attention_no(st, name):
            return int(name[1:])

        def stack_dmas(st):
            upto = range(attention_no(st, st.attn) + 1)
            return 12 * len(upto) + sum(f"a{n}" in (*WITH_LENGTHS, CLEARS_LENGTHS) for n in upto)

        def pairs(ap):
            return ap.rearrange("p h t -> p (h t)").bitcast(f32)

        with nc.Block() as block:
            @block.sync
            def _(sp):
                sp.dma_start(COL[:, :], cols).then_inc(consts_loaded, 16)
                sp.dma_start(mask_in[:, 0, :].rearrange("p (t k) -> p t k", t=QT),
                             mask0.rearrange("(t p) k -> p t k", p=128)).then_inc(consts_loaded, 16)
                sp.dma_start(mask_in[:, 1, :].rearrange("p (t k) -> p t k", t=QT),
                             mask1.rearrange("(t p) k -> p t k", p=128)).then_inc(consts_loaded, 16)
                sp.dma_start(ROW[:, :], rows.partition_broadcast(128)).then_inc(consts_loaded, 16)
                sp.dma_start(FC2B[:, :], fc2_bias).then_inc(consts_loaded, 16)
                for i, end in enumerate(PART_ENDS):
                    at = PART_ENDS[i - 1] if i else 0
                    sp.dma_start(MAT[:, at:end], mats[:, at:end]).then_inc(mats_loaded[i], 16)
                sp.wait_ge(consts_loaded, 80)

            @block.gpsimd
            def _(pool):
                made = [0]

                def link(ins):
                    made[0] += 1
                    ins.then_inc(pool_consts, 1)
                    pool.wait_ge(pool_consts, made[0])

                def select(dst, pattern, op, fill, base, per_partition):
                    link(pool.affine_select(out=dst, in_=dst, pattern=pattern, compare_op=op, fill=fill, base=base,
                                            channel_multiplier=per_partition))

                for t in (identf, identb):
                    link(pool.memset(t[:, :], 0.0))
                    select(t[:, :], [[-1, 128]], ALU.not_equal, 1.0, 0, 1)
                for t, shape in ((block_mask[:, :, :], [[-LHD, LHEADS], [0, LHD]]), (block_sum[:, :], [[-LHD, LHEADS]])):
                    link(pool.memset(t, 1.0))
                    select(t, shape, ALU.is_ge, 0.0, 0, 1)
                    select(t, [[LHD if s else 0, n] for s, n in shape], ALU.is_ge, 0.0, LHD - 1, -1)
                link(pool.memset(causal_q[:, :], 0.0))
                select(causal_q[:, :], [[-1, 128]], ALU.is_ge, MASKED, 0, 1)
                link(pool.memset(causal_k[:, :], 0.0))
                select(causal_k[:, :], [[1, 128]], ALU.is_ge, MASKED, 0, -1)
                link(pool.iota(mask_vis[:, 0, 0:EXPERTS].bitcast(i32), pattern=[[1, EXPERTS]], base=0,
                               channel_multiplier=0))
                link(pool.iota(mask_vis[0:HEADS, 1, 0:SEQ].bitcast(i32), pattern=[[1, SEQ]], base=0,
                               channel_multiplier=0))
                link(pool.tensor_copy(expert_no[:, :], mask_vis[:, 0, 0:EXPERTS].bitcast(i32)))
                link(pool.tensor_copy(key_no[:, :], mask_vis[0:HEADS, 1, 0:SEQ].bitcast(i32)))
                pool.sem_inc(pool_consts, 100)
                made[0] += 100
                for s in range(1, STREAMS, 2):
                    link(pool.memset(pairs(SK[s][:, :, :]), 0.0))
                    link(pool.memset(pairs(SK[s][MAX_ROW:MAX_ROW + 2, :, :]), TWO_ONES))

            @block.vector
            def _(dve):
                made = [0]

                def link(ins):
                    made[0] += 1
                    ins.then_inc(dve_consts, 1)
                    dve.wait_ge(dve_consts, made[0])

                for s in range(STREAMS):
                    if s % 2 == 0:
                        dve.memset(pairs(SK[s][:, :, :]), 0.0)
                    dve.memset(V[s][:, :, :], 0.0)
                dve.memset(no_len[:, :], 0.0)
                link(dve.memset(minus_half[:, :], -0.5))
                for s in range(STREAMS):
                    if s % 2 == 0:
                        dve.memset(pairs(SK[s][MAX_ROW:MAX_ROW + 2, :, :]), TWO_ONES)
                    dve.memset(V[s][:, :, 0:V_COLS].rearrange("p t (h d) -> p t h d", d=HD + 1)[:, :, :, HD:HD + 1], 1.0)
                dve.wait_ge(pool_consts, 100)
                dve.tensor_reduce(head_mask[:, :], identf[:, :].rearrange("p (d h) -> p h d", h=HEADS), AX.X, ALU.add)
                dve.wait_ge(consts_loaded, 80)
                dve.tensor_scalar(mask_q[:, :, :, :].rearrange("p m t k -> p m (t k)"), mask_in[:, :, :], 0.0, MASKED,
                                  ALU.is_equal, ALU.mult)
                link(dve.tensor_scalar(mask_vis[:, :, :], mask_in[:, :, :], 0.0, None, ALU.not_equal))
                link(dve.tensor_reduce(mask_any[:, :, :], mask_vis[:, :, :].rearrange("p m (t k) -> p m t k", t=QT),
                                       AX.X, ALU.max))
                for b in range(NB):
                    link(dve.tensor_scalar(row_nan[:, :, b, :], mask_any[:, :, :], 0.0, HUGE, ALU.is_equal, ALU.mult))
                    link(dve.tensor_scalar(row_nan[:, :, b, :], row_nan[:, :, b, :], HUGE, 0.0, ALU.mult, ALU.mult))
                link(dve.memset(LZ[0][:, :, :], 0.0))
                dve.sem_inc(dve_consts, 100)
                for m in range(2):
                    dve.wait_ge(mask_turned, m + 1)
                    dve.tensor_copy(mask_k[:, m, :, :].rearrange("p t k -> p (t k)"), W[m][:, :].bitcast(bf16)[:, 0:QT * SEQ]) \
                       .then_inc(mask_copied, 1)
                dve.wait_ge(mask_copied, 2)

            @block.tensor
            def _(pe):
                pe.wait_ge(dve_consts, 100)
                for m in range(2):
                    for kt in range(QT):
                        for qt in range(QT):
                            at = kt * SEQ + qt * 128
                            last = pe.transpose(W[m][:, :].bitcast(bf16)[:, at:at + 128],
                                                mask_q[:, m, qt, kt * 128:(kt + 1) * 128], identb[:, :])
                    last.then_inc(mask_turned, 1)

        def a_round(first_batch, streams):
            steps, by, released, _ = plan(streams)
            with nc.Block() as block:
                @block.sync
                def _(sp):
                    stacks = [0] * STREAMS

                    def load(st):
                        first = first_batch + st.s * NB
                        sp.dma_start(X[st.s][:, :, :].rearrange("p (n t) d -> p n t d", n=NB),
                                     x_tok[:, bass.ds(first, NB), :, :]).then_inc(loaded[st.s], 16)
                        sp.dma_start(C[st.s][:, :, :].rearrange("p (n t) d -> p n t d", n=NB),
                                     ctx_tok[:, bass.ds(first, NB), :, :]).then_inc(loaded[st.s], 16)

                    def qkv(st):
                        s = st.s
                        if st.name == "a0":
                            sp.wait_ge(sem["restored"], st.own["restored"])
                        for stack, parts, part, what, at in (
                                (SQ, Q3, 0, "q_one", (0, 1, 2)), (SK, K3, 0, "k_one", (0, 3, 5)),
                                (SQ, Q3, 1, "q_two", (3, 4)), (SQ, Q3, 2, "q_three", (5,)),
                                (SK, K3, 1, "k_two", (1, 4)), (SK, K3, 2, "k_three", (2,))):
                            sp.wait_ge(sem[what], st.end[what])
                            for r in at:
                                sp.dma_start(stack[s][HD * r:HD * r + HD, :, :], parts[s][:, part, :]) \
                                  .then_inc(stacked[s], 16)
                        if st.name == CLEARS_LENGTHS:
                            sp.dma_start(SK[s][LEN_ROW:LEN_ROW + 1, :, :], no_len[:, :]).then_inc(stacked[s], 16)

                    def lengths(st):
                        sp.wait_ge(sem["len_row"], st.end["len_row"])
                        sp.dma_start(SK[st.s][LEN_ROW:LEN_ROW + 1, :, :], LB[st.s][:, :]).then_inc(stacked[st.s], 16)

                    def fetch(st):
                        s, e = st.s, st.e
                        if e < 2:
                            sp.wait_ge(sem["prob"], by[s, f"a5e{GROUPS - 1}/{TILES - 1}"].end["prob"])
                        elif e == 2:
                            sp.wait_ge(sem["prob"], by[s, "mix0"].end["prob"])
                        else:
                            sp.wait_ge(sem["expert_mixed"], by[s, f"mix{e - 2}"].end["expert_mixed"])
                        for m, n in ((0, e), (1, e - 1)):
                            if 0 <= n < EXPERTS:
                                sp.dma_start(expert_room[s][:, m, n % 2, :], expert_mats[:, m, n, :]) \
                                  .then_inc(fetched[s][e % 2], 16)

                    def store(st):
                        sp.wait_ge(sem["expert_mixed"], st.own["expert_mixed"])
                        first = first_batch + st.s * NB
                        sp.dma_start(out_tok[:, bass.ds(first, NB), :, :],
                                     X[st.s][:, :, :].rearrange("p (n t) d -> p n t d", n=NB)).then_inc(stored, 16)

                    for st in steps:
                        if st.kind in ("load", "qkv", "lengths", "fetch", "store"):
                            {"load": load, "qkv": qkv, "lengths": lengths, "fetch": fetch, "store": store}[st.kind](st)
                    sp.wait_ge(stored, 16 * streams)

                @block.tensor
                def _(pe):
                    def wide(w):
                        if w >= 2:
                            what, value = released[w - 2]
                            pe.wait_ge(sem[what], value)
                        return W[w % 2]

                    def turn(st):
                        s = st.s
                        src = {"X": X, "C": C, "CC": CC, "CM": CM, "XH": XH}[st.src][s]
                        kind = st.after[0]
                        if kind == "load":
                            pe.wait_ge(loaded[s], 32)
                        elif kind == "double":
                            pe.wait_ge(sem["doubled"], st.own["doubled"])
                        elif kind == "pool affine":
                            pe.wait_ge(sem["affined"], st.own["affined"])
                        elif kind == "norm":
                            pe.wait_ge(sem["normed"], st.own["normed"])
                        elif kind == "affine":
                            pe.wait_ge(sem["summed"], st.own["summed"])
                        else:
                            pe.wait_ge(sem["row_kept"], st.own["row_kept"])
                        w = wide(st.w)
                        for t in range(TT):
                            last = pe.transpose(w[:, t * 128:(t + 1) * 128], src[:, t, :], identf[:, :])
                        last.then_inc(wide_full, 1)

                    def qkv(st):
                        s = st.s
                        xq, xk = ({"XT": XT, "CT": CT, "CMT": CMT}[n][s] for n in (st.q_from, st.kv_from))
                        pe.wait_ge(sem["turned"], st.own["turned"])
                        pe.wait_ge(mats_loaded[PART_OF[st.w_names[0]]], 16)
                        pe.matmul(wide(st.w)[:, 0:T], mat(st.w_names[0]), xq[:, :], start=True, stop=True) \
                          .then_inc(wide_full, 1)
                        pe.matmul(wide(st.w + 1)[:, 0:T], mat(st.w_names[1]), xk[:, :], start=True, stop=True) \
                          .then_inc(wide_full, 1)
                        w = wide(st.w + 2)
                        for t in range(TT):
                            last = pe.matmul(w[:, t * 128:(t + 1) * 128], xk[:, t * 128:(t + 1) * 128],
                                             mat(st.w_names[2]), start=True, stop=True)
                        last.then_inc(wide_full, 1)

                    def lengths(st):
                        s = st.s
                        pe.wait_ge(sem["q_first"], st.own["q_first"])
                        pe.wait_ge(sem["k_read"], st.own["k_read"])
                        w = wide(st.w)
                        for b in range(NB):
                            last = pe.matmul(w[0:HEADS, b * SEQ:(b + 1) * SEQ], QF[s][:, b, :],
                                             K32[s][:, b * SEQ:(b + 1) * SEQ], start=True, stop=True)
                        last.then_inc(wide_full, 1)

                    def maxima(st):
                        s, k, n = st.s, st.k, st.base.get("stile", 0)
                        if st.g == 0 and k == 0:
                            pe.wait_ge(stacked[s], 16 * stack_dmas(st))
                        if n >= 2:
                            pe.wait_ge(sem["stile"], n - 1)
                        for j in range(2):
                            pair = st.g * PAIRS + 2 * k + j
                            h, b = pair // NB, pair % NB
                            bank = SA[n % 2][:, j * 2 * SEQ:(j + 1) * 2 * SEQ]
                            for qt in range(QT):
                                keys = (qt + 1) * 128 if st.mask == "causal" else SEQ
                                lhs = SQ[s][0:MAX_ROW, h, b * SEQ + qt * 128:b * SEQ + (qt + 1) * 128]
                                rhs = SK[s][0:MAX_ROW, h, b * SEQ:b * SEQ + keys]
                                at = qt * SEQ
                                if st.mask == "causal":
                                    last = pe.matmul(bank[:, at:at + keys], lhs, rhs, start=True, stop=False,
                                                     skip_group_check=True)
                                    last = pe.matmul(bank[:, at + keys - 128:at + keys], identb[:, :], causal_q[:, :],
                                                     start=False, stop=True, skip_group_check=True)
                                elif st.mask is None:
                                    last = pe.matmul(bank[:, at:at + keys], lhs, rhs, start=True, stop=True)
                                else:
                                    if qt == 0:
                                        pe.matmul(bank, identb[:, :], mask_q[:, st.mask, :, :].rearrange(
                                            "p t k -> p (t k)"), start=True, stop=False, skip_group_check=True)
                                    last = pe.matmul(bank[:, at:at + keys], lhs, rhs, start=False, stop=True,
                                                     skip_group_check=True)
                        last.then_inc(tile_full, 1)

                    def exp_scores(st, i):
                        s, g, n = st.s, st.g, st.base.get("prob", 0) + i
                        if n >= 2:
                            pe.wait_ge(sem["prob"], n - 1)
                        pair = g * PAIRS + 2 * st.k + i
                        h, b = pair // NB, pair % NB
                        bank = ST[n % 2]
                        for kt in range(QT):
                            lhs = SK[s][:, h, b * SEQ + kt * 128:b * SEQ + (kt + 1) * 128]
                            first = kt * 128 if st.mask == "causal" else 0
                            at = kt * SEQ
                            rhs = SQ[s][:, h, b * SEQ + first:(b + 1) * SEQ]
                            n_q = SEQ - first
                            if st.mask == "causal":
                                pe.matmul(bank[:, at:at + n_q], lhs, rhs, start=True, stop=False,
                                          skip_group_check=True)
                                last = pe.matmul(bank[:, at:at + 128], identb[:, :], causal_k[:, :], start=False,
                                                 stop=True, skip_group_check=True)
                            elif st.mask is None:
                                last = pe.matmul(bank[:, at:at + n_q], lhs, rhs, start=True, stop=True)
                            else:
                                if kt == 0:
                                    pe.matmul(bank[:, :], identb[:, :], mask_k[:, st.mask, :, :].rearrange(
                                        "p t k -> p (t k)"), start=True, stop=False, skip_group_check=True)
                                last = pe.matmul(bank[:, at:at + n_q], lhs, rhs, start=False, stop=True,
                                                 skip_group_check=True)
                        last.then_inc(prob_full, 1)

                    def exps(st):
                        s, g = st.s, st.g
                        if st.k == 0:
                            pe.wait_ge(neg_row[s][g % 2], 16 * (attention_no(st, st.attn) * GROUPS // 2 + g // 2 + 1))
                        exp_scores(st, 0)
                        exp_scores(st, 1)

                    def negatives(st):
                        pe.wait_ge(sem["neg_parts"], by[st.s, f"{st.attn}s{st.g}"].end["neg_parts"])
                        bank = wide(st.w)[:, :].bitcast(bf16)
                        for t in range(TT):
                            last = pe.transpose(bank[0:2 * GROUP, t * 128:(t + 1) * 128],
                                                HL[st.s][:, st.g % 2, t, :], identb[:, :])
                        last.then_inc(wide_full, 1)

                    def out_rows(st):
                        s, g = st.s, st.g
                        pe.wait_ge(sem["out_copied"], by[s, f"{st.attn}v{g}"].end["out_copied"])
                        bank = wide(st.w)
                        for t in range(TT):
                            last = pe.transpose(bank[:, t * 128:(t + 1) * 128],
                                                OG[s][:, t * 128:(t + 1) * 128], identf[:, :])
                        last.then_inc(wide_full, 1)

                    def values(st):
                        s, g = st.s, st.g
                        pe.wait_ge(sem["prob"], by[s, f"{st.attn}e{g}/{TILES - 1}"].end["prob"])
                        pe.wait_ge(sem["v_ready"], st.own["v_ready"])
                        bank = wide(st.w)
                        for b in range(NB):
                            for kt in range(QT):
                                first = kt * 128 if st.mask == "causal" else 0
                                for j in range(GROUP):
                                    last = pe.matmul(
                                        bank[32 * j:32 * j + 32, b * SEQ + first:(b + 1) * SEQ],
                                        V[s][:, b * QT + kt, (GROUP * g + j) * (HD + 1):
                                             (GROUP * g + j) * (HD + 1) + PV_ROWS],
                                        P[s][:, *probs(g, j * NB + b, kt * SEQ, SEQ - first)],
                                        start=(kt == 0), stop=(kt == QT - 1), skip_group_check=True)
                        last.then_inc(wide_full, 1)

                    def turn_rows(w, src):
                        bank = wide(w)
                        for t in range(TT):
                            last = pe.transpose(bank[:, t * 128:(t + 1) * 128], src[:, t, :], identf[:, :])
                        last.then_inc(wide_full, 1)

                    def times(w, left, right):
                        bank = wide(w)
                        for t in range(TT):
                            last = pe.matmul(bank[:, t * 128:(t + 1) * 128], left[:, t * 128:(t + 1) * 128], right,
                                             start=True, stop=True)
                        last.then_inc(wide_full, 1)

                    def out_turn(st):
                        pe.wait_ge(sem[st.of], st.own[st.of])
                        turn_rows(st.w, OT[st.s])

                    def out_product(st):
                        pe.wait_ge(sem["turned"], st.own["turned"])
                        times(st.w, OF[st.s], mat(st.wo))

                    def product_down(w, s, half, chunks, weight):
                        bank = wide(w)
                        for t in range(TT):
                            for c in range(chunks):
                                last = pe.matmul(bank[:, t * 128:(t + 1) * 128],
                                                 HB[s][:, half, c, t * 128:(t + 1) * 128], weight(c),
                                                 start=(c == 0), stop=(c == chunks - 1))
                        last.then_inc(wide_full, 1)

                    def up(st):
                        src = {"XT": XT, "ET": ET}[st.x][st.s]
                        pe.wait_ge(sem["turned"], st.own["turned"])
                        pe.wait_ge(mats_loaded[PART_OF[st.w1]], 16)
                        for c in range(st.chunks):
                            pe.matmul(wide(st.w + c)[:, 0:T], mat(st.w1, c, 128), src[:, :], start=True, stop=True) \
                              .then_inc(wide_full, 1)

                    def down(st):
                        pe.wait_ge(sem["hidden"], st.own["hidden"])
                        product_down(st.w, st.s, 0, st.chunks, lambda c: mat(st.w2, c, 128))

                    def lin_qkv(st):
                        s, w = st.s, st.w
                        xq, xk = ({"XT": XT, "ET": ET}[n][s] for n in (st.q, st.kv))
                        pe.wait_ge(sem["turned"], st.own["turned"])
                        pe.wait_ge(mats_loaded[PART_OF[st.w_names[0]]], 16)
                        times(w, xk, mat(st.w_names[2]))
                        pe.matmul(wide(w + 1)[:, 0:T], mat(st.w_names[0]), xq[:, :], start=True, stop=True) \
                          .then_inc(wide_full, 1)
                        times(w + 2, xk, mat(st.w_names[1]))

                    def lin_kv(st):
                        s = st.s
                        pe.wait_ge(sem["lin_feature"], st.own["lin_feature"])
                        pe.wait_ge(sem["lin_v"], st.own["lin_v"])
                        for b in range(NB):
                            bank = wide(st.w + b)
                            for qt in range(QT):
                                last = pe.matmul(bank[:, 0:D + 1], LK[s][:, b * QT + qt, :], LV[s][:, b * QT + qt, :],
                                                 start=(qt == 0), stop=(qt == QT - 1))
                            last.then_inc(wide_full, 1)

                    def lin_out(st):
                        s = st.s
                        for b in range(NB):
                            pe.wait_ge(sem["lin_kv"], st.own["lin_kv"] - NB + b + 1)
                            bank = wide(st.w + b)
                            for qt in range(QT):
                                at = (b * QT + qt) * 128
                                last = pe.matmul(bank[:, qt * (D + LHEADS):(qt + 1) * (D + LHEADS)],
                                                 LQ[s][:, at:at + 128], KVB[s][:, b, :], start=True, stop=True)
                            last.then_inc(wide_full, 1)

                    def logits(st):
                        s = st.s
                        pe.wait_ge(sem["turned"], st.own["turned"])
                        bank = wide(st.w)
                        for t in range(TT):
                            last = pe.matmul(bank[:, t * EXPERTS:(t + 1) * EXPERTS], XT[s][:, t * 128:(t + 1) * 128],
                                             mat("L3_r"), start=True, stop=True)
                        last.then_inc(wide_full, 1)

                    def gates_turn(st):
                        s = st.s
                        pe.wait_ge(sem["gates"], st.own["gates"])
                        bank = wide(st.w)
                        for t in range(TT):
                            last = pe.transpose(bank[0:EXPERTS, t * 128:(t + 1) * 128], G[s][:, t, :], identf[:, :])
                        last.then_inc(wide_full, 1)

                    def expert_bias(st):
                        s = st.s
                        pe.wait_ge(sem["gates_turned"], st.own["gates_turned"])
                        bank = wide(st.w)
                        for t in range(TT):
                            last = pe.matmul(bank[:, t * 128:(t + 1) * 128], GT[s][:, t * 128:(t + 1) * 128],
                                             FC2B[:, :], start=True, stop=True)
                        last.then_inc(wide_full, 1)

                    def expert(st):
                        s, w, e = st.s, st.w, st.e
                        pe.wait_ge(fetched[s][e % 2], 16 * sum((n < EXPERTS) + (n >= 1) for n in range(e % 2, e + 1, 2)))
                        if e >= 1:
                            pe.wait_ge(sem["prob"], st.own["prob"])
                            bank = wide(w)
                        for c in range(CHUNKS):
                            if e < EXPERTS:
                                n = st.base["prob"] + c
                                pe.wait_ge(sem["prob"], n - 1)
                                pe.matmul(ST[n % 2][:, 0:T], expert_room[s][:, 0, e % 2, c * 128:(c + 1) * 128], XT[s][:, :],
                                          start=True, stop=True).then_inc(prob_full, 1)
                            if e >= 1:
                                for i in range(c * TT, (c + 1) * TT):
                                    t, d = i // CHUNKS, i % CHUNKS
                                    last = pe.matmul(bank[:, t * 128:(t + 1) * 128],
                                                     HB[s][:, (e - 1) % 2, d, t * 128:(t + 1) * 128],
                                                     expert_room[s][:, 1, (e - 1) % 2, d * 128:(d + 1) * 128],
                                                     start=(d == 0), stop=(d == CHUNKS - 1), skip_group_check=True)
                        if e >= 1:
                            last.then_inc(wide_full, 1)

                    kinds = {"turn": turn, "qkv": qkv, "lengths": lengths, "maxima": maxima,
                             "negatives": negatives, "exps": exps, "values": values, "out_rows": out_rows,
                             "out_turn": out_turn,
                             "out_product": out_product, "up": up, "down": down, "lin_qkv": lin_qkv, "lin_kv": lin_kv,
                             "lin_out": lin_out, "logits": logits, "gates_turn": gates_turn, "expert_bias": expert_bias,
                             "expert": expert}
                    for st in steps:
                        if st.kind in kinds:
                            kinds[st.kind](st)

                @block.scalar
                def _(act):
                    def wide(w):
                        act.wait_ge(wide_full, w + 1)
                        return W[w % 2]

                    def turn(st):
                        dst = {"XT": XT, "CT": CT, "CMT": CMT, "ET": ET}[st.dst][st.s]
                        w = wide(st.w)
                        if st.g:
                            act.activation(dst[:, :], w[:, 0:T], ACT.Identity, bias=col(st.g[1]), scale=col(st.g[0])) \
                               .then_inc(sem["turned"], 1)
                        else:
                            act.activation(dst[:, :], w[:, 0:T], ACT.Copy).then_inc(sem["turned"], 1)

                    def qkv(st):
                        s = st.s
                        w = wide(st.w + 2)
                        for t in range(TT):
                            ins = act.activation(
                                V[s][:, t, 0:V_COLS].rearrange("p (h d) -> p h d", d=HD + 1)[:, :, 0:HD],
                                w[:, t * 128:(t + 1) * 128].rearrange("p (h d) -> p h d", d=HD), ACT.Copy)
                        ins.then_inc(sem["v_ready"], 1)

                    def exps(st):
                        s, g = st.s, st.g
                        for i in range(2):
                            n = st.base.get("prob", 0) + i
                            used = 2 * SEQ - (128 if st.mask == "causal" else 0)
                            act.wait_ge(prob_full, n + 1)
                            act.activation(P[s][:, *probs(g, 2 * st.k + i, 0, used)], ST[n % 2][:, 0:used], ACT.Exp) \
                               .then_inc(sem["prob"], 1)

                    def negatives(st):
                        s, g = st.s, st.g
                        bank = wide(st.w)[:, :].bitcast(bf16)
                        act.activation(MT[s][:, g % 2, :], bank[0:2 * GROUP, 0:T], ACT.Copy) \
                           .then_inc(sem["neg_turned"], 1)
                        act.wait_ge(sem["neg_turned"], st.end["neg_turned"])
                        act.dma_start(SQ[s][MAX_ROW:MAX_ROW + 2, GROUP * g:GROUP * (g + 1), :], MT[s][:, g % 2, :]) \
                           .then_inc(neg_row[s][g % 2], 16)

                    def values(st):
                        act.activation(OG[st.s][:, :], wide(st.w)[:, 0:T], ACT.Copy) \
                           .then_inc(sem["out_copied"], 1)

                    def out_turn(st):
                        if st.bv:
                            act.activation(OF[st.s][:, :], wide(st.w)[:, 0:T], ACT.Identity, bias=col(st.bv)) \
                               .then_inc(sem["turned"], 1)
                        else:
                            act.activation(OF[st.s][:, :], wide(st.w)[:, 0:T], ACT.Copy).then_inc(sem["turned"], 1)

                    def up(st):
                        for c in range(st.chunks):
                            w = wide(st.w + c)
                            dst = HB[st.s][:, 0, c, :]
                            if st.b1:
                                act.activation(dst, w[:, 0:T], ACT.Relu, bias=col(st.b1, c)).then_inc(sem["hidden"], 1)
                            else:
                                act.activation(dst, w[:, 0:T], ACT.Relu).then_inc(sem["hidden"], 1)

                    def lin_qkv(st):
                        s = st.s
                        act.activation(LV[s][:, :, 0:D], wide(st.w)[:, 0:TT * 128].rearrange(
                            "p (t d) -> p t d", d=D), ACT.Copy).then_inc(sem["lin_v"], 1)
                        for i in range(2):
                            act.wait_ge(sem["lin_min"], st.base.get("lin_min", 0) + i + 1)
                            act.activation(LE[s][:, i, :], LM[s][:, i, :], ACT.Exp).then_inc(sem["lin_exp"], 1)

                    def logits(st):
                        s = st.s
                        act.wait_ge(sem["gate_diff"], st.end["gate_diff"])
                        act.activation(GE[s][:, :], GD[s][:, :], ACT.Exp).then_inc(sem["gate_exp"], 1)

                    def gates_turn(st):
                        act.activation(GT[st.s][:, :], wide(st.w)[0:EXPERTS, 0:T], ACT.Copy) \
                           .then_inc(sem["gates_turned"], 1)

                    def expert(st):
                        if st.e < EXPERTS:
                            for c in range(CHUNKS):
                                n = st.base["prob"] + c
                                act.wait_ge(prob_full, n + 1)
                                act.activation(HB[st.s][:, st.e % 2, c, :], ST[n % 2][:, 0:T], ACT.Gelu,
                                               bias=col("M_fb1", st.e * CHUNKS + c)).then_inc(sem["prob"], 1)

                    kinds = {"turn": turn, "qkv": qkv, "exps": exps, "negatives": negatives, "values": values,
                             "out_turn": out_turn, "up": up,
                             "lin_qkv": lin_qkv, "logits": logits, "gates_turn": gates_turn,
                             "expert": expert}
                    for st in steps:
                        if st.kind in kinds:
                            kinds[st.kind](st)

                @block.gpsimd
                def _(pool):
                    chain = [0]

                    def link(ins):
                        chain[0] += 1
                        ins.then_inc(pool_chain, 1)
                        pool.wait_ge(pool_chain, chain[0])

                    def stats(st):
                        s = st.s
                        pool.wait_ge(sem["variance"], st.end["variance"])
                        link(pool.tensor_scalar(RS[s][:, :], MV[s][:, :, 1], EPS, None, ALU.add))
                        pool.tensor_tensor(RS[s][:, :], RS[s][:, :], minus_half[:, :], ALU.pow) \
                            .then_inc(sem["rstd"], 1)

                    def affine(st):
                        if st.plus:
                            return
                        s = st.s
                        pool.wait_ge(sem["normed"], st.own["normed"])
                        link(pool.tensor_tensor(X[s][:, :, :], XH[s][:, :, :], row(st.g), ALU.mult))
                        pool.tensor_tensor(X[s][:, :, :], X[s][:, :, :], row(st.b), ALU.add) \
                            .then_inc(sem["affined"], 1)

                    def restore(st):
                        rows = SQ[st.s][:, :, :].rearrange("p h t -> p (h t)").bitcast(f32)
                        link(pool.memset(rows, 0.0))
                        pool.memset(rows[LEN_ROW:LEN_ROW + 1, :], TWO_ONES).then_inc(sem["restored"], 1)
                        pool.wait_ge(sem["restored"], st.end["restored"])

                    def qkv(st):
                        s = st.s
                        pool.wait_ge(sem["k_one"], st.end["k_one"])
                        link(pool.tensor_tensor(KR[s][:, :], K32[s][:, :], K3[s][:, 0, :], ALU.subtract))
                        pool.tensor_scalar(K3[s][:, 1, :], KR[s][:, :], 1.0, None, ALU.mult) \
                            .then_inc(sem["k_two"], 1)
                        pool.wait_ge(sem["k_two"], st.end["k_two"])
                        pool.tensor_tensor(K3[s][:, 2, :], KR[s][:, :], K3[s][:, 1, :], ALU.subtract) \
                            .then_inc(sem["k_three"], 1)

                    def neg_split(st):
                        s, g = st.s, st.g
                        pool.wait_ge(sem["stile"], by[s, f"{st.attn}m{g}/{TILES - 1}"].end["stile"])
                        neg = NEG[s][:, g * PAIRS * QT:(g + 1) * PAIRS * QT].rearrange("p (h t) -> p t h", t=TT)
                        src = neg
                        if st.mask in (0, 1):
                            if st.own.get("neg_parts"):
                                pool.wait_ge(sem["neg_parts"], st.own["neg_parts"])
                            src = HF[s][:, :, :]
                            nan = row_nan[:, st.mask, :, :].rearrange("p b t -> p (b t)")
                            link(pool.tensor_tensor(src, neg, nan.unsqueeze(2).to_broadcast([128, TT, GROUP]), ALU.add))
                        high, low = HL[s][:, g % 2, :, 0:GROUP], HL[s][:, g % 2, :, GROUP:2 * GROUP]
                        link(pool.tensor_scalar(high, src, 1.0, None, ALU.mult))
                        pool.tensor_tensor(low, src, high, ALU.subtract).then_inc(sem["neg_parts"], 1)

                    kinds = {"stats": stats, "affine": affine, "restore": restore, "qkv": qkv, "neg_split": neg_split}
                    for st in steps:
                        if st.kind in kinds:
                            kinds[st.kind](st)

                @block.vector
                def _(dve):
                    chain = [0]

                    def link(ins):
                        chain[0] += 1
                        ins.then_inc(dve_chain, 1)
                        dve.wait_ge(dve_chain, chain[0])

                    def own(st, *names):
                        for n in names:
                            if st.own.get(n, 0):
                                dve.wait_ge(sem[n], st.own[n])

                    def wide(w):
                        dve.wait_ge(wide_full, w + 1)
                        return W[w % 2]

                    def tokens(bank):
                        return bank[:, 0:TT * 128].rearrange("p (t d) -> p t d", d=128)

                    def double(st):
                        dve.wait_ge(loaded[st.s], 32)
                        dve.tensor_tensor(CC[st.s][:, :, :], C[st.s][:, :, :], C[st.s][:, :, :], ALU.add) \
                           .then_inc(sem["doubled"], 1)

                    def stats(st):
                        s = st.s
                        src = {"R": R, "X": X, "C": C}[st.src][s]
                        own(st, "residual", "summed")
                        for t in range(TT):
                            ins = dve.bn_stats(BN[s][:, t, :], src[:, t, :])
                        link(ins)
                        for t in range(TT):
                            ins = dve.bn_aggr(MV[s][:, t, :], BN[s][:, t, :])
                        ins.then_inc(sem["variance"], 1)

                    def normalise(st):
                        s = st.s
                        src = {"R": R, "X": X, "C": C}[st.src][s]
                        own(st, "rstd", "variance", "turned", "affined")
                        for t in range(TT):
                            ins = dve.tensor_scalar(XH[s][:, t, :], src[:, t, :], MV[s][:, t, 0:1], RS[s][:, t:t + 1],
                                                    ALU.subtract, ALU.mult)
                        ins.then_inc(sem["normed"], 1)

                    def affine(st):
                        if not st.plus:
                            return
                        s = st.s
                        dst = {"X": X, "CC": CC}[st.dst][s]
                        own(st, "normed", "doubled")
                        link(dve.tensor_tensor(XH[s][:, :, :], XH[s][:, :, :], row(st.g), ALU.mult))
                        own(st, "affined")
                        link(dve.tensor_tensor(XH[s][:, :, :], XH[s][:, :, :], row(st.b), ALU.add))
                        dve.tensor_tensor(dst[:, :, :], XH[s][:, :, :], dst[:, :, :], ALU.add) \
                           .then_inc(sem["summed"], 1)

                    def rowmask(st):
                        s = st.s
                        m = {"M0": M0, "M1": M1}[st.dst][s]
                        own(st, "affined")
                        link(dve.tensor_reduce(AM[s][:, :], X[s][:, :, :], AX.X, ALU.max, apply_absolute_value=True))
                        dve.tensor_scalar(m[:, :], AM[s][:, :], 0.0, None, ALU.not_equal).then_inc(sem["rowmask"], 1)
                        dve.wait_ge(sem["rowmask"], st.end["rowmask"])
                        if st.kv:
                            for t in range(TT):
                                ins = dve.tensor_scalar(CM[s][:, t, :], C[s][:, t, :], m[:, t:t + 1], None, ALU.mult)
                            ins.then_inc(sem["row_kept"], 1)

                    def qkv(st):
                        s = st.s
                        own(st, "q_three")
                        w = wide(st.w)
                        if st.bias[0]:
                            ins = dve.tensor_scalar(Q32[s][:, :], w[:, 0:T], col(st.bias[0]), ATTN_SCALE, ALU.add,
                                                    ALU.mult)
                        else:
                            ins = dve.tensor_scalar(Q32[s][:, :], w[:, 0:T], ATTN_SCALE, None, ALU.mult)
                        ins.then_inc(sem["q_read"], 1)
                        dve.wait_ge(sem["q_read"], st.end["q_read"])
                        if st.lengths:
                            for b in range(NB):
                                ins = dve.tensor_scalar(QF[s][:, b, :], head_mask[:, :],
                                                        Q32[s][:, b * SEQ:b * SEQ + 1], None, ALU.mult)
                            ins.then_inc(sem["q_first"], 1)
                        dve.tensor_copy(Q3[s][:, 0, :], Q32[s][:, :]).then_inc(sem["q_one"], 1)
                        dve.wait_ge(sem["q_one"], st.end["q_one"])
                        if st.lengths:
                            dve.wait_ge(sem["q_first"], st.end["q_first"])
                        link(dve.tensor_tensor(Q32[s][:, :], Q32[s][:, :], Q3[s][:, 0, :], ALU.subtract))
                        w = wide(st.w + 1)
                        if st.bias[1]:
                            ins = dve.tensor_scalar(K32[s][:, :], w[:, 0:T], col(st.bias[1]), None, ALU.add)
                        else:
                            ins = dve.tensor_copy(K32[s][:, :], w[:, 0:T])
                        ins.then_inc(sem["k_read"], 1)
                        dve.wait_ge(sem["k_read"], st.end["k_read"])
                        dve.tensor_copy(K3[s][:, 0, :], K32[s][:, :]).then_inc(sem["k_one"], 1)
                        dve.tensor_copy(Q3[s][:, 1, :], Q32[s][:, :]).then_inc(sem["q_two"], 1)
                        dve.wait_ge(sem["q_two"], st.end["q_two"])
                        dve.tensor_tensor(Q3[s][:, 2, :], Q32[s][:, :], Q3[s][:, 1, :], ALU.subtract) \
                           .then_inc(sem["q_three"], 1)

                    def lengths(st):
                        s = st.s
                        w = wide(st.w)
                        dve.tensor_scalar(NZ[s][:, :, :].rearrange("h b k -> h (b k)"), w[0:HEADS, 0:T], 0.0, None,
                                          ALU.not_equal).then_inc(sem["len_read"], 1)
                        dve.wait_ge(sem["len_read"], st.end["len_read"])
                        link(dve.tensor_reduce(LEN[s][:, :], NZ[s][:, :, :], AX.X, ALU.add))
                        link(dve.tensor_scalar(LNAN[s][:, :], LEN[s][:, :], 0.0, HUGE, ALU.is_equal, ALU.mult))
                        link(dve.tensor_scalar(LNAN[s][:, :], LNAN[s][:, :], HUGE, 0.0, ALU.mult, ALU.mult))
                        for b in range(NB):
                            ins = dve.tensor_scalar(NZ[s][:, b, :], key_no[:, :], LEN[s][:, b:b + 1], MASKED,
                                                    ALU.is_ge, ALU.mult)
                        link(ins)
                        for b in range(NB):
                            ins = dve.tensor_scalar(LB[s][:, b * SEQ:(b + 1) * SEQ], NZ[s][:, b, :],
                                                    LNAN[s][:, b:b + 1], None, ALU.add)
                        ins.then_inc(sem["len_row"], 1)

                    def maxima(st):
                        s, n = st.s, st.base.get("stile", 0)
                        dve.wait_ge(tile_full, n + 1)
                        at = (st.g * TILES + st.k) * 2 * QT
                        dst = NEG[s][:, at:at + 2 * QT]
                        tile = SA[n % 2][:, :].rearrange("p (j t k) -> p j t k", j=2, t=QT)
                        if st.mask == "causal":
                            dst = dst.rearrange("p (j t) -> p j t", t=QT)
                            for qt in range(QT):
                                ins = dve.tensor_reduce(dst[:, :, qt], tile[:, :, qt, 0:(qt + 1) * 128], AX.X,
                                                        ALU.max, negate=True)
                        else:
                            ins = dve.tensor_reduce(dst, tile.rearrange("p j t k -> p (j t) k"), AX.X, ALU.max,
                                                    negate=True)
                        ins.then_inc(sem["stile"], 1)

                    def out_rows(st):
                        s, g = st.s, st.g
                        w = wide(st.w)[:, 0:TT * 128].rearrange("p (t j m) -> p t j m", t=TT, j=GROUP)
                        own(st, "out_scaled")
                        link(dve.reciprocal(RC[s][:, :, :], w[:, :, :, HD]))
                        if st.lengths:
                            own(st, "rowmask")
                            m = (M0 if st.mask == "causal" else M1)[s]
                            link(dve.tensor_tensor(RC[s][:, :, :], RC[s][:, :, :],
                                                   m[:, :].unsqueeze(2).to_broadcast([128, TT, GROUP]), ALU.mult))
                        dst = OT[s][:, :, GROUP * HD * g:GROUP * HD * (g + 1)].rearrange("p t (j d) -> p t j d", d=HD)
                        dve.tensor_tensor(dst, w[:, :, :, 0:HD],
                                          RC[s][:, :, :].unsqueeze(3).to_broadcast([128, TT, GROUP, HD]), ALU.mult) \
                           .then_inc(sem["out_scaled"], 1)

                    def out_product(st):
                        s = st.s
                        bank = tokens(wide(st.w))
                        own(st, "affined", "summed", "turned")
                        if not st.acc:
                            dve.tensor_copy(R[s][:, :, :], bank).then_inc(sem["residual"], 1)
                            return
                        dve.tensor_tensor(R[s][:, :, :], bank, row(st.bo), ALU.add).then_inc(sem["out_read"], 1)
                        dve.wait_ge(sem["out_read"], st.end["out_read"])
                        dve.tensor_tensor({"R": R, "X": X}[st.acc][s][:, :, :], R[s][:, :, :], X[s][:, :, :],
                                          ALU.add).then_inc(sem["residual"], 1)

                    def addz(st):
                        s = st.s
                        own(st, "affined", "out_scaled")
                        dve.tensor_tensor(R[s][:, :, :], OT[s][:, :, :], X[s][:, :, :], ALU.add) \
                           .then_inc(sem["residual"], 1)

                    def down(st):
                        s = st.s
                        w = wide(st.w)
                        own(st, "affined", "summed")
                        if not st.b2:
                            dve.tensor_copy(R[s][:, :, :], tokens(w)).then_inc(sem["residual"], 1)
                            return
                        dve.tensor_tensor(R[s][:, :, :], tokens(w), row(st.b2), ALU.add).then_inc(sem["ff_read"], 1)
                        dve.wait_ge(sem["ff_read"], st.end["ff_read"])
                        if st.mask:
                            for t in range(TT):
                                ins = dve.tensor_scalar(R[s][:, t, :], R[s][:, t, :], M0[s][:, t:t + 1], None, ALU.mult)
                            link(ins)
                        dve.tensor_tensor(R[s][:, :, :], R[s][:, :, :], X[s][:, :, :], ALU.add) \
                           .then_inc(sem["residual"], 1)

                    def lin_qkv(st):
                        s = st.s
                        dve.memset(LV[s][:, :, D:D + 1], 1.0)
                        for i in range(2):
                            dve.tensor_scalar(LM[s][:, i, :], wide(st.w + 1 + i)[:, 0:T], 0.0, None, ALU.min) \
                               .then_inc(sem["lin_min"], 1)
                        for i, dst in enumerate((LQ[s][:, :], LK[s][:, :, :].rearrange("p t d -> p (t d)"))):
                            dve.wait_ge(sem["lin_exp"], st.base.get("lin_exp", 0) + i + 1)
                            dve.scalar_tensor_tensor(out=dst, in0=W[(st.w + 1 + i) % 2][:, 0:T], scalar=0.0,
                                                     in1=LE[s][:, i, :], op0=ALU.max, op1=ALU.add) \
                               .then_inc(sem["lin_feature"], 1)

                    def lin_kv(st):
                        s = st.s
                        for b in range(NB):
                            w = wide(st.w + b)
                            dve.tensor_tensor(KVB[s][:, b, 0:D], w[:, 0:D],
                                              block_mask[:, :, :].rearrange("p h d -> p (h d)"), ALU.mult)
                            dve.tensor_scalar(KVB[s][:, b, D:D + LHEADS], block_sum[:, :], w[:, D:D + 1], None,
                                              ALU.mult).then_inc(sem["lin_kv"], 1)

                    def lin_out(st):
                        s = st.s
                        own(st, "residual")
                        for b in range(NB):
                            w = wide(st.w + b)[:, 0:QT * (D + LHEADS)].rearrange("p (t n) -> p t n", t=QT)
                            link(dve.tensor_scalar(LZ[s][:, :, :], w[:, :, D:D + LHEADS], 1e-6, None, ALU.add))
                            link(dve.reciprocal(LZ[s][:, :, :], LZ[s][:, :, :]))
                            dve.tensor_tensor(
                                OT[s][:, b * QT:(b + 1) * QT, :].rearrange("p t (h d) -> p t h d", d=LHD),
                                w[:, :, 0:D].rearrange("p t (h d) -> p t h d", d=LHD),
                                LZ[s][:, :, :].unsqueeze(3).to_broadcast([128, QT, LHEADS, LHD]), ALU.mult) \
                               .then_inc(sem["lin_out"], 1)

                    def logits(st):
                        s = st.s
                        w = wide(st.w)[:, 0:TT * EXPERTS].rearrange("p (t e) -> p t e", t=TT)
                        dve.tensor_tensor(LG[s][:, :, :], w, row("L3_rb"), ALU.add).then_inc(sem["route_read"], 1)
                        dve.wait_ge(sem["route_read"], st.end["route_read"])
                        for t in range(TT):
                            ins = dve.max(MX[s][:, t, :], LG[s][:, t, :])
                        link(ins)
                        dve.tensor_tensor(GD[s][:, :], MX[s][:, :, 1], MX[s][:, :, 0], ALU.subtract) \
                           .then_inc(sem["gate_diff"], 1)
                        for t in range(TT):
                            ins = dve.max_index(IX[s][:, t, :], MX[s][:, t, :], LG[s][:, t, :])
                        link(ins)
                        link(dve.tensor_copy(IXF[s][:, :, :], IX[s][:, :, 0:2]))

                    def gates(st):
                        s = st.s
                        dve.wait_ge(sem["gate_exp"], st.own["gate_exp"])
                        link(dve.tensor_scalar(GP[s][:, :], GE[s][:, :], 1.0, None, ALU.add))
                        link(dve.reciprocal(GP[s][:, :], GP[s][:, :]))
                        link(dve.tensor_tensor(GQ[s][:, :], GE[s][:, :], GP[s][:, :], ALU.mult))
                        for t in range(TT):
                            dve.tensor_scalar(G[s][:, t, :], expert_no[:, :], IXF[s][:, t, 0:1], GP[s][:, t:t + 1],
                                              ALU.is_equal, ALU.mult)
                            ins = dve.tensor_scalar(G2[s][:, t, :], expert_no[:, :], IXF[s][:, t, 1:2],
                                                    GQ[s][:, t:t + 1], ALU.is_equal, ALU.mult)
                        link(ins)
                        dve.tensor_tensor(G[s][:, :, :], G[s][:, :, :], G2[s][:, :, :], ALU.add) \
                           .then_inc(sem["gates"], 1)

                    def expert_bias(st):
                        s = st.s
                        own(st, "gates", "residual")
                        dve.tensor_tensor(X[s][:, :, :], tokens(wide(st.w)), X[s][:, :, :], ALU.add) \
                           .then_inc(sem["expert_mixed"], 1)

                    def expert(st):
                        s, e = st.s, st.e - 1
                        if e < 0:
                            return
                        w = tokens(wide(st.w))
                        own(st, "expert_mixed")
                        for t in range(TT):
                            ins = dve.scalar_tensor_tensor(out=X[s][:, t, :], in0=w[:, t, :],
                                                           scalar=G[s][:, t, e:e + 1], in1=X[s][:, t, :],
                                                           op0=ALU.mult, op1=ALU.add)
                        ins.then_inc(sem["expert_mixed"], 1)

                    kinds = {"double": double, "stats": stats, "normalise": normalise, "affine": affine,
                             "rowmask": rowmask, "qkv": qkv, "lengths": lengths, "maxima": maxima, "out_rows": out_rows,
                             "out_product": out_product, "addz": addz, "down": down, "lin_qkv": lin_qkv,
                             "lin_kv": lin_kv, "lin_out": lin_out, "logits": logits, "gates": gates,
                             "expert_bias": expert_bias, "expert": expert}
                    for st in steps:
                        if st.kind in kinds:
                            kinds[st.kind](st)
            nc.all_engine_barrier()
            nc.gpsimd.sem_clear(range(min(numbers), max(numbers) + 1))
            nc.all_engine_barrier()

        with nc.Fori(0, ROUNDS) as rnd:
            a_round(rnd * (STREAMS * NB), STREAMS)
        if LAST_STREAMS:
            a_round(ROUNDS * STREAMS * NB, LAST_STREAMS)


def _by_dim(w):
    import numpy as np
    return np.transpose(w, (1, 2, 0)).reshape(D, D)


def _cols_by_dim(w):
    import numpy as np
    return np.swapaxes(w.reshape(*w.shape[:-1], HEADS, HD), -1, -2).reshape(w.shape)


def _down(w):
    import numpy as np
    return np.transpose(w.reshape(-1, 128, w.shape[1]), (1, 0, 2)).reshape(128, -1)


def kernel(**inputs):
    import numpy as np
    import concourse.bacc as bacc
    from concourse.bass_utils import run_bass_kernel_spmd

    a = {k: np.asarray(v) for k, v in inputs.items()}
    L = [{k[len(f"L{i}_xattn_"):]: v for k, v in a.items() if k.startswith(f"L{i}_xattn_")} for i in range(4)]
    sa, ca = L[3]["sa_in_w"], L[3]["ca_in_w"]
    m = {
        "L0_q": _cols_by_dim(L[0]["wq_s"]), "L0_k": _cols_by_dim(L[0]["wk_s"]), "L0_v": L[0]["wv_s"], "L0_o": L[0]["wo_s"],
        "L0_cq": _cols_by_dim(L[0]["wq_c"]), "L0_ck": _cols_by_dim(L[0]["wk_c"]), "L0_cv": L[0]["wv_c"],
        "L0_co": L[0]["wo_c"], "L0_f1": L[0]["ff1_w"], "L0_f2": _down(L[0]["ff2_w"]),
        "L1_q": _by_dim(L[1]["Wq1"]), "L1_k": _by_dim(L[1]["Wk1"]),
        "L1_v": np.transpose(L[1]["Wv1"], (1, 0, 2)).reshape(D, D),
        "L1_cq": _by_dim(L[1]["Wq2"]), "L1_ck": _by_dim(L[1]["Wk2"]),
        "L1_cv": np.transpose(L[1]["Wv2"], (1, 0, 2)).reshape(D, D),
        "L1_f1": L[1]["fc1_w"].T, "L1_f2": L[1]["fc2_w"].T,
        "E_q": L[2]["e_wq"], "E_k": L[2]["e_wk"], "E_v": L[2]["e_wv"], "E_m": L[2]["e_wm"], "E_f1": L[2]["e_w1"],
        "E_f2": _down(L[2]["e_w2"]),
        "S_q": L[2]["d_wq0"], "S_k": L[2]["d_wk0"], "S_v": L[2]["d_wv0"], "S_m": L[2]["d_wm0"],
        "C_q": L[2]["d_wq1"], "C_k": L[2]["d_wk1"], "C_v": L[2]["d_wv1"], "C_m": L[2]["d_wm1"],
        "D_f1": L[2]["d_w1"], "D_f2": _down(L[2]["d_w2"]),
        "L3_q": _cols_by_dim(sa[0:D].T), "L3_k": _cols_by_dim(sa[D:2 * D].T), "L3_v": sa[2 * D:].T,
        "L3_o": L[3]["sa_out_w"].T,
        "L3_cq": _cols_by_dim(ca[0:D].T), "L3_ck": _cols_by_dim(ca[D:2 * D].T), "L3_cv": ca[2 * D:].T,
        "L3_co": L[3]["ca_out_w"].T, "L3_r": L[3]["router_w"].T,
    }
    experts = {
        "M_f1": np.transpose(L[3]["e_fc1_w"], (2, 0, 1)).reshape(D, -1),
        "M_f2": np.transpose(L[3]["e_fc2_w"].reshape(EXPERTS, D, DFF // 128, 128), (3, 0, 2, 1)).reshape(128, -1),
    }
    sb_, cb_ = L[3]["sa_in_b"], L[3]["ca_in_b"]
    c = {
        "L0_bq": _cols_by_dim(L[0]["bq_s"]), "L0_bk": _cols_by_dim(L[0]["bk_s"]), "L0_bv": L[0]["bv_s"],
        "L0_cbq": _cols_by_dim(L[0]["bq_c"]), "L0_cbk": _cols_by_dim(L[0]["bk_c"]), "L0_cbv": L[0]["bv_c"],
        "L0_fb1": L[0]["ff1_b"], "L1_fb1": L[1]["fc1_b"],
        "L3_bq": _cols_by_dim(sb_[0:D]), "L3_bk": _cols_by_dim(sb_[D:2 * D]), "L3_bv": sb_[2 * D:],
        "L3_cbq": _cols_by_dim(cb_[0:D]), "L3_cbk": _cols_by_dim(cb_[D:2 * D]), "L3_cbv": cb_[2 * D:],
        "L3_g1": L[3]["sa_ln_g"], "L3_b1": L[3]["sa_ln_b"], "L3_g2": L[3]["ca_q_ln_g"], "L3_b2": L[3]["ca_q_ln_b"],
        "L3_gk": L[3]["ca_kv_ln_g"], "L3_bkv": L[3]["ca_kv_ln_b"], "L3_g3": L[3]["moe_ln_g"], "L3_b3": L[3]["moe_ln_b"],
        "M_fb1": L[3]["e_fc1_b"].reshape(-1),
    }
    r = {"L0_bo": L[0]["bo_s"], "L0_cbo": L[0]["bo_c"], "L0_fb2": L[0]["ff2_b"], "L1_fb2": L[1]["fc2_b"],
         "L3_bo": L[3]["sa_out_b"], "L3_cbo": L[3]["ca_out_b"], "L3_rb": L[3]["router_b"]}
    for i in (0, 1):
        for n in (1, 2, 3):
            for kind in "gb":
                c[f"L{i}_{kind}{n}"] = r[f"L{i}_{kind}{n}"] = L[i][f"ln{n}_{kind}"]
    for kind in "gb":
        for n in (1, 2):
            r[f"E_{kind}{n}"] = L[2][f"e_{kind}{n}"]
        for n in (0, 1, 2):
            r[f"D_{kind}{n}"] = L[2][f"d_{kind}{n}"]

    arrays = {
        "x": a["x"], "ctx": a["ctx_1024"],
        "mask0": a["mask_1x1xSxS2_ik0"].reshape(SEQ, SEQ), "mask1": a["mask_1x1xSxS2_if1"].reshape(SEQ, SEQ),
        "mats": np.concatenate([m[n] for n in MAT_AT], axis=1),
        "expert_mats": np.stack([experts[n].reshape(128, EXPERTS, DFF) for n in EXPERT_MATS], axis=1),
        "cols": np.concatenate([c[n].reshape(-1, 128) for n in COL_AT], axis=0).T,
        "rows": np.concatenate([r[n] for n in ROW_AT]),
        "fc2_bias": L[3]["e_fc2_b"],
    }
    arrays = {k: np.ascontiguousarray(v) for k, v in arrays.items()}
    nc = bacc.Bacc("TRN2", target_bir_lowering=False, num_devices=1)
    args = [nc.dram_tensor(f"in_{k}", v.shape, mybir.dt.from_np(v.dtype), kind="ExternalInput").ap()
            for k, v in arrays.items()]
    out = nc.dram_tensor("out", (BATCHES, SEQ, D), mybir.dt.float32, kind="ExternalOutput").ap()
    build(nc, *args, out)
    got = run_bass_kernel_spmd(nc, [{f"in_{k}": v for k, v in arrays.items()}], core_ids=[0])
    return got.results[0]["out"]
```
